# Optimizing a Trainium2 kernel written in Bass

```python
import numpy as np
import jax
import jax.numpy as jnp

def _softmax(x, axis=-1):
    return jax.nn.softmax(x, axis=axis)

def _gelu(x):
    return jax.nn.gelu(x, approximate=True)

def _silu(x):
    return jax.nn.silu(x)

def _sigmoid(x):
    return jax.nn.sigmoid(x)

def _layernorm(x, axis=-1, eps=1e-05):
    m = jnp.mean(x, axis=axis, keepdims=True)
    v = jnp.var(x, axis=axis, keepdims=True)
    return (x - m) / jnp.sqrt(v + eps)

def _scatter_add(tgt, idx, src, axis=0):
    return tgt.at[idx].add(src)

def _segment_sum(src, seg, n):
    return jax.ops.segment_sum(src, seg, n)
kernel_name = 'mk_vit_tower_cls_d1_tok_img768_r4_34872f'

def setup_inputs(seed: int=0):
    np.random.seed(seed)
    _w = jnp.asarray

    def _rec_inputs():
        import jax
        import jax.numpy as jnp
        _rk = jax.random.key(seed)
        x = -0.000222058 + 0.999998 * jax.random.normal(jax.random.fold_in(_rk, 1), (32, 3, 84, 84), jnp.float32)
        cls_tok = 0.02 * jax.random.normal(jax.random.fold_in(_rk, 5), (1, 1, 192), jnp.float32)
        return (x, cls_tok)
    x, cls_tok = _rec_inputs()

    def _L0_tok_setup():
        import jax, jax.numpy as jnp
        import numpy as np
        from jax import lax
        HIDDEN = 192
        C_IN = 3
        PATCH = 16
        SIDE = 32
        NUM_PATCHES = SIDE * SIDE

        def _position_ids(nb_h, nb_w):
            boundaries = np.arange(1.0 / SIDE, 1.0, 1.0 / SIDE, dtype=np.float32)
            frac_h = np.arange(0.0, 1.0 - 1e-06, 1.0 / nb_h, dtype=np.float32)
            frac_w = np.arange(0.0, 1.0 - 1e-06, 1.0 / nb_w, dtype=np.float32)
            bh = np.searchsorted(boundaries, frac_h, side='right')
            bw = np.searchsorted(boundaries, frac_w, side='right')
            return jnp.asarray((bh[:, None] * SIDE + bw).reshape(-1), dtype=jnp.int32)
        key = jax.random.key(seed)
        k1, k2, k3 = jax.random.split(key, 3)
        pixel_values = jax.random.normal(k1, (32, C_IN, 128, 128), dtype=jnp.float32)
        conv_w = jax.random.normal(k2, (HIDDEN, C_IN, PATCH, PATCH), dtype=jnp.float32) * 0.02
        conv_b = jnp.zeros((HIDDEN,), dtype=jnp.float32)
        pos_table = jax.random.normal(k3, (NUM_PATCHES, HIDDEN), dtype=jnp.float32) * 0.02
        return {'pixel_values': pixel_values, 'conv_w': conv_w, 'conv_b': conv_b, 'pos_table': pos_table}
    _L0_tok_all = _L0_tok_setup()
    _L0_tok_in = {k: v for k, v in _L0_tok_all.items() if k in ('conv_w', 'conv_b', 'pos_table')}
    del _L0_tok_all

    def _L0_attn_setup():
        import jax, jax.numpy as jnp
        import numpy as np
        from jax import lax
        H = 192
        I = 384
        N = 16
        R = 48
        K = 4
        NL = 16
        B, L = (2, 256)
        EPS = 1e-05

        def rmsnorm(x, w):
            return x * lax.rsqrt(jnp.mean(x * x, axis=-1, keepdims=True) + EPS) * w

        def causal_conv(u, w, b):
            uc = jnp.swapaxes(u, 1, 2)
            y = lax.conv_general_dilated(uc, w, (1,), [(K - 1, 0)], dimension_numbers=('NCH', 'OIH', 'NCH'), feature_group_count=I)
            return jnp.swapaxes(y + b[None, :, None], 1, 2)

        def selective_scan(u, dt, A, Bm, Cm, Dp):

            def step(h, inp):
                u_t, dt_t, B_t, C_t = inp
                dA = jnp.exp(dt_t[:, :, None] * A)
                h = dA * h + (dt_t * u_t)[:, :, None] * B_t[:, None, :]
                y = jnp.einsum('bin,bn->bi', h, C_t)
                return (h, y)
            inputs = tuple((jnp.moveaxis(a, 1, 0) for a in (u, dt, Bm, Cm)))
            h0 = jnp.zeros((u.shape[0],) + A.shape, u.dtype)
            _, ys = lax.scan(step, h0, inputs)
            return jnp.moveaxis(ys, 0, 1) + u * Dp

        def mamba_layer(x, p):
            in_w, cw, cb, xp_w, dtw, dtb, a_log, dp, ow, nw = p
            h = rmsnorm(x, nw)
            xz = jnp.einsum('blh,ch->blc', h, in_w)
            u, z = jnp.split(xz, 2, axis=-1)
            u = jax.nn.silu(causal_conv(u, cw, cb))
            proj = jnp.einsum('bli,ci->blc', u, xp_w)
            dt_r, Bm, Cm = (proj[..., :R], proj[..., R:R + N], proj[..., R + N:])
            dt = jax.nn.softplus(jnp.einsum('blr,ir->bli', dt_r, dtw) + dtb)
            A = -jnp.exp(a_log)
            y = selective_scan(u, dt, A, Bm, Cm, dp)
            y = y * jax.nn.silu(z)
            return x + jnp.einsum('bli,hi->blh', y, ow)
        key = jax.random.key(seed)
        ks = jax.random.split(key, 8)
        s = 0.02
        x = jax.random.normal(ks[0], (B, L, H), jnp.float32)
        in_proj_w = jax.random.normal(ks[1], (NL, 2 * I, H), jnp.float32) * s
        conv_w = jax.random.normal(ks[2], (NL, I, 1, K), jnp.float32) * 0.1
        conv_b = jnp.zeros((NL, I), jnp.float32)
        x_proj_w = jax.random.normal(ks[3], (NL, R + 2 * N, I), jnp.float32) * s
        dt_proj_w = jax.random.normal(ks[4], (NL, I, R), jnp.float32) * 0.01
        dt_proj_b = -4.0 + 0.1 * jax.random.normal(ks[5], (NL, I), jnp.float32)
        A_log = jnp.log(jnp.tile(jnp.arange(1, N + 1, dtype=jnp.float32), (NL, I, 1)))
        D = jnp.ones((NL, I), jnp.float32)
        out_proj_w = jax.random.normal(ks[6], (NL, H, I), jnp.float32) * s
        norm_w = jnp.ones((NL, H), jnp.float32)
        final_norm_w = jnp.ones((H,), jnp.float32)
        return {'x': x, 'in_proj_w': in_proj_w, 'conv_w': conv_w, 'conv_b': conv_b, 'x_proj_w': x_proj_w, 'dt_proj_w': dt_proj_w, 'dt_proj_b': dt_proj_b, 'A_log': A_log, 'D': D, 'out_proj_w': out_proj_w, 'norm_w': norm_w, 'final_norm_w': final_norm_w}
    _L0_attn_all = _L0_attn_setup()
    _L0_attn_in = {k: v for k, v in _L0_attn_all.items() if k in ('in_proj_w', 'conv_w', 'conv_b', 'x_proj_w', 'dt_proj_w', 'dt_proj_b', 'A_log', 'D', 'out_proj_w', 'norm_w', 'final_norm_w')}
    del _L0_attn_all

    def _L0_ffn_setup():
        import jax, jax.numpy as jnp
        import numpy as np
        import math
        B, S, D = (4, 1024, 192)
        E = 8
        TOP_K = 2
        H = 512
        CAP_F = 1.25
        EPS = 1e-06
        ALPHA = 1.0
        key = jax.random.key(seed)
        k0, k1, k2, k3 = jax.random.split(key, 4)
        x = jax.random.normal(k0, (B, S, D), jnp.float32)
        gate_w = jax.random.normal(k1, (E, D), jnp.float32) * 0.02
        w13 = jax.random.normal(k2, (E, 2 * H, D), jnp.float32) * 0.02
        w2 = jax.random.normal(k3, (E, D, H), jnp.float32) * 0.02
        norm_w = jnp.ones((E, D), jnp.float32)
        return {'x': x, 'gate_w': gate_w, 'w13': w13, 'w2': w2, 'norm_w': norm_w}
    _L0_ffn_all = _L0_ffn_setup()
    _L0_ffn_in = {k: v for k, v in _L0_ffn_all.items() if k in ('gate_w', 'w13', 'w2', 'norm_w')}
    del _L0_ffn_all
    return {'x': x, 'cls_tok': cls_tok, 'L0_tok_conv_w': _L0_tok_in['conv_w'], 'L0_tok_conv_b': _L0_tok_in['conv_b'], 'L0_tok_pos_table': _L0_tok_in['pos_table'], 'L0_attn_in_proj_w': _L0_attn_in['in_proj_w'], 'L0_attn_conv_w': _L0_attn_in['conv_w'], 'L0_attn_conv_b': _L0_attn_in['conv_b'], 'L0_attn_x_proj_w': _L0_attn_in['x_proj_w'], 'L0_attn_dt_proj_w': _L0_attn_in['dt_proj_w'], 'L0_attn_dt_proj_b': _L0_attn_in['dt_proj_b'], 'L0_attn_A_log': _L0_attn_in['A_log'], 'L0_attn_D': _L0_attn_in['D'], 'L0_attn_out_proj_w': _L0_attn_in['out_proj_w'], 'L0_attn_norm_w': _L0_attn_in['norm_w'], 'L0_attn_final_norm_w': _L0_attn_in['final_norm_w'], 'L0_ffn_gate_w': _L0_ffn_in['gate_w'], 'L0_ffn_w13': _L0_ffn_in['w13'], 'L0_ffn_w2': _L0_ffn_in['w2'], 'L0_ffn_norm_w': _L0_ffn_in['norm_w']}

def reference(x, cls_tok, L0_tok_conv_w, L0_tok_conv_b, L0_tok_pos_table, L0_attn_in_proj_w, L0_attn_conv_w, L0_attn_conv_b, L0_attn_x_proj_w, L0_attn_dt_proj_w, L0_attn_dt_proj_b, L0_attn_A_log, L0_attn_D, L0_attn_out_proj_w, L0_attn_norm_w, L0_attn_final_norm_w, L0_ffn_gate_w, L0_ffn_w13, L0_ffn_w2, L0_ffn_norm_w):
    import jax
    import jax.numpy as jnp

    def _L0_tok_ref(pixel_values, conv_w, conv_b, pos_table):
        import jax, jax.numpy as jnp
        import numpy as np
        from jax import lax
        HIDDEN = 192
        C_IN = 3
        PATCH = 16
        SIDE = 32
        NUM_PATCHES = SIDE * SIDE

        def _position_ids(nb_h, nb_w):
            boundaries = np.arange(1.0 / SIDE, 1.0, 1.0 / SIDE, dtype=np.float32)
            frac_h = np.arange(0.0, 1.0 - 1e-06, 1.0 / nb_h, dtype=np.float32)
            frac_w = np.arange(0.0, 1.0 - 1e-06, 1.0 / nb_w, dtype=np.float32)
            bh = np.searchsorted(boundaries, frac_h, side='right')
            bw = np.searchsorted(boundaries, frac_w, side='right')
            return jnp.asarray((bh[:, None] * SIDE + bw).reshape(-1), dtype=jnp.int32)
        B, _, H, W = pixel_values.shape
        nb_h, nb_w = (H // PATCH, W // PATCH)
        patches = lax.conv_general_dilated(pixel_values, conv_w, window_strides=(PATCH, PATCH), padding='VALID', dimension_numbers=('NCHW', 'OIHW', 'NCHW'))
        patches = patches + conv_b[None, :, None, None]
        embeddings = patches.reshape(B, HIDDEN, nb_h * nb_w).transpose(0, 2, 1)
        pos_ids = _position_ids(nb_h, nb_w)
        pos_emb = pos_table[pos_ids]
        return embeddings + pos_emb[None, :, :]

    def _L0_attn_ref(x, in_proj_w, conv_w, conv_b, x_proj_w, dt_proj_w, dt_proj_b, A_log, D, out_proj_w, norm_w, final_norm_w):
        import jax, jax.numpy as jnp
        import numpy as np
        from jax import lax
        H = 192
        I = 384
        N = 16
        R = 48
        K = 4
        NL = 16
        B, L = (2, 256)
        EPS = 1e-05

        def rmsnorm(x, w):
            return x * lax.rsqrt(jnp.mean(x * x, axis=-1, keepdims=True) + EPS) * w

        def causal_conv(u, w, b):
            uc = jnp.swapaxes(u, 1, 2)
            y = lax.conv_general_dilated(uc, w, (1,), [(K - 1, 0)], dimension_numbers=('NCH', 'OIH', 'NCH'), feature_group_count=I)
            return jnp.swapaxes(y + b[None, :, None], 1, 2)

        def selective_scan(u, dt, A, Bm, Cm, Dp):

            def step(h, inp):
                u_t, dt_t, B_t, C_t = inp
                dA = jnp.exp(dt_t[:, :, None] * A)
                h = dA * h + (dt_t * u_t)[:, :, None] * B_t[:, None, :]
                y = jnp.einsum('bin,bn->bi', h, C_t)
                return (h, y)
            inputs = tuple((jnp.moveaxis(a, 1, 0) for a in (u, dt, Bm, Cm)))
            h0 = jnp.zeros((u.shape[0],) + A.shape, u.dtype)
            _, ys = lax.scan(step, h0, inputs)
            return jnp.moveaxis(ys, 0, 1) + u * Dp

        def mamba_layer(x, p):
            in_w, cw, cb, xp_w, dtw, dtb, a_log, dp, ow, nw = p
            h = rmsnorm(x, nw)
            xz = jnp.einsum('blh,ch->blc', h, in_w)
            u, z = jnp.split(xz, 2, axis=-1)
            u = jax.nn.silu(causal_conv(u, cw, cb))
            proj = jnp.einsum('bli,ci->blc', u, xp_w)
            dt_r, Bm, Cm = (proj[..., :R], proj[..., R:R + N], proj[..., R + N:])
            dt = jax.nn.softplus(jnp.einsum('blr,ir->bli', dt_r, dtw) + dtb)
            A = -jnp.exp(a_log)
            y = selective_scan(u, dt, A, Bm, Cm, dp)
            y = y * jax.nn.silu(z)
            return x + jnp.einsum('bli,hi->blh', y, ow)
        params = (in_proj_w, conv_w, conv_b, x_proj_w, dt_proj_w, dt_proj_b, A_log, D, out_proj_w, norm_w)

        def body(carry, p):
            return (mamba_layer(carry, p), None)
        out, _ = lax.scan(body, x, params)
        return rmsnorm(out, final_norm_w)

    def _L0_ffn_ref(x, gate_w, w13, w2, norm_w):
        import jax, jax.numpy as jnp
        import numpy as np
        import math
        B, S, D = (4, 1024, 192)
        E = 8
        TOP_K = 2
        H = 512
        CAP_F = 1.25
        EPS = 1e-06
        ALPHA = 1.0
        Bx, Sx, Dx = x.shape
        N = Bx * Sx
        cap = int(math.ceil(CAP_F * TOP_K * N / E))
        xf = x.reshape(N, Dx)
        logits = xf.astype(jnp.float32) @ gate_w.T
        probs = jax.nn.softmax(logits, axis=-1)
        top_p, top_i = jax.lax.top_k(probs, TOP_K)
        w = top_p / jnp.sum(top_p, axis=-1, keepdims=True)
        flat_e = top_i.reshape(-1)
        onehot = jax.nn.one_hot(flat_e, E, dtype=jnp.int32)
        pos = jnp.take_along_axis(jnp.cumsum(onehot, axis=0) - 1, flat_e[:, None], axis=1)[:, 0]
        keep = pos < cap
        didx = flat_e * cap + jnp.minimum(pos, cap - 1)
        safe = jnp.where(keep, didx, E * cap)
        x_rep = jnp.repeat(xf, TOP_K, axis=0)
        buf = jnp.zeros((E * cap + 1, Dx), x.dtype).at[safe].set(x_rep)
        buf = buf[:-1].reshape(E, cap, Dx)
        z = 2.0 * buf
        z = z * jax.lax.rsqrt(jnp.mean(z * z, axis=-1, keepdims=True) + EPS)
        z = z * norm_w[:, None, :]
        gu = jnp.einsum('ecd,ehd->ech', z, w13)
        g, u = jnp.split(gu, 2, axis=-1)
        y = buf + ALPHA * jnp.einsum('ech,edh->ecd', jax.nn.silu(g) * u, w2)
        y_tok = y.reshape(E * cap, Dx)[didx]
        cw = (w.reshape(-1) * keep.astype(w.dtype)).astype(x.dtype)
        out = (cw[:, None] * y_tok).reshape(N, TOP_K, Dx).sum(axis=1)
        return out.reshape(Bx, Sx, Dx)
    h = _L0_tok_ref(x, L0_tok_conv_w, L0_tok_conv_b, L0_tok_pos_table)
    h = jnp.concatenate([jnp.broadcast_to(cls_tok, (h.shape[0], 1, h.shape[2])), h], axis=1)
    h = h + _L0_attn_ref(_layernorm(h, axis=-1), L0_attn_in_proj_w, L0_attn_conv_w, L0_attn_conv_b, L0_attn_x_proj_w, L0_attn_dt_proj_w, L0_attn_dt_proj_b, L0_attn_A_log, L0_attn_D, L0_attn_out_proj_w, L0_attn_norm_w, L0_attn_final_norm_w)
    h = h + _L0_ffn_ref(_layernorm(h, axis=-1), L0_ffn_gate_w, L0_ffn_w13, L0_ffn_w2, L0_ffn_norm_w)
    return h

_drawn_inputs = setup_inputs


def setup_inputs(seed=0):
    import zlib

    import numpy as np

    out = dict(_drawn_inputs(seed))
    spreads = {'L0_tok_conv_b': (0.0, 0.1),
     'L0_attn_conv_b': (0.0, 0.719),
     'L0_attn_D': (1.0, 0.6),
     'L0_attn_norm_w': (1.0, 0.6),
     'L0_attn_final_norm_w': (1.0, 0.2),
     'L0_ffn_norm_w': (1.0, 0.6)}
    factors = {'L0_attn_in_proj_w': 6.273,
     'L0_attn_conv_w': 8.0,
     'L0_attn_x_proj_w': 8.0,
     'L0_attn_dt_proj_w': 8.0,
     'L0_attn_dt_proj_b': 8.0,
     'L0_attn_A_log': 8.0,
     'L0_attn_out_proj_w': 6.211,
     'L0_ffn_w13': 8.0,
     'L0_ffn_w2': 8.0}
    for name, (base, spread) in spreads.items():
        noise = np.random.default_rng([zlib.crc32(name.encode()), seed]).standard_normal(out[name].shape)
        drawn = base * np.exp(spread * noise) if base else spread * noise
        out[name] = jnp.asarray(drawn.astype(out[name].dtype))
    for name, factor in factors.items():
        out[name] = (out[name] * factor).astype(out[name].dtype)
    return out
```

```python
import concourse.bass as bass
from concourse import mybir
from contextlib import ExitStack

NB, SEQ, D = 32, 26, 192
NTOK = NB * SEQ
TT = 104
NT = NTOK // TT
HB = NB // 2
HT = HB * SEQ
HNT = HT // TT
KP, KC = 128, 6
DC, DP = 2, 96
NL, I, NS, R, K = 16, 384, 16, 48, 4
IC = I // 128
XR = 96
BC0, NBC = 64, 2 * NS
UNITS = NS * IC
TPAD = K - 1 + SEQ
E, FF, CAP = 8, 512, 260
FC = FF // 128

LN_SLACK = 1.3e-7
R_DBU, R_H, R_HC, R_DA = 6, 3, 4, 2
NPRE = 31
NPOST = 2
NSH = NPRE + NPOST
J_TR, J_U, J_Z0, J_CONV, J_Z1, J_XP, J_DT, J_B = 0, 2, 5, 6, 9, 11, 12, 15

fp32 = mybir.dt.float32
bf16 = mybir.dt.bfloat16
ALU = mybir.AluOpType
ACT = mybir.ActivationFunctionType
AX = mybir.AxisListType


def embed_program(nc, a, h0, xres, eps5):
    with ExitStack() as ctx:
        def sb(name, shape, dt=fp32):
            return ctx.enter_context(nc.sbuf_tensor(name, shape, dt))

        def sem(name):
            return ctx.enter_context(nc.semaphore(name))

        patches = sb("patches", [KP, KC, NTOK])
        wconv = sb("wconv", [KP, KC, D])
        posb = sb("posb", [TT, D])
        cbias = sb("cbias", [TT, D])
        stats = sb("stats", [TT, NT, 6])
        mv = sb("mv", [TT, NT, 2])
        rstd = sb("rstd", [TT, NT])
        ps = [ctx.enter_context(nc.psum_tensor(f"pe{i}", [128, 512], fp32)) for i in range(2)]
        patch_in = [sem(f"patch_in{i}") for i in range(KC)]
        w_in, b_in = sem("w_in"), sem("b_in")
        eps_set = sem("eps_set")
        bias_ready, emb_ready, emb_taken = sem("bias_ready"), sem("emb_ready"), sem("emb_taken")
        stat_ready, mv_ready, ln_ready, rstd_ready, x_ready = (
            sem("stat_ready"), sem("mv_ready"), sem("ln_ready"), sem("rstd_ready"), sem("x_ready"))

        with nc.Block() as block:
            @block.sync
            def _(sp):
                sp.dma_start(wconv[:], a["wconv"]).then_inc(w_in, 16)
                for c in range(KC):
                    sp.dma_start(patches[:, c, :], a["patches"][:, c, :]).then_inc(patch_in[c], 16)
                sp.dma_start(posb[:], a["posb"]).then_inc(b_in, 16)
                sp.dma_start(cbias[:], a["cbias"]).then_inc(b_in, 16)

            @block.tensor
            def _(pe):
                pe.wait_ge(w_in, 16)
                for c in range(KC):
                    pe.wait_ge(patch_in[c], 16)
                for j in range(NT):
                    if j >= 2:
                        pe.wait_ge(emb_taken, j - 1)
                    for c in range(KC):
                        mm = nc.tensor.matmul(ps[j % 2][:TT, :D], patches[:, c, j * TT:(j + 1) * TT],
                                              wconv[:, c, :], start=(c == 0), stop=(c == KC - 1))
                    mm.then_inc(emb_ready, 1)

            @block.vector
            def _(dve):
                nc.vector.memset(eps5[:], 1e-5).then_inc(eps_set, 1)
                dve.wait_ge(b_in, 32)
                nc.vector.tensor_tensor(posb[:], posb[:], cbias[:], ALU.add).then_inc(bias_ready, 1)
                dve.wait_ge(bias_ready, 1)
                for j in range(NT):
                    dve.wait_ge(emb_ready, j + 1)
                    nc.vector.tensor_tensor(h0[:, j, :], ps[j % 2][:TT, :D], posb[:], ALU.add
                                            ).then_inc(emb_taken, 1)
                    dve.wait_ge(emb_taken, j + 1)
                    nc.vector.bn_stats(stats[:, j, :], h0[:, j, :]).then_inc(stat_ready, 1)
                    dve.wait_ge(stat_ready, j + 1)
                    nc.vector.bn_aggr(mv[:, j, :], stats[:, j, :]).then_inc(mv_ready, 1)
                dve.wait_ge(rstd_ready, 1)
                for j in range(NT):
                    nc.vector.tensor_scalar(xres[:, j, :], h0[:, j, :], mv[:, j, 0:1], rstd[:, j:j + 1],
                                            ALU.subtract, ALU.mult).then_inc(x_ready, 1)

            @block.scalar
            def _(act):
                nc.scalar.preload_act_table_set("natural_log_exp_and_others")
                act.wait_ge(eps_set, 1)
                act.wait_ge(mv_ready, NT)
                nc.scalar.activation(rstd[:], mv[:, :, 1], ACT.Ln, bias=eps5[:TT, 0:1]).then_inc(ln_ready, 1)
                act.wait_ge(ln_ready, 1)
                nc.scalar.activation(rstd[:], rstd[:], ACT.Exp, scale=-0.5).then_inc(rstd_ready, 1)


def mamba_program(nc, a, xres, eps5, ident):
    with ExitStack() as ctx:
        def sb(name, shape, dt=fp32):
            return ctx.enter_context(nc.sbuf_tensor(name, shape, dt))

        def sem(name):
            return ctx.enter_context(nc.semaphore(name))

        win = sb("win", [DP, DC, 2 * I])
        nw = sb("nw", [DP, DC])
        chan = sb("chan", [128, IC, K + 2])
        cdiag = sb("cdiag", [128, IC, K, 128])
        wxp = sb("wxp", [128, IC, XR])
        wdt = sb("wdt", [R, I])
        wout = sb("wout", [128, IC, D])
        dskip = sb("dskip", [128, IC])
        alog = sb("alog", [128, IC * NS])
        nega = sb("nega", [128, IC * NS])
        id3 = sb("id3", [XR, NBC])
        sel = sb("sel", [XR, NBC, 128], bf16)
        one, third = sb("one", [128, 1]), sb("third", [128, 1])
        sq = sb("sq", [TT, D])
        ssq = sb("ssq", [TT, HNT])
        rrms = sb("rrms", [TT, HNT])
        xn = sb("xn", [TT, HNT, D])
        hT = sb("hT", [DP, DC, HT])
        upad = sb("upad", [128, IC, HB, TPAD])
        uc = sb("uc", [128, IC, HT])
        zraw = sb("zraw", [128, IC, HT])
        gA = sb("gA", [128, IC, HT])
        gB = sb("gB", [128, IC, HT])
        gC = sb("gC", [128, IC, HT])
        gD = sb("gD", [128, IC, HT])
        gZ = sb("gZ", [128, IC, HT])
        dtr = sb("dtr", [R, HT])
        resid = sb("resid", [XR, HT])
        u = [sb(f"u{h}", [128, IC, HT]) for h in range(2)]
        zs = [sb(f"zs{h}", [128, IC, HT]) for h in range(2)]
        dt = [sb(f"dt{h}", [128, IC, HT]) for h in range(2)]
        dtu = [sb(f"dtu{h}", [128, IC, HT]) for h in range(2)]
        parts = [sb(f"parts{h}", [XR, HT], bf16) for h in range(2)]
        y = sb("y", [128, IC, HT])
        ball = sb("ball", [128, NS, HT])
        dbu = sb("dbu", [128, R_DBU, HT])
        hst = sb("hst", [128, R_H, HT])
        hc = sb("hc", [128, R_HC, HT])

        pb = [ctx.enter_context(nc.psum_tensor(f"pm{i}", [128, 512], fp32)) for i in range(8)]
        yacc = pb[0:3]
        cbank = pb[3:5]
        dab = pb[5:7]
        shared = pb[7]

        zeroed = sem("zeroed")
        pre_in, post_in, alog_in, id3_in = sem("pre_in"), sem("post_in"), sem("alog_in"), sem("id3_in")
        sel_ready, nega_exp, nega_ready = sem("sel_ready"), sem("nega_exp"), sem("nega_ready")
        diag_ready = sem("diag_ready")
        sh_full, sh_free = sem("sh_full"), sem("sh_free")
        exp_done, m1_done, scan_done, c_ready, m2_done, reduce_done = (
            sem("exp_done"), sem("m1_done"), sem("scan_done"), sem("c_ready"), sem("m2_done"),
            sem("reduce_done"))
        yfin, y_ready = sem("yfin"), sem("y_ready")
        sq_done, rms_ln, rms_ready, xn_ready = sem("sq_done"), sem("rms_ln"), sem("rms_ready"), sem("xn_ready")
        uclamp, uexp, uln, usig, u_ready = sem("uclamp"), sem("uexp"), sem("uln"), sem("usig"), sem("u_ready")
        zclamp, zexp, zln, zsig, z_ready = sem("zclamp"), sem("zexp"), sem("zln"), sem("zsig"), sem("z_ready")
        bc_hi, bc_r1, bc_mid, parts_ready = sem("bc_hi"), sem("bc_r1"), sem("bc_mid"), sem("parts_ready")
        dclamp, dexp, dln, dpoly = sem("dclamp"), sem("dexp"), sem("dln"), sem("dpoly")
        dpoly4, dpoly3 = sem("dpoly4"), sem("dpoly3")
        dt_ready, dtu_ready = sem("dt_ready"), sem("dtu_ready")

        CREDIT = 6

        def pre_tile(p, j):
            return j if isinstance(p, int) and p == 0 else p * NSH - NPOST + j

        def post_tile(k, i):
            return k * NSH - NPOST + (0 if isinstance(k, int) and k == 2 * NL else NPRE) + i

        with nc.Block() as block:
            @block.sync
            def _(sp):
                def load_pre(l):
                    for dst, src in ((win, "win"), (nw, "nw"), (chan, "chan"), (wxp, "wxp"), (wdt, "wdt")):
                        s = a[src]
                        sp.dma_start(dst[:], s[bass.ds(l, 1)].rearrange(
                            "o p a b -> p (o a) b" if len(s.shape) == 4 else "o p a -> p (o a)")
                        ).then_inc(pre_in, 16)

                def load_post(l):
                    sp.dma_start(wout[:], a["wout"][bass.ds(l, 1)].rearrange("o p a b -> p (o a) b")
                                 ).then_inc(post_in, 16)
                    sp.dma_start(dskip[:], a["dskip"][bass.ds(l, 1)].rearrange("o p a -> p (o a)")
                                 ).then_inc(post_in, 16)

                def load_alog(l):
                    sp.dma_start(alog[:], a["alog"][bass.ds(l, 1)].rearrange("o p a -> p (o a)")
                                 ).then_inc(alog_in, 16)

                def layer(l, first, last):
                    if not first:
                        sp.wait_ge(sh_full, post_tile(2 * l, 1) + 1)
                        load_post(l)
                    if not last:
                        sp.wait_ge(nega_ready, l + 1)
                        load_alog(l + 1)
                        sp.wait_ge(sh_free, pre_tile(2 * l + 1, J_DT + IC - 1) + 1)
                        load_pre(l + 1)

                sp.dma_start(id3[:], a["id3"]).then_inc(id3_in, 16)
                load_pre(0)
                load_alog(0)
                load_post(0)
                layer(0, True, False)
                with sp.Fori(1, NL - 1) as l:
                    layer(l, False, False)
                layer(NL - 1, False, True)

            @block.gpsimd
            def _(pool):
                def pre(p, slot, o):
                    if slot in (21, 22, 23):
                        i = slot - 21
                        pool.wait_ge(usig, p * IC + i + 1)
                        nc.gpsimd.tensor_tensor(u[o][:, i, :], uc[:, i, :], gA[:, i, :], ALU.mult
                                                ).then_inc(u_ready, 1)
                    if slot in (27, 28, 29):
                        i = slot - 27
                        pool.wait_ge(zsig, p * IC + i + 1)
                        nc.gpsimd.tensor_tensor(zs[o][:, i, :], zraw[:, i, :], gZ[:, i, :], ALU.mult
                                                ).then_inc(z_ready, 1)
                    if slot in (33, 34, 35):
                        i = slot - 33
                        pool.wait_ge(dpoly4, p * IC + i + 1)
                        nc.gpsimd.tensor_tensor(gC[:, i, :], gC[:, i, :], gA[:, i, :], ALU.mult
                                                ).then_inc(dpoly3, 1)
                    if slot in (39, 40, 41):
                        i = slot - 39
                        pool.wait_ge(dt_ready, p * IC + i + 1)
                        nc.gpsimd.tensor_tensor(dtu[o][:, i, :], dt[o][:, i, :], u[o][:, i, :], ALU.mult
                                                ).then_inc(dtu_ready, 1)

                def step(l, h, first, last):
                    k = l * 2 + h
                    for v in range(UNITS):
                        n, i = divmod(v, IC)
                        if v == 0:
                            pool.wait_ge(dtu_ready, k * IC + IC)
                        if i == 0:
                            pool.wait_ge(sh_free, pre_tile(k, J_B + n) + 1)
                        pool.wait_ge(scan_done, k * UNITS + v - R_DBU + 1 + CREDIT)
                        nc.gpsimd.tensor_tensor(dbu[:, v % R_DBU, :], dtu[h][:, i, :], ball[:, n, :],
                                                ALU.mult).then_inc(m1_done, 1)
                        if not last:
                            pre(k + 1, v, 1 - h)

                nc.gpsimd.memset(upad[:], 0.0).then_inc(zeroed, 1)
                for slot in range(UNITS):
                    pre(0, slot, 0)
                for h in range(2):
                    step(0, h, h == 0, False)
                with pool.Fori(1, NL - 1) as l:
                    for h in range(2):
                        step(l, h, False, False)
                for h in range(2):
                    step(NL - 1, h, False, h == 1)

            @block.scalar
            def _(act):
                def diagonals(l):
                    for i in range(IC):
                        for t in range(K):
                            nc.scalar.activation(cdiag[:, i, t, :], ident[:], ACT.Copy,
                                                 scale=chan[:, i, t:t + 1]).then_inc(diag_ready, 1)

                def take(p, j, out, view, func=ACT.Identity, **kw):
                    act.wait_ge(sh_full, pre_tile(p, j) + 1)
                    return nc.scalar.activation(out, view, func, **kw)

                def pre(p, slot, o):
                    if slot == 8:
                        for j in range(HNT):
                            nc.scalar.activation(sq[:], xres[:, o * HNT + j, :], ACT.Square,
                                                 accum_out=ssq[:, j:j + 1]).then_inc(sq_done, 1)
                            act.wait_ge(sq_done, p * HNT + j + 1)
                        nc.scalar.activation(rrms[:], ssq[:], ACT.Ln, bias=eps5[:TT, 0:1], scale=1.0 / D
                                             ).then_inc(rms_ln, 1)
                        act.wait_ge(rms_ln, p + 1)
                        nc.scalar.activation(rrms[:], rrms[:], ACT.Exp, scale=-0.5).then_inc(rms_ready, 1)
                    if slot in (11, 12):
                        c = slot - 11
                        take(p, J_TR + c, hT[:, c, :], shared[:DP, :HT], scale=nw[:, c:c + 1]
                             ).then_inc(sh_free, 1)
                    if slot in (13, 14, 15):
                        i = slot - 13
                        take(p, J_U + i, upad[:, i, :, K - 1:],
                             shared[:, :HT].rearrange("q (b t) -> q b t", t=SEQ)).then_inc(sh_free, 1)
                    if slot in (16, 20, 21):
                        i = (16, 20, 21).index(slot)
                        take(p, J_Z0 if i == 0 else J_Z1 + i - 1, zraw[:, i, :], shared[:, :HT]
                             ).then_inc(sh_free, 1)
                    if slot in (17, 18, 19):
                        i = slot - 17
                        take(p, J_CONV + i, uc[:, i, :], shared[:, :HT], bias=chan[:, i, K:K + 1]
                             ).then_inc(sh_free, 1)
                    if slot in (20, 21, 22):
                        i = slot - 20
                        act.wait_ge(uclamp, p * IC + i + 1)
                        nc.scalar.activation(gA[:, i, :], gA[:, i, :], ACT.Exp, scale=-1.0).then_inc(uexp, 1)
                        act.wait_ge(uexp, p * IC + i + 1)
                        nc.scalar.activation(gA[:, i, :], gA[:, i, :], ACT.Ln, bias=one[:, 0:1]).then_inc(uln, 1)
                        act.wait_ge(uln, p * IC + i + 1)
                        nc.scalar.activation(gA[:, i, :], gA[:, i, :], ACT.Exp, scale=-1.0).then_inc(usig, 1)
                    if slot in (23, 24, 25):
                        i = slot - 23
                        act.wait_ge(zclamp, p * IC + i + 1)
                        nc.scalar.activation(gZ[:, i, :], gZ[:, i, :], ACT.Exp, scale=-1.0).then_inc(zexp, 1)
                        act.wait_ge(zexp, p * IC + i + 1)
                        nc.scalar.activation(gZ[:, i, :], gZ[:, i, :], ACT.Ln, bias=one[:, 0:1]).then_inc(zln, 1)
                        act.wait_ge(zln, p * IC + i + 1)
                        nc.scalar.activation(gZ[:, i, :], gZ[:, i, :], ACT.Exp, scale=-1.0).then_inc(zsig, 1)
                    if slot == 26:
                        take(p, J_XP, dtr[:], shared[:R, :HT]).then_inc(bc_hi, 1)
                        nc.scalar.activation(parts[o][0:NBC, :], shared[BC0:XR, :HT], ACT.Identity
                                             ).then_inc(bc_hi, 1)
                    if slot in (28, 29, 30):
                        i = slot - 28
                        take(p, J_DT + i, uc[:, i, :], shared[:, :HT], bias=chan[:, i, K + 1:K + 2]
                             ).then_inc(sh_free, 1)
                    if slot in (31, 32, 33):
                        i = slot - 31
                        act.wait_ge(dclamp, p * IC + i + 1)
                        nc.scalar.activation(gA[:, i, :], gA[:, i, :], ACT.Exp).then_inc(dexp, 1)
                        act.wait_ge(dexp, p * IC + i + 1)
                        nc.scalar.activation(gC[:, i, :], gA[:, i, :], ACT.Identity, bias=third[:, 0:1],
                                             scale=-0.25).then_inc(dpoly4, 1)
                        nc.scalar.activation(gB[:, i, :], gA[:, i, :], ACT.Ln, bias=one[:, 0:1]).then_inc(dln, 1)
                    if 31 <= slot < 31 + NS:
                        n = slot - 31
                        if prev_units is not None:
                            act.wait_ge(m1_done, prev_units + n * IC + IC)
                        take(p, J_B + n, ball[:, n, :], shared[:, :HT]).then_inc(sh_free, 1)

                prev_units = None
                act.wait_ge(zeroed, 5)
                act.wait_ge(pre_in, 80)
                diagonals(0)
                for slot in range(UNITS):
                    pre(0, slot, 0)

                def step(l, h, first, last):
                    nonlocal prev_units
                    k = l * 2 + h
                    prev_units = k * UNITS
                    if h == 0:
                        act.wait_ge(alog_in, l * 16 + 16)
                        if not first:
                            act.wait_ge(exp_done, k * UNITS)
                        nc.scalar.activation(nega[:], alog[:], ACT.Exp).then_inc(nega_exp, 1)
                        act.wait_ge(nega_exp, l + 1)
                        nc.scalar.mul(nega[:], nega[:], -1.0).then_inc(nega_ready, 1)
                        act.wait_ge(nega_ready, l + 1)
                    for v in range(UNITS):
                        n, i = divmod(v, IC)
                        if v == 0:
                            act.wait_ge(dt_ready, k * IC + IC)
                        act.wait_ge(scan_done, k * UNITS + v - R_DA + 1 + CREDIT)
                        nc.scalar.activation(
                            dab[v % R_DA][:, :HT].rearrange("q (b t) -> q b t", t=SEQ)[:, :, 1:],
                            dt[h][:, i, :].rearrange("q (b t) -> q b t", t=SEQ)[:, :, 1:],
                            ACT.Exp, scale=nega[:, i * NS + n:i * NS + n + 1]).then_inc(exp_done, 1)
                        if not last:
                            if h == 1 and v == 0:
                                act.wait_ge(pre_in, l * 80 + 160)
                                diagonals(l + 1)
                            if v == 8 and not first:
                                act.wait_ge(sh_free, post_tile(k, 1) + 1)
                            pre(k + 1, v, 1 - h)

                for h in range(2):
                    step(0, h, h == 0, False)
                with act.Fori(1, NL - 1) as l:
                    for h in range(2):
                        step(l, h, False, False)
                for h in range(2):
                    step(NL - 1, h, False, h == 1)

            @block.vector
            def _(dve):
                def pre(p, slot, o):
                    if slot == 9:
                        dve.wait_ge(rms_ready, p + 1)
                        for j in range(HNT):
                            nc.vector.tensor_scalar(xn[:, j, :], xres[:, o * HNT + j, :], rrms[:, j:j + 1],
                                                    None, ALU.mult).then_inc(xn_ready, 1)
                    if slot in (18, 19, 20):
                        i = slot - 18
                        dve.wait_ge(sh_free, pre_tile(p, J_CONV + i) + 1)
                        nc.vector.tensor_scalar(gA[:, i, :], uc[:, i, :], -40.0, None, ALU.max
                                                ).then_inc(uclamp, 1)
                    if slot in (22, 23, 24):
                        i = slot - 22
                        dve.wait_ge(sh_free, pre_tile(p, J_Z0 if i == 0 else J_Z1 + i - 1) + 1)
                        nc.vector.tensor_scalar(gZ[:, i, :], zraw[:, i, :], -40.0, None, ALU.max
                                                ).then_inc(zclamp, 1)
                    if slot == 26:
                        dve.wait_ge(bc_hi, p * 2 + 2)
                        nc.vector.tensor_tensor(resid[NBC:2 * NBC, :], shared[BC0:XR, :HT], parts[o][0:NBC, :],
                                                ALU.subtract).then_inc(sh_free, 1)
                    if slot == 27:
                        dve.wait_ge(sh_free, pre_tile(p, J_XP) + 1)
                        nc.vector.tensor_copy(parts[o][NBC:2 * NBC, :], resid[NBC:2 * NBC, :]).then_inc(bc_mid, 1)
                        dve.wait_ge(bc_mid, p + 1)
                        nc.vector.tensor_tensor(parts[o][2 * NBC:XR, :], resid[NBC:2 * NBC, :],
                                                parts[o][NBC:2 * NBC, :], ALU.subtract).then_inc(parts_ready, 1)
                    if slot in (29, 30, 31):
                        i = slot - 29
                        dve.wait_ge(sh_free, pre_tile(p, J_DT + i) + 1)
                        nc.vector.tensor_scalar(gA[:, i, :], uc[:, i, :], 17.0, None, ALU.min
                                                ).then_inc(dclamp, 1)
                    if slot in (35, 36, 37):
                        i = slot - 35
                        dve.wait_ge(dpoly3, p * IC + i + 1)
                        nc.vector.scalar_tensor_tensor(gD[:, i, :], gC[:, i, :], -0.5, gA[:, i, :],
                                                       ALU.add, ALU.mult).then_inc(dpoly, 1)
                        dve.wait_ge(dpoly, (p * IC + i) * 3 + 1)
                        nc.vector.scalar_tensor_tensor(gD[:, i, :], gD[:, i, :], 1.0, gA[:, i, :],
                                                       ALU.add, ALU.mult).then_inc(dpoly, 1)
                        dve.wait_ge(dpoly, (p * IC + i) * 3 + 2)
                        dve.wait_ge(dln, p * IC + i + 1)
                        nc.vector.scalar_tensor_tensor(gD[:, i, :], gB[:, i, :], -LN_SLACK, gD[:, i, :],
                                                       ALU.add, ALU.max).then_inc(dpoly, 1)
                        dve.wait_ge(dpoly, (p * IC + i) * 3 + 3)
                        nc.vector.tensor_tensor(dt[o][:, i, :], gD[:, i, :], uc[:, i, :], ALU.max
                                                ).then_inc(dt_ready, 1)

                def finish_y(k, o, loads):
                    dve.wait_ge(post_in, loads)
                    dve.wait_ge(reduce_done, k * UNITS)
                    for i in range(IC):
                        nc.vector.scalar_tensor_tensor(y[:, i, :], u[o][:, i, :], dskip[:, i:i + 1],
                                                       yacc[i][:, :HT], ALU.mult, ALU.add).then_inc(yfin, 1)
                    for i in range(IC):
                        dve.wait_ge(yfin, (k - 1) * IC + i + 1)
                        if i == 0:
                            dve.wait_ge(z_ready, k * IC)
                        nc.vector.tensor_tensor(y[:, i, :], y[:, i, :], zs[o][:, i, :], ALU.mult
                                                ).then_inc(y_ready, 1)

                def add_residual(k, o, i):
                    dve.wait_ge(sh_full, post_tile(k, i) + 1)
                    j = o * HNT + 2 * i
                    nc.vector.tensor_tensor(xres[:, j:j + 2, :], xres[:, j:j + 2, :],
                                            shared[:TT, :2 * D].rearrange("q (a d) -> q a d", a=2),
                                            ALU.add).then_inc(sh_free, 1)

                def times_c(k, h, v):
                    n, i = divmod(v, IC)
                    dve.wait_ge(scan_done, k * UNITS + v + 1 + CREDIT)
                    dve.wait_ge(c_ready, k * NS + n + 1)
                    if v >= R_HC:
                        dve.wait_ge(reduce_done, k * UNITS + v - R_HC + 1)
                    nc.vector.tensor_tensor(hc[:, v % R_HC, :], hst[:, v % R_H, :], cbank[n % 2][:, :HT],
                                            ALU.mult).then_inc(m2_done, 1)

                def step(l, h, first, last):
                    k = l * 2 + h
                    for v in range(UNITS):
                        n, i = divmod(v, IC)
                        dve.wait_ge(exp_done, k * UNITS + v + 1)
                        dve.wait_ge(m1_done, k * UNITS + v + 1)
                        if v == 0 and not first:
                            dve.wait_ge(m2_done, k * UNITS)
                        if v >= R_H:
                            dve.wait_ge(m2_done, k * UNITS + v - R_H + 1)
                        nc.vector.tensor_tensor_scan(hst[:, v % R_H, :], dab[v % R_DA][:, :HT],
                                                     dbu[:, v % R_DBU, :], 0.0, ALU.mult, ALU.add
                                                     ).then_inc(scan_done, 1)
                        if v == 1 and not first:
                            finish_y(k, 1 - h, l * 32 + 32 * h)
                        if v >= 1:
                            times_c(k, h, v - 1)
                        if v in (5, 7) and not first:
                            add_residual(k, 1 - h, (v - 5) // 2)
                        if not last:
                            pre(k + 1, v, 1 - h)
                    times_c(k, h, UNITS - 1)

                nc.vector.memset(one[:], 1.0).then_inc(zeroed, 1)
                nc.vector.memset(third[:], 1.0 / 3.0).then_inc(zeroed, 1)
                for b in dab:
                    nc.vector.memset(b[:], 0.0).then_inc(zeroed, 1)
                for r in range(R_DBU):
                    nc.vector.memset(dbu[:, r, 0:1], 0.0).then_inc(scan_done, 1)
                dve.wait_ge(id3_in, 16)
                nc.vector.tensor_copy(sel[:], id3[:].rearrange("q (n o) -> q n o", o=1).to_broadcast([XR, NBC, 128])
                                      ).then_inc(sel_ready, 1)
                dve.wait_ge(zeroed, 5)
                for slot in range(UNITS):
                    pre(0, slot, 0)
                for h in range(2):
                    step(0, h, h == 0, False)
                with dve.Fori(1, NL - 1) as l:
                    for h in range(2):
                        step(l, h, False, False)
                for h in range(2):
                    step(NL - 1, h, False, h == 1)
                finish_y(2 * NL, 1, NL * 32)
                for i in range(NPOST):
                    add_residual(2 * NL, 1, i)

            @block.tensor
            def _(pe):
                def open_shared(t):
                    if not (isinstance(t, int) and t == 0):
                        pe.wait_ge(sh_free, t)

                def pre(p, slot, o, diagonals):
                    if slot in (10, 11):
                        c = slot - 10
                        open_shared(pre_tile(p, J_TR + c))
                        pe.wait_ge(xn_ready, p * HNT + HNT)
                        for j in range(HNT):
                            mm = nc.tensor.transpose(shared[:DP, j * TT:(j + 1) * TT],
                                                     xn[:, j, c * DP:(c + 1) * DP], ident[:TT, :TT])
                        mm.then_inc(sh_full, 1)
                    if slot in (12, 13, 14, 15, 19, 20):
                        q = (12, 13, 14, 15, 19, 20).index(slot)
                        j = J_U + q if q < 4 else J_Z1 + q - 4
                        open_shared(pre_tile(p, j))
                        for c in range(DC):
                            mm = nc.tensor.matmul(shared[:, :HT], win[:, c, q * 128:(q + 1) * 128], hT[:, c, :],
                                                  start=(c == 0), stop=(c == DC - 1))
                        mm.then_inc(sh_full, 1)
                    if slot in (16, 17, 18):
                        i = slot - 16
                        open_shared(pre_tile(p, J_CONV + i))
                        if i == 0:
                            pe.wait_ge(diag_ready, diagonals)
                        for t in range(K):
                            mm = nc.tensor.matmul(shared[:, :HT], cdiag[:, i, t, :], upad[:, i, :, t:t + SEQ],
                                                  start=(t == 0), stop=(t == K - 1))
                        mm.then_inc(sh_full, 1)
                    if slot == 25:
                        open_shared(pre_tile(p, J_XP))
                        pe.wait_ge(u_ready, p * IC + IC)
                        for i in range(IC):
                            mm = nc.tensor.matmul(shared[:XR, :HT], wxp[:, i, :], u[o][:, i, :],
                                                  start=(i == 0), stop=(i == IC - 1))
                        mm.then_inc(sh_full, 1)
                    if slot in (27, 28, 29):
                        i = slot - 27
                        open_shared(pre_tile(p, J_DT + i))
                        nc.tensor.matmul(shared[:, :HT], wdt[:, i * 128:(i + 1) * 128], dtr[:],
                                         start=True, stop=True).then_inc(sh_full, 1)
                    if 30 <= slot < 30 + NS:
                        n = slot - 30
                        open_shared(pre_tile(p, J_B + n))
                        if n == 0:
                            pe.wait_ge(parts_ready, p + 1)
                        nc.tensor.matmul(shared[:, :HT], sel[:, n, :], parts[o][:], start=True, stop=True
                                         ).then_inc(sh_full, 1)

                def out_projection(k, i):
                    open_shared(post_tile(k, i))
                    if i == 0:
                        pe.wait_ge(y_ready, k * IC)
                    for jj in range(2):
                        j = 2 * i + jj
                        for c in range(IC):
                            mm = nc.tensor.matmul(shared[:TT, jj * D:(jj + 1) * D], y[:, c, j * TT:(j + 1) * TT],
                                                  wout[:, c, :], start=(c == 0), stop=(c == IC - 1))
                    mm.then_inc(sh_full, 1)

                def broadcast_c(k, h, n):
                    if n >= 2:
                        pe.wait_ge(m2_done, k * UNITS + (n - 1) * IC)
                    nc.tensor.matmul(cbank[n % 2][:, :HT], sel[:, NS + n, :], parts[h][:], start=True, stop=True
                                     ).then_inc(c_ready, 1)

                def reduce(k, v):
                    n, i = divmod(v, IC)
                    pe.wait_ge(m2_done, k * UNITS + v + 1)
                    if n == 0 and not (isinstance(k, int) and k == 0):
                        pe.wait_ge(yfin, (k - 1) * IC + i + 1)
                    nc.tensor.matmul(yacc[i][:, :HT], ident[:], hc[:, v % R_HC, :], start=(n == 0),
                                     stop=(n == NS - 1)).then_inc(reduce_done, 1)

                def step(l, h, first, last):
                    k = l * 2 + h
                    broadcast_c(k, h, 0)
                    for v in range(UNITS):
                        n, i = divmod(v, IC)
                        if i == 0 and n + 1 < NS:
                            broadcast_c(k, h, n + 1)
                        if v in (4, 6) and not first:
                            out_projection(k, (v - 4) // 2)
                        if not last:
                            if h == 1 and v == 12:
                                pe.wait_ge(pre_in, l * 80 + 160)
                            pre(k + 1, v, 1 - h, (l + 1 + h) * IC * K)
                        if v >= 2:
                            reduce(k, v - 2)
                    reduce(k, UNITS - 2)
                    reduce(k, UNITS - 1)

                pe.wait_ge(zeroed, 5)
                pe.wait_ge(sel_ready, 1)
                pe.wait_ge(pre_in, 80)
                for slot in range(UNITS):
                    pre(0, slot, 0, IC * K)
                for h in range(2):
                    step(0, h, h == 0, False)
                with pe.Fori(1, NL - 1) as l:
                    for h in range(2):
                        step(l, h, False, False)
                for h in range(2):
                    step(NL - 1, h, False, h == 1)
                for i in range(NPOST):
                    out_projection(2 * NL, i)


def gating_program(nc, a, h0, xres, eps5, ident, xl, zT, cw, cws):
    with ExitStack() as ctx:
        def sb(name, shape, dt=fp32):
            return ctx.enter_context(nc.sbuf_tensor(name, shape, dt))

        def sem(name):
            return ctx.enter_context(nc.semaphore(name))

        fnw = sb("fnw", [TT, D])
        gw = sb("gw", [DP, DC, E])
        trif, onesf = sb("trif", [TT, TT]), sb("onesf", [TT, TT])
        tri, ones = sb("tri", [TT, TT], bf16), sb("ones", [TT, TT], bf16)
        rank = sb("rank", [TT, NT, E])
        eps6 = sb("eps6", [128, 1])
        sq, sq2 = sb("sqe", [TT, NT, D]), sb("sqf", [TT, NT, D])
        ssq, ssq2 = sb("ssqe", [TT, NT]), sb("ssqf", [TT, NT])
        rrms, rstd, rrms2 = sb("rrmse", [TT, NT]), sb("rstde", [TT, NT]), sb("rrmsf", [TT, NT])
        stats, mv = sb("statse", [TT, NT, 6]), sb("mve", [TT, NT, 2])
        zt = sb("zt", [TT, NT, D])
        xT = sb("xT", [DP, DC, NTOK])
        lg, lg2 = sb("lg", [TT, NT, E]), sb("lg2", [TT, NT, E])
        mask1, mask2 = sb("mask1", [TT, NT, E]), sb("mask2", [TT, NT, E])
        both = sb("both", [TT, NT, E], bf16)
        top1, top2, idx = sb("top1", [TT, NT]), sb("top2", [TT, NT]), sb("idx", [TT, NT])
        w1, w2 = sb("w1", [TT, NT]), sb("w2", [TT, NT])
        keep = sb("keep", [TT, NT, E])
        pb = [ctx.enter_context(nc.psum_tensor(f"pg{i}", [128, 512], fp32)) for i in range(6)]
        plogit, pplace = pb[4], pb[5]

        const_in, own = sem("const_in"), sem("vector_chain")
        eps_set, sq_done, ln1, rms_ready, mv_ready, ln2, std_ready, xl_ready = (
            sem("eps_set"), sem("sqe_done"), sem("ln1"), sem("rmse_ready"), sem("mve_ready"), sem("ln2"),
            sem("std_ready"), sem("xl_ready"))
        sq2_done, ln3, rms2_ready, zt_ready = sem("sqf_done"), sem("ln3"), sem("rmsf_ready"), sem("zt_ready")
        xt_full, xt_copied, zt_full, zt_copied = (sem("xt_full"), sem("xt_copied"), sem("zt_full"),
                                                  sem("zt_copied"))
        logits_full, logits_ready, gap_ready, gap_exp, both_ready, places_full, tri_ready = (
            sem("logits_full"), sem("logits_ready"), sem("gap_ready"), sem("gap_exp"), sem("both_ready"),
            sem("places_full"), sem("tri_ready"))

        with nc.Block() as block:
            @block.sync
            def _(sp):
                for dst, src in ((fnw, "fnw"), (gw, "gw"), (trif, "tri"), (onesf, "ones"), (rank, "rank")):
                    sp.dma_start(dst[:], a[src]).then_inc(const_in, 16)

            @block.scalar
            def _(act):
                for j in range(NT):
                    nc.scalar.activation(sq[:, j, :], xres[:, j, :], ACT.Square, accum_out=ssq[:, j:j + 1]
                                         ).then_inc(sq_done, 1)
                act.wait_ge(sq_done, NT)
                nc.scalar.activation(rrms[:], ssq[:], ACT.Ln, bias=eps5[:TT, 0:1], scale=1.0 / D).then_inc(ln1, 1)
                act.wait_ge(ln1, 1)
                nc.scalar.activation(rrms[:], rrms[:], ACT.Exp, scale=-0.5).then_inc(rms_ready, 1)
                act.wait_ge(mv_ready, NT)
                nc.scalar.activation(rstd[:], mv[:, :, 1], ACT.Ln, bias=eps5[:TT, 0:1]).then_inc(ln2, 1)
                act.wait_ge(ln2, 1)
                nc.scalar.activation(rstd[:], rstd[:], ACT.Exp, scale=-0.5).then_inc(std_ready, 1)
                for j in range(NT):
                    act.wait_ge(xl_ready, j + 1)
                    nc.scalar.activation(sq2[:, j, :], xl[:, j, :], ACT.Square, accum_out=ssq2[:, j:j + 1]
                                         ).then_inc(sq2_done, 1)
                act.wait_ge(sq2_done, NT)
                act.wait_ge(eps_set, 1)
                nc.scalar.activation(rrms2[:], ssq2[:], ACT.Ln, bias=eps6[:TT, 0:1], scale=4.0 / D).then_inc(ln3, 1)
                act.wait_ge(ln3, 1)
                nc.scalar.activation(rrms2[:], rrms2[:], ACT.Exp, scale=-0.5).then_inc(rms2_ready, 1)
                for b in range(2 * DC):
                    c, hf = divmod(b, 2)
                    act.wait_ge(xt_full, b + 1)
                    nc.scalar.copy(xT[:, c, hf * HT:(hf + 1) * HT], pb[b][:DP, :HT]).then_inc(xt_copied, 1)
                act.wait_ge(logits_full, 1)
                nc.scalar.copy(lg[:].rearrange("q j e -> q (j e)"), plogit[:TT, :NT * E]).then_inc(logits_ready, 1)
                for b in range(2 * DC):
                    c, hf = divmod(b, 2)
                    act.wait_ge(zt_full, b + 1)
                    nc.scalar.copy(zT[:, c, hf * HT:(hf + 1) * HT], pb[b][:DP, :HT]).then_inc(zt_copied, 1)
                act.wait_ge(gap_ready, 1)
                nc.scalar.activation(w2[:], w2[:], ACT.Exp).then_inc(gap_exp, 1)

            @block.tensor
            def _(pe):
                def transposes(src, ready, full, copied):
                    for b in range(2 * DC):
                        c, hf = divmod(b, 2)
                        pe.wait_ge(ready, hf * HNT + HNT)
                        if copied is not None:
                            pe.wait_ge(copied, b + 1)
                        for jj in range(HNT):
                            mm = nc.tensor.transpose(pb[b][:DP, jj * TT:(jj + 1) * TT],
                                                     src[:, hf * HNT + jj, c * DP:(c + 1) * DP], ident[:TT, :TT])
                        mm.then_inc(full, 1)

                transposes(xl, xl_ready, xt_full, None)
                pe.wait_ge(const_in, 80)
                pe.wait_ge(xt_copied, 2 * DC)
                for j in range(NT):
                    for c in range(DC):
                        mm = nc.tensor.matmul(plogit[:TT, j * E:(j + 1) * E], xT[:, c, j * TT:(j + 1) * TT],
                                              gw[:, c, :], start=(c == 0), stop=(c == DC - 1))
                mm.then_inc(logits_full, 1)
                transposes(zt, zt_ready, zt_full, xt_copied)
                pe.wait_ge(tri_ready, 2)
                pe.wait_ge(both_ready, 1)
                for j in range(NT):
                    for jj in range(j):
                        nc.tensor.matmul(pplace[:TT, j * E:(j + 1) * E], ones[:], both[:, jj, :],
                                         start=(jj == 0), stop=False)
                    mm = nc.tensor.matmul(pplace[:TT, j * E:(j + 1) * E], tri[:], both[:, j, :],
                                          start=(j == 0), stop=True)
                mm.then_inc(places_full, 1)

            @block.vector
            def _(dve):
                n = [0]

                def link(ins):
                    n[0] += 1
                    ins.then_inc(own, 1)
                    dve.wait_ge(own, n[0])

                vec = nc.vector
                vec.memset(eps6[:], 1e-6).then_inc(eps_set, 1)
                dve.wait_ge(const_in, 80)
                vec.tensor_copy(tri[:], trif[:]).then_inc(tri_ready, 1)
                vec.tensor_copy(ones[:], onesf[:]).then_inc(tri_ready, 1)
                dve.wait_ge(rms_ready, 1)
                for j in range(NT):
                    link(vec.scalar_tensor_tensor(xl[:, j, :], xres[:, j, :], rrms[:, j:j + 1], fnw[:],
                                                  ALU.mult, ALU.mult))
                    link(vec.tensor_tensor(h0[:, j, :], h0[:, j, :], xl[:, j, :], ALU.add))
                    link(vec.bn_stats(stats[:, j, :], h0[:, j, :]))
                    vec.bn_aggr(mv[:, j, :], stats[:, j, :]).then_inc(mv_ready, 1)
                dve.wait_ge(std_ready, 1)
                for j in range(NT):
                    vec.tensor_scalar(xl[:, j, :], h0[:, j, :], mv[:, j, 0:1], rstd[:, j:j + 1],
                                      ALU.subtract, ALU.mult).then_inc(xl_ready, 1)
                dve.wait_ge(rms2_ready, 1)
                for j in range(NT):
                    vec.tensor_scalar(zt[:, j, :], xl[:, j, :], rrms2[:, j:j + 1], 2.0, ALU.mult, ALU.mult
                                      ).then_inc(zt_ready, 1)

                def spread(t):
                    return t[:].rearrange("q (j o) -> q j o", o=1).to_broadcast([TT, NT, E])

                def pick(logits, top, mask):
                    link(vec.tensor_reduce(top[:], logits[:], AX.X, ALU.max))
                    link(vec.tensor_tensor(mask[:], logits[:], spread(top), ALU.is_equal))
                    link(vec.tensor_tensor(mask[:], mask[:], rank[:], ALU.mult))
                    link(vec.tensor_reduce(idx[:], mask[:], AX.X, ALU.max))
                    link(vec.tensor_tensor(mask[:], rank[:], spread(idx), ALU.is_equal))

                dve.wait_ge(logits_ready, 1)
                pick(lg, top1, mask1)
                link(vec.tensor_scalar(lg2[:], mask1[:], -3.0e38, None, ALU.mult))
                link(vec.tensor_tensor(lg2[:], lg2[:], lg[:], ALU.add))
                pick(lg2, top2, mask2)
                vec.tensor_tensor(both[:], mask1[:], mask2[:], ALU.add).then_inc(both_ready, 1)
                vec.tensor_tensor(w2[:], top2[:], top1[:], ALU.subtract).then_inc(gap_ready, 1)
                dve.wait_ge(gap_exp, 1)
                link(vec.tensor_scalar(w1[:], w2[:], 1.0, None, ALU.add))
                link(vec.reciprocal(w1[:], w1[:]))
                link(vec.tensor_tensor(w2[:], w2[:], w1[:], ALU.mult))
                link(vec.tensor_tensor(mask1[:], mask1[:], spread(w1), ALU.mult))
                link(vec.tensor_tensor(mask2[:], mask2[:], spread(w2), ALU.mult))
                link(vec.tensor_tensor(mask1[:], mask1[:], mask2[:], ALU.add))
                dve.wait_ge(places_full, 1)
                link(vec.tensor_scalar(keep[:].rearrange("q j e -> q (j e)"), pplace[:TT, :NT * E],
                                       float(CAP), None, ALU.is_lt))
                link(vec.tensor_tensor(cw[:], mask1[:], keep[:], ALU.mult))
                link(vec.tensor_reduce(cws[:], cw[:], AX.X, ALU.add))


def expert_program(nc, a, h0, xl, zT, cw, cws, out):
    with ExitStack() as ctx:
        def sb(name, shape, dt=fp32):
            return ctx.enter_context(nc.sbuf_tensor(name, shape, dt))

        def sem(name):
            return ctx.enter_context(nc.semaphore(name))

        enw = sb("enw", [DP, DC, E])
        acc = sb("acc", [TT, NT, D])
        w13 = [sb(f"w13_{b}", [DP, DC, 2 * FF]) for b in range(2)]
        wd = [sb(f"wd_{b}", [128, FC, D]) for b in range(2)]
        ze = [sb(f"ze{b}", [DP, DC, NTOK]) for b in range(2)]
        sg = [sb(f"sg{b}", [128, HT]) for b in range(2)]
        hid = [sb(f"hid{b}", [128, FC, HT]) for b in range(2)]
        pb = [ctx.enter_context(nc.psum_tensor(f"px{i}", [128, 512], fp32)) for i in range(8)]
        gbank, ubank, ybank = pb[0:2], pb[2:4], pb[4:8]
        enw_in, w_in = sem("enw_in"), [sem(f"we_in{b}") for b in range(2)]
        ze_ready, gu_ready, silu_ready, hid_ready, y_ready, acc_ready, out_done = (
            sem("ze_ready"), sem("gu_ready"), sem("silu_ready"), sem("hid_ready"), sem("ye_ready"),
            sem("acc_ready"), sem("out_done"))
        GU, YT = 4 * FC, 4 * HNT

        with nc.Block() as block:
            @block.sync
            def _(sp):
                def load(e, b):
                    sp.dma_start(w13[b][:], a["w13"][bass.ds(e, 1)].rearrange("o p a b -> p (o a) b")
                                 ).then_inc(w_in[b], 16)
                    sp.dma_start(wd[b][:], a["wd"][bass.ds(e, 1)].rearrange("o p a b -> p (o a) b")
                                 ).then_inc(w_in[b], 16)

                sp.dma_start(enw[:], a["enw"]).then_inc(enw_in, 16)
                load(0, 0)
                load(1, 1)
                with sp.Fori(0, E // 2 - 1) as q:
                    for b in range(2):
                        sp.wait_ge(y_ready, q * YT + (b + 1) * NT)
                        load(q * 2 + (2 + b), b)
                outv = out.rearrange("(j g) t d -> j (g t) d", j=NT)
                for j in range(NT):
                    sp.wait_ge(acc_ready, NT + E * NT + j + 1)
                    sp.dma_start(outv[j], acc[:, j, :]).then_inc(out_done, 16)
                sp.wait_ge(out_done, 16 * NT)

            @block.tensor
            def _(pe):
                def gate_up(q, m):
                    b, hf = divmod(m, 2)
                    if hf == 0:
                        pe.wait_ge(w_in[b], q * 32 + 32)
                        pe.wait_ge(ze_ready, (q * 2 + b) * DC + DC)
                    for t in range(FC):
                        if m * FC + t >= 2:
                            pe.wait_ge(hid_ready, q * GU + m * FC + t - 1)
                        for bank, off in ((gbank[t % 2], 0), (ubank[t % 2], FF)):
                            for c in range(DC):
                                mm = nc.tensor.matmul(bank[:, :HT], w13[b][:, c, off + t * 128:off + (t + 1) * 128],
                                                      ze[b][:, c, hf * HT:(hf + 1) * HT], start=(c == 0),
                                                      stop=(c == DC - 1))
                        mm.then_inc(gu_ready, 1)

                def down(q, m):
                    b, hf = divmod(m, 2)
                    pe.wait_ge(hid_ready, q * GU + (m + 1) * FC)
                    for jj in range(HNT):
                        y = m * HNT + jj
                        pe.wait_ge(acc_ready, q * YT + (NT + y - len(ybank) + 1))
                        for t in range(FC):
                            mm = nc.tensor.matmul(ybank[jj][:TT, :D], hid[hf][:, t, jj * TT:(jj + 1) * TT],
                                                  wd[b][:, t, :], start=(t == 0), stop=(t == FC - 1))
                        mm.then_inc(y_ready, 1)

                with pe.Fori(0, E // 2) as q:
                    gate_up(q, 0)
                    for m in range(3):
                        gate_up(q, m + 1)
                        down(q, m)
                    down(q, 3)

            @block.scalar
            def _(act):
                with act.Fori(0, E // 2) as q:
                    for m in range(4):
                        for t in range(FC):
                            act.wait_ge(gu_ready, q * GU + m * FC + t + 1)
                            nc.scalar.activation(sg[t % 2][:], gbank[t % 2][:, :HT], ACT.Silu
                                                 ).then_inc(silu_ready, 1)

            @block.vector
            def _(dve):
                def expert_norm(q, b):
                    e = q * 2 + b
                    for c in range(DC):
                        nc.vector.tensor_scalar(ze[b][:, c, :], zT[:, c, :], enw[:, c, bass.ds(e, 1)], None,
                                                ALU.mult).then_inc(ze_ready, 1)

                def hidden(q, m):
                    for t in range(FC):
                        dve.wait_ge(silu_ready, q * GU + m * FC + t + 1)
                        nc.vector.tensor_tensor(hid[m % 2][:, t, :], sg[t % 2][:], ubank[t % 2][:, :HT], ALU.mult
                                                ).then_inc(hid_ready, 1)

                def weigh(q, m):
                    b, hf = divmod(m, 2)
                    for jj in range(HNT):
                        y, j = m * HNT + jj, hf * HNT + jj
                        dve.wait_ge(y_ready, q * YT + y + 1)
                        dve.wait_ge(acc_ready, q * YT + y + 1)
                        nc.vector.scalar_tensor_tensor(acc[:, j, :], ybank[jj][:TT, :D],
                                                       cw[:, j, bass.ds(q * 2 + b, 1)], acc[:, j, :],
                                                       ALU.mult, ALU.add).then_inc(acc_ready, 1)

                for j in range(NT):
                    nc.vector.tensor_scalar(acc[:, j, :], xl[:, j, :], cws[:, j:j + 1], None, ALU.mult
                                            ).then_inc(acc_ready, 1)
                dve.wait_ge(enw_in, 16)
                with dve.Fori(0, E // 2) as q:
                    expert_norm(q, 0)
                    hidden(q, 0)
                    expert_norm(q, 1)
                    hidden(q, 1)
                    weigh(q, 0)
                    hidden(q, 2)
                    weigh(q, 1)
                    hidden(q, 3)
                    weigh(q, 2)
                    weigh(q, 3)
                for j in range(NT):
                    dve.wait_ge(acc_ready, E * NT + j + 1)
                    nc.vector.tensor_tensor(acc[:, j, :], acc[:, j, :], h0[:, j, :], ALU.add).then_inc(acc_ready, 1)


def build(nc, a, out):
    with ExitStack() as ctx:
        def sb(name, shape):
            return ctx.enter_context(nc.sbuf_tensor(name, shape, fp32))

        h0 = sb("h0", [TT, NT, D])
        xres = sb("xres", [TT, NT, D])
        eps5 = sb("eps5", [128, 1])
        ident = sb("ident", [128, 128])
        ident_in = ctx.enter_context(nc.semaphore("ident_in"))
        with nc.Block() as block:
            @block.sync
            def _(sp):
                sp.dma_start(ident[:], a["ident"]).then_inc(ident_in, 16)
                sp.wait_ge(ident_in, 16)
        embed_program(nc, a, h0, xres, eps5)
        mamba_program(nc, a, xres, eps5, ident)
        xl, zT = sb("xl", [TT, NT, D]), sb("zT", [DP, DC, NTOK])
        cw, cws = sb("cw", [TT, NT, E]), sb("cws", [TT, NT])
        gating_program(nc, a, h0, xres, eps5, ident, xl, zT, cw, cws)
        expert_program(nc, a, h0, xl, zT, cw, cws, out)


def kernel(**inputs):
    import numpy as np
    import concourse.bacc as bacc
    from concourse.bass_utils import run_bass_kernel_spmd

    g = {name: np.asarray(v) for name, v in inputs.items()}
    f = lambda name: g[name]
    rows = lambda t, p: t.reshape(t.shape[0], t.shape[1] // p, p, *t.shape[2:]).swapaxes(1, 2)
    side = 84 // 16
    px = f("x")[:, :, :side * 16, :side * 16].reshape(NB, 3, side, 16, side, 16).transpose(1, 3, 5, 0, 2, 4)
    patches = np.zeros((KP * KC, NB, SEQ), np.float32)
    patches[:, :, 1:] = px.reshape(KP * KC, NB, side * side)
    cells = 32
    edges = np.arange(1.0 / cells, 1.0, 1.0 / cells, dtype=np.float32)
    frac = np.arange(0.0, 1.0 - 1e-06, 1.0 / side, dtype=np.float32)
    at = np.searchsorted(edges, frac, side="right")
    pos = f("L0_tok_pos_table")[(at[:, None] * cells + at).reshape(-1)]
    posb = np.tile(np.concatenate([f("cls_tok").reshape(1, D), pos]), (TT // SEQ, 1))
    cbias = np.zeros((TT // SEQ, SEQ, D), np.float32)
    cbias[:, 1:] = f("L0_tok_conv_b")
    xp = f("L0_attn_x_proj_w").swapaxes(1, 2)
    wxp = np.zeros((NL, I, XR), np.float32)
    wxp[:, :, :R] = xp[:, :, :R]
    wxp[:, :, BC0:] = xp[:, :, R:]
    chan = np.concatenate([f("L0_attn_conv_w").reshape(NL, I, K), f("L0_attn_conv_b")[:, :, None],
                           f("L0_attn_dt_proj_b")[:, :, None]], 2)
    ident = np.eye(128, dtype=np.float32)
    arrays = {
        "patches": patches.reshape(KC, KP, NTOK).swapaxes(0, 1),
        "wconv": f("L0_tok_conv_w").reshape(D, KC, KP).transpose(2, 1, 0),
        "posb": posb, "cbias": cbias.reshape(TT, D),
        "ident": ident, "id3": np.tile(np.eye(NBC, dtype=np.float32), (3, 1)),
        "win": rows(f("L0_attn_in_proj_w").swapaxes(1, 2), DP),
        "nw": rows(f("L0_attn_norm_w"), DP), "chan": rows(chan, 128), "wxp": rows(wxp, 128),
        "wdt": f("L0_attn_dt_proj_w").swapaxes(1, 2), "wout": rows(f("L0_attn_out_proj_w").swapaxes(1, 2), 128),
        "dskip": rows(f("L0_attn_D"), 128),
        "alog": rows(f("L0_attn_A_log"), 128).reshape(NL, 128, IC * NS),
        "fnw": np.tile(f("L0_attn_final_norm_w"), (TT, 1)),
        "gw": f("L0_ffn_gate_w").T.reshape(DC, DP, E).swapaxes(0, 1),
        "enw": f("L0_ffn_norm_w").T.reshape(DC, DP, E).swapaxes(0, 1),
        "w13": rows(f("L0_ffn_w13").swapaxes(1, 2), DP), "wd": rows(f("L0_ffn_w2").swapaxes(1, 2), 128),
        "tri": np.triu(np.ones((TT, TT), np.float32), 1), "ones": np.ones((TT, TT), np.float32),
        "rank": np.tile(np.arange(E, 0, -1, dtype=np.float32), (TT, NT, 1)),
    }
    nc = bacc.Bacc("TRN2", target_bir_lowering=False, num_devices=1)
    maps, a = {}, {}
    for name, v in arrays.items():
        maps[f"in_{name}"] = np.ascontiguousarray(v)
        a[name] = nc.dram_tensor(f"in_{name}", v.shape, fp32, kind="ExternalInput").ap()
    out = nc.dram_tensor("out_0", (NB, SEQ, D), fp32, kind="ExternalOutput").ap()
    build(nc, a, out)
    r = run_bass_kernel_spmd(nc, [maps], core_ids=[0])
    return r.results[0]["out_0"]
```

```python
import concourse.bass as bass
from concourse import mybir
from contextlib import ExitStack

NB, SEQ, D = 32, 26, 192
NTOK = NB * SEQ
TT = 104
NT = NTOK // TT
HB = NB // 2
HT = HB * SEQ
HNT = HT // TT
KP, KC = 128, 6
DC, DP = 2, 96
NL, I, NS, R, K = 16, 384, 16, 48, 4
IC = I // 128
XR = 96
BC0, NBC = 64, 2 * NS
UNITS = NS * IC
TPAD = K - 1 + SEQ
E, FF, CAP = 8, 512, 260
FC = FF // 128
SLOTS = E * CAP
QT = 3

LN_SLACK = 1.3e-7
R_DBU, R_H, R_HC = 4, 2, 2
R_DA = 2
NQ, QS = 4, NS // 4

J_TR, J_U, J_CONV, J_XP, J_DT, J_Z, NPRE = 0, 2, 5, 8, 9, 12, 15
O_Y, O_OUT, NPOST = 0, 3, 5
NSH = NPRE + NPOST

WHEN = dict(
    act_sums=(4, 4, 5), act_spread_late=(1,), act_diagonal=(19, 20, 20, 21, 21, 22), act_rms=(12,),
    act_ddiag=(17,), act_hT=(14, 15), act_upad=(15, 17, 23), act_conv=(25, 27, 29), act_usig=(25, 28, 29),
    act_bc=(31,), act_spread=(36, 36, 40), act_dtx=(35, 35, 38), act_dexp=(38, 39, 39),
    act_z=(40, 40, 41), act_zsig=(42, 43, 44),
    dve_y=(4, 5, 5), dve_resid=(8, 9), dve_uclamp=(24, 27, 27), dve_bc=(31,),
    dve_parts=(35,), dve_dclamp=(36, 36, 38), dve_dt=(38, 38, 41), dve_zclamp=(40, 40, 40),
    pe_sums=(0, 1, 2), pe_out=(5, 6), pe_hT=(12, 12), pe_u=(12, 13, 17), pe_conv=(22, 23, 24),
    pe_xp=(27,), pe_dt=(31, 31, 32), pe_z=(36, 39, 40),
    dve_times_c=(1,), pe_broadcast=(2,), pe_reduce=(2,),
    pool_u=(34, 34, 34), pool_poly=(39, 40, 43), pool_dtu=(45, 45, 47), pool_z=(45, 47, 47))


def turns(name, v):
    return [i for i, at in enumerate(WHEN[name]) if at == v]


fp32 = mybir.dt.float32
bf16 = mybir.dt.bfloat16
int32 = mybir.dt.int32
ALU = mybir.AluOpType
ACT = mybir.ActivationFunctionType
AX = mybir.AxisListType


def embed_program(nc, a, h0, xres, eps5):
    with ExitStack() as ctx:
        def sb(name, shape, dt=fp32):
            return ctx.enter_context(nc.sbuf_tensor(name, shape, dt))

        def sem(name):
            return ctx.enter_context(nc.semaphore(name))

        patches = sb("patches", [KP, KC, NTOK])
        wconv = sb("wconv", [KP, KC, D])
        posb = sb("posb", [TT, D])
        cbias = sb("cbias", [TT, D])
        stats = sb("stats", [TT, NT, 6])
        mv = sb("mv", [TT, NT, 2])
        rstd = sb("rstd", [TT, NT])
        ps = [ctx.enter_context(nc.psum_tensor(f"pe{i}", [128, 512], fp32)) for i in range(2)]
        patch_in = [sem(f"patch_in{i}") for i in range(KC)]
        w_in, b_in = sem("w_in"), sem("b_in")
        clear = sb("clear", [TT, SLOTS // TT * D])
        clear_set, cleared = sem("clear_set"), sem("cleared")
        eps_set = sem("eps_set")
        bias_ready, emb_ready, emb_taken = sem("bias_ready"), sem("emb_ready"), sem("emb_taken")
        stat_ready, mv_ready, ln_ready, rstd_ready, x_ready = (
            sem("stat_ready"), sem("mv_ready"), sem("ln_ready"), sem("rstd_ready"), sem("x_ready"))

        with nc.Block() as block:
            @block.sync
            def _(sp):
                sp.dma_start(wconv[:], a["wconv"]).then_inc(w_in, 16)
                for c in range(KC):
                    sp.dma_start(patches[:, c, :], a["patches"][:, c, :]).then_inc(patch_in[c], 16)
                sp.dma_start(posb[:], a["posb"]).then_inc(b_in, 16)
                sp.dma_start(cbias[:], a["cbias"]).then_inc(b_in, 16)
                sp.wait_ge(clear_set, 1)
                sp.dma_start(a["queues"][:SLOTS].rearrange("(q r) d -> q (r d)", q=TT), clear[:]
                             ).then_inc(cleared, 16)
                sp.wait_ge(cleared, 16)

            @block.gpsimd
            def _(pool):
                nc.gpsimd.memset(clear[:], 0.0).then_inc(clear_set, 1)

            @block.tensor
            def _(pe):
                pe.wait_ge(w_in, 16)
                for c in range(KC):
                    pe.wait_ge(patch_in[c], 16)
                for j in range(NT):
                    if j >= 2:
                        pe.wait_ge(emb_taken, j - 1)
                    for c in range(KC):
                        mm = nc.tensor.matmul(ps[j % 2][:TT, :D], patches[:, c, j * TT:(j + 1) * TT],
                                              wconv[:, c, :], start=(c == 0), stop=(c == KC - 1))
                    mm.then_inc(emb_ready, 1)

            @block.vector
            def _(dve):
                nc.vector.memset(eps5[:], 1e-5).then_inc(eps_set, 1)
                dve.wait_ge(b_in, 32)
                nc.vector.tensor_tensor(posb[:], posb[:], cbias[:], ALU.add).then_inc(bias_ready, 1)
                dve.wait_ge(bias_ready, 1)
                for j in range(NT):
                    dve.wait_ge(emb_ready, j + 1)
                    nc.vector.tensor_tensor(h0[:, j, :], ps[j % 2][:TT, :D], posb[:], ALU.add
                                            ).then_inc(emb_taken, 1)
                    dve.wait_ge(emb_taken, j + 1)
                    nc.vector.bn_stats(stats[:, j, :], h0[:, j, :]).then_inc(stat_ready, 1)
                    dve.wait_ge(stat_ready, j + 1)
                    nc.vector.bn_aggr(mv[:, j, :], stats[:, j, :]).then_inc(mv_ready, 1)
                dve.wait_ge(rstd_ready, 1)
                for j in range(NT):
                    nc.vector.tensor_scalar(xres[:, j, :], h0[:, j, :], mv[:, j, 0:1], rstd[:, j:j + 1],
                                            ALU.subtract, ALU.mult).then_inc(x_ready, 1)

            @block.scalar
            def _(act):
                nc.scalar.preload_act_table_set("natural_log_exp_and_others")
                act.wait_ge(eps_set, 1)
                act.wait_ge(mv_ready, NT)
                nc.scalar.activation(rstd[:], mv[:, :, 1], ACT.Ln, bias=eps5[:TT, 0:1]).then_inc(ln_ready, 1)
                act.wait_ge(ln_ready, 1)
                nc.scalar.activation(rstd[:], rstd[:], ACT.Exp, scale=-0.5).then_inc(rstd_ready, 1)


def mamba_program(nc, a, xres, eps5, ident):
    with ExitStack() as ctx:
        def sb(name, shape, dt=fp32):
            return ctx.enter_context(nc.sbuf_tensor(name, shape, dt))

        def sem(name):
            return ctx.enter_context(nc.semaphore(name))

        win = sb("win", [DP, DC, 2 * I])
        nw = sb("nw", [DP, DC])
        chan = sb("chan", [128, IC, K + 2])
        cdiag = sb("cdiag", [128, IC, K, 128])
        wxp = sb("wxp", [128, IC, XR])
        wdt = sb("wdt", [R, I])
        wout = sb("wout", [128, IC, D])
        dskip = sb("dskip", [128, IC])
        ddiag = sb("ddiag", [128, IC, 128])
        alog = sb("alog", [128, IC * NS])
        nega = sb("nega", [128, IC * NS])
        id3 = sb("id3", [XR, NBC])
        sel = sb("sel", [XR, NS, 128], bf16)
        one, third = sb("one", [128, 1]), sb("third", [128, 1])
        sq = sb("sq", [TT, D])
        ssq = sb("ssq", [TT, HNT])
        rrms = sb("rrms", [TT, HNT])
        xn = sb("xn", [TT, HNT, D])
        hT = sb("hT", [DP, DC, HT])
        upad = sb("upad", [128, IC, HB, TPAD])
        uc = sb("uc", [128, IC, HT])
        zraw = sb("zraw", [128, IC, HT])
        gA = sb("gA", [128, IC, HT])
        gB = sb("gB", [128, IC, HT])
        gC = sb("gC", [128, IC, HT])
        gZ = sb("gZ", [128, IC, HT])
        dtr = sb("dtr", [R, HT])
        brow = sb("brow", [NS, HT])
        resid = sb("resid", [XR, HT])
        u = [sb(f"u{h}", [128, IC, HT]) for h in range(2)]
        zs = [sb(f"zs{h}", [128, IC, HT]) for h in range(2)]
        dt = [sb(f"dt{h}", [128, IC, HT]) for h in range(2)]
        dtu = [sb(f"dtu{h}", [128, IC, HT]) for h in range(2)]
        parts = [sb(f"parts{h}", [XR, HT], bf16) for h in range(2)]
        sums = sb("sums", [TT, IC, HNT * 128])
        y = sb("y", [128, IC, HT])
        ball = sb("ball", [128, NS, HT])
        dbu = sb("dbu", [128, R_DBU, IC, HT])
        hst = sb("hst", [128, R_H, IC, HT])
        hc = sb("hc", [128, R_HC, IC, HT])

        pb = [ctx.enter_context(nc.psum_tensor(f"pm{i}", [128, 512], fp32)) for i in range(8)]
        yacc = pb[0:3]
        cbank = pb[3]
        dab = pb[4:6]
        shared = pb[6:8]

        zeroed = sem("zeroed")
        pre_in, post_in, alog_in, id3_in = sem("pre_in"), sem("post_in"), sem("alog_in"), sem("id3_in")
        sel_ready, nega_exp, nega_ready = sem("sel_ready"), sem("nega_exp"), sem("nega_ready")
        diag_ready, ddiag_ready = sem("diag_ready"), sem("ddiag_ready")
        sh_full, sh_free = sem("sh_full"), [sem("sh_free0"), sem("sh_free1")]
        exp_done, m1_done, scan_done, c_ready, m2_done, reduce_done = (
            sem("exp_done"), sem("m1_done"), sem("scan_done"), sem("c_ready"), sem("m2_done"),
            sem("reduce_done"))
        sums_copied = sem("sums_copied")
        sq_done, rms_ln, rms_ready, xn_ready = sem("sq_done"), sem("rms_ln"), sem("rms_ready"), sem("xn_ready")
        uclamp, uexp, uln, usig, u_ready = sem("uclamp"), sem("uexp"), sem("uln"), sem("usig"), sem("u_ready")
        zclamp, zexp, zln, zsig, z_ready = sem("zclamp"), sem("zexp"), sem("zln"), sem("zsig"), sem("z_ready")
        bc_hi, bc_mid, parts_ready = sem("bc_hi"), sem("bc_mid"), sem("parts_ready")
        b_saved = sem("b_saved")
        b_in = [sem(f"b_in{q}") for q in range(NQ)]
        dclamp, dexp, dln, dpoly = sem("dclamp"), sem("dexp"), sem("dln"), sem("dpoly")
        dpoly4, dpoly3 = sem("dpoly4"), sem("dpoly3")
        dt_ready, dtu_ready = sem("dt_ready"), sem("dtu_ready")

        CREDIT = R_DBU * IC

        def first_of(x):
            return isinstance(x, int) and x == 0

        def pre_tile(p, j):
            if first_of(p):
                return j % 2, j // 2, j
            return (j - NPOST) % 2, p * (NSH // 2) + (j - NPOST) // 2, p * NSH + (j - NPOST)

        def post_tile(k, i):
            i = i - NPOST + (0 if isinstance(k, int) and k == 2 * NL else NPRE)
            return i % 2, k * (NSH // 2) + i // 2, k * NSH + i

        def wait_full(engine, tile):
            engine.wait_ge(sh_full, tile[2] + 1)

        def wait_taken(engine, tile):
            engine.wait_ge(sh_free[tile[0]], tile[1] + 1)

        with nc.Block() as block:
            @block.sync
            def _(sp):
                def load_pre(l):
                    for dst, src in ((win, "win"), (nw, "nw"), (chan, "chan"), (wxp, "wxp"), (wdt, "wdt")):
                        s = a[src]
                        sp.dma_start(dst[:], s[bass.ds(l, 1)].rearrange(
                            "o p a b -> p (o a) b" if len(s.shape) == 4 else "o p a -> p (o a)")
                        ).then_inc(pre_in, 16)

                def load_post(l):
                    sp.dma_start(wout[:], a["wout"][bass.ds(l, 1)].rearrange("o p a b -> p (o a) b")
                                 ).then_inc(post_in, 16)
                    sp.dma_start(dskip[:], a["dskip"][bass.ds(l, 1)].rearrange("o p a -> p (o a)")
                                 ).then_inc(post_in, 16)

                def load_alog(l):
                    sp.dma_start(alog[:], a["alog"][bass.ds(l, 1)].rearrange("o p a -> p (o a)")
                                 ).then_inc(alog_in, 16)

                def layer(l, first, last):
                    if not first:
                        sp.wait_ge(sh_full, post_tile(2 * l, O_OUT + 1)[2] + 1)
                        load_post(l)
                    if not last:
                        sp.wait_ge(nega_ready, l + 1)
                        load_alog(l + 1)
                    if not last:
                        wait_taken(sp, pre_tile(l * 2 + 1, J_Z + IC - 1))
                        load_pre(l + 1)

                sp.dma_start(id3[:], a["id3"]).then_inc(id3_in, 16)
                load_pre(0)
                load_alog(0)
                load_post(0)
                layer(0, True, False)
                with sp.Fori(1, NL - 1) as l:
                    layer(l, False, False)
                layer(NL - 1, False, True)

            @block.gpsimd
            def _(pool):
                def pre(p, slot, o):
                    for i in turns("pool_u", slot):
                        pool.wait_ge(usig, p * IC + i + 1)
                        nc.gpsimd.tensor_tensor(u[o][:, i, :], uc[:, i, :], gA[:, i, :], ALU.mult
                                                ).then_inc(u_ready, 1)
                    for i in turns("pool_poly", slot):
                        pool.wait_ge(dpoly4, p * IC + i + 1)
                        nc.gpsimd.tensor_tensor(gC[:, i, :], gC[:, i, :], gA[:, i, :], ALU.mult
                                                ).then_inc(dpoly3, 1)
                    for i in turns("pool_dtu", slot):
                        pool.wait_ge(dt_ready, p * IC + i + 1)
                        nc.gpsimd.tensor_tensor(dtu[o][:, i, :], dt[o][:, i, :], u[o][:, i, :], ALU.mult
                                                ).then_inc(dtu_ready, 1)
                    for i in turns("pool_z", slot):
                        pool.wait_ge(zsig, p * IC + i + 1)
                        nc.gpsimd.tensor_tensor(zs[o][:, i, :], zraw[:, i, :], gZ[:, i, :], ALU.mult
                                                ).then_inc(z_ready, 1)

                def times_b(k, h, n):
                    if n == 0:
                        pool.wait_ge(dtu_ready, k * IC + IC)
                    if n % QS == 0:
                        pool.wait_ge(b_in[n // QS], k * 16 + 16)
                    pool.wait_ge(scan_done, k * UNITS + (n + 1) * IC)
                    nc.gpsimd.tensor_tensor(
                        dbu[:, n % R_DBU, :, :], dtu[h][:],
                        ball[:, n, :].rearrange("q (o t) -> q o t", o=1).to_broadcast([128, IC, HT]),
                        ALU.mult).then_inc(m1_done, 1)

                def step(l, h, first, last):
                    k = l * 2 + h
                    for v in range(UNITS):
                        n, i = divmod(v, IC)
                        if i == 0:
                            times_b(k, h, n)
                        if not last:
                            pre(k + 1, v, 1 - h)

                nc.gpsimd.memset(upad[:], 0.0).then_inc(zeroed, 1)
                for slot in range(UNITS):
                    pre(0, slot, 0)
                for h in range(2):
                    step(0, h, h == 0, False)
                with pool.Fori(1, NL - 1) as l:
                    for h in range(2):
                        step(l, h, False, False)
                for h in range(2):
                    step(NL - 1, h, False, h == 1)

            @block.scalar
            def _(act):
                def diagonal(i, t):
                    nc.scalar.activation(cdiag[:, i, t, :], ident[:], ACT.Copy,
                                         scale=chan[:, i, t:t + 1]).then_inc(diag_ready, 1)

                def take(tile, out, rows, func=ACT.Identity, **kw):
                    wait_full(act, tile)
                    src = shared[tile[0]][rows, :HT]
                    if len(out.shape) == 3:
                        src = src.rearrange("q (b t) -> q b t", t=SEQ)
                    return nc.scalar.activation(out, src, func, **kw)

                def sigmoid(x, i, p, clamped, exps, lns, done):
                    act.wait_ge(clamped, p * IC + i + 1)
                    nc.scalar.activation(x[:, i, :], x[:, i, :], ACT.Exp, scale=-1.0).then_inc(exps, 1)
                    act.wait_ge(exps, p * IC + i + 1)
                    nc.scalar.activation(x[:, i, :], x[:, i, :], ACT.Ln, bias=one[:, 0:1]).then_inc(lns, 1)
                    act.wait_ge(lns, p * IC + i + 1)
                    nc.scalar.activation(x[:, i, :], x[:, i, :], ACT.Exp, scale=-1.0).then_inc(done, 1)

                def save_b(p):
                    if not first_of(p):
                        for q in range(NQ):
                            act.wait_ge(b_in[q], p * 16)
                    act.wait_ge(bc_hi, p * 3 + 2)
                    act.dma_start(a["brows"], brow[:]).then_inc(b_saved, 16)

                def spread_b(p, q):
                    if not first_of(p):
                        act.wait_ge(m1_done, p * NS + ((q + 1) * QS - NS))
                    act.wait_ge(b_saved, p * 16 + 16)
                    act.dma_start(ball[:, q * QS:(q + 1) * QS, :],
                                  a["brows"][q * QS:(q + 1) * QS, :].rearrange("(o n) t -> o n t", o=1)
                                  .to_broadcast([128, QS, HT])).then_inc(b_in[q], 16)

                def pre(p, slot, o):
                    for _ in turns("act_rms", slot):
                        for j in range(HNT):
                            nc.scalar.activation(sq[:], xres[:, o * HNT + j, :], ACT.Square,
                                                 accum_out=ssq[:, j:j + 1]).then_inc(sq_done, 1)
                            act.wait_ge(sq_done, p * HNT + j + 1)
                        nc.scalar.activation(rrms[:], ssq[:], ACT.Ln, bias=eps5[:TT, 0:1], scale=1.0 / D
                                             ).then_inc(rms_ln, 1)
                        act.wait_ge(rms_ln, p + 1)
                        nc.scalar.activation(rrms[:], rrms[:], ACT.Exp, scale=-0.5).then_inc(rms_ready, 1)
                        act.wait_ge(rms_ready, p + 1)
                        for j in range(HNT):
                            nc.scalar.activation(xn[:, j, :], xres[:, o * HNT + j, :], ACT.Copy,
                                                 scale=rrms[:, j:j + 1]).then_inc(xn_ready, 1)
                    for c in turns("act_hT", slot):
                        t = pre_tile(p, J_TR + c)
                        take(t, hT[:, c, :], slice(0, DP), scale=nw[:, c:c + 1]).then_inc(sh_free[t[0]], 1)
                    for i in turns("act_upad", slot):
                        t = pre_tile(p, J_U + i)
                        take(t, upad[:, i, :, K - 1:], slice(0, 128)).then_inc(sh_free[t[0]], 1)
                    for i in turns("act_conv", slot):
                        t = pre_tile(p, J_CONV + i)
                        take(t, uc[:, i, :], slice(0, 128), bias=chan[:, i, K:K + 1]).then_inc(sh_free[t[0]], 1)
                    for i in turns("act_usig", slot):
                        sigmoid(gA, i, p, uclamp, uexp, uln, usig)
                    for _ in turns("act_bc", slot):
                        t = pre_tile(p, J_XP)
                        take(t, dtr[:], slice(0, R)).then_inc(bc_hi, 1)
                        if not first_of(p):
                            act.wait_ge(b_saved, p * 16)
                        take(t, brow[:], slice(BC0, BC0 + NS)).then_inc(bc_hi, 1)
                        take(t, parts[o][0:NBC, :], slice(BC0, XR)).then_inc(bc_hi, 1)
                        save_b(p)
                    for q in turns("act_spread", slot):
                        spread_b(p, q)
                    for i in turns("act_dtx", slot):
                        t = pre_tile(p, J_DT + i)
                        take(t, uc[:, i, :], slice(0, 128), bias=chan[:, i, K + 1:K + 2]
                             ).then_inc(sh_free[t[0]], 1)
                    for i in turns("act_dexp", slot):
                        act.wait_ge(dclamp, p * IC + i + 1)
                        nc.scalar.activation(gA[:, i, :], gA[:, i, :], ACT.Exp).then_inc(dexp, 1)
                        act.wait_ge(dexp, p * IC + i + 1)
                        nc.scalar.activation(gC[:, i, :], gA[:, i, :], ACT.Identity, bias=third[:, 0:1],
                                             scale=-0.25).then_inc(dpoly4, 1)
                        nc.scalar.activation(gB[:, i, :], gA[:, i, :], ACT.Ln, bias=one[:, 0:1]).then_inc(dln, 1)
                    for i in turns("act_z", slot):
                        t = pre_tile(p, J_Z + i)
                        take(t, zraw[:, i, :], slice(0, 128)).then_inc(sh_free[t[0]], 1)
                    for i in turns("act_zsig", slot):
                        sigmoid(gZ, i, p, zclamp, zexp, zln, zsig)

                def copy_sums(k, i):
                    act.wait_ge(reduce_done, k * NS)
                    nc.scalar.copy(sums[:, i, :], yacc[i][:TT, :]).then_inc(sums_copied, 1)

                def step(l, h, first, last):
                    k = l * 2 + h
                    if h == 0:
                        act.wait_ge(alog_in, l * 16 + 16)
                        if not first:
                            act.wait_ge(exp_done, k * UNITS)
                        nc.scalar.activation(nega[:], alog[:], ACT.Exp).then_inc(nega_exp, 1)
                        act.wait_ge(nega_exp, l + 1)
                        nc.scalar.mul(nega[:], nega[:], -1.0).then_inc(nega_ready, 1)
                        act.wait_ge(nega_ready, l + 1)
                    for v in range(UNITS):
                        n, i = divmod(v, IC)
                        if n == 0:
                            act.wait_ge(dt_ready, k * IC + i + 1)
                        act.wait_ge(scan_done, k * UNITS + v - R_DA + 1 + CREDIT)
                        nc.scalar.activation(
                            dab[v % R_DA][:, :HT].rearrange("q (b t) -> q b t", t=SEQ)[:, :, 1:],
                            dt[h][:, i, :].rearrange("q (b t) -> q b t", t=SEQ)[:, :, 1:],
                            ACT.Exp, scale=nega[:, i * NS + n:i * NS + n + 1]).then_inc(exp_done, 1)
                        for i in turns("act_sums", v):
                            if not first:
                                copy_sums(k, i)
                        for _ in turns("act_ddiag", v):
                            if h == 0:
                                act.wait_ge(post_in, l * 32 + 32)
                                if not first:
                                    wait_full(act, post_tile(k, O_OUT))
                                for c in range(IC):
                                    nc.scalar.activation(ddiag[:, c, :], ident[:], ACT.Copy,
                                                         scale=dskip[:, c:c + 1]).then_inc(ddiag_ready, 1)
                        for _ in turns("act_spread_late", v):
                            spread_b(k, NQ - 1)
                        if not last:
                            for q in turns("act_diagonal", v):
                                if h == 0:
                                    break
                                if q == 0:
                                    act.wait_ge(pre_in, l * 80 + 160)
                                for t in range(2):
                                    diagonal(q // 2, (q % 2) * 2 + t)
                            if v == WHEN["act_rms"][0] and not first:
                                wait_taken(act, post_tile(k, O_OUT))
                                wait_taken(act, post_tile(k, O_OUT + 1))
                            pre(k + 1, v, 1 - h)

                act.wait_ge(zeroed, 5)
                act.wait_ge(pre_in, 80)
                for i in range(IC):
                    for t in range(K):
                        diagonal(i, t)
                for slot in range(UNITS):
                    pre(0, slot, 0)
                for h in range(2):
                    step(0, h, h == 0, False)
                with act.Fori(1, NL - 1) as l:
                    for h in range(2):
                        step(l, h, False, False)
                for h in range(2):
                    step(NL - 1, h, False, h == 1)
                for i in range(IC):
                    copy_sums(2 * NL, i)

            @block.vector
            def _(dve):
                def pre(p, slot, o):
                    for i in turns("dve_uclamp", slot):
                        wait_taken(dve, pre_tile(p, J_CONV + i))
                        nc.vector.tensor_scalar(gA[:, i, :], uc[:, i, :], -40.0, None, ALU.max
                                                ).then_inc(uclamp, 1)
                    for _ in turns("dve_bc", slot):
                        t = pre_tile(p, J_XP)
                        dve.wait_ge(bc_hi, p * 3 + 3)
                        nc.vector.tensor_tensor(resid[NBC:2 * NBC, :], shared[t[0]][BC0:XR, :HT],
                                                parts[o][0:NBC, :], ALU.subtract).then_inc(sh_free[t[0]], 1)
                    for _ in turns("dve_parts", slot):
                        wait_taken(dve, pre_tile(p, J_XP))
                        nc.vector.tensor_copy(parts[o][NBC:2 * NBC, :], resid[NBC:2 * NBC, :]).then_inc(bc_mid, 1)
                        dve.wait_ge(bc_mid, p + 1)
                        nc.vector.tensor_tensor(parts[o][2 * NBC:XR, :], resid[NBC:2 * NBC, :],
                                                parts[o][NBC:2 * NBC, :], ALU.subtract).then_inc(parts_ready, 1)
                    for i in turns("dve_dclamp", slot):
                        wait_taken(dve, pre_tile(p, J_DT + i))
                        nc.vector.tensor_scalar(gA[:, i, :], uc[:, i, :], 17.0, None, ALU.min
                                                ).then_inc(dclamp, 1)
                    for i in turns("dve_dt", slot):
                        dve.wait_ge(dpoly3, p * IC + i + 1)
                        nc.vector.scalar_tensor_tensor(gC[:, i, :], gC[:, i, :], -0.5, gA[:, i, :],
                                                       ALU.add, ALU.mult).then_inc(dpoly, 1)
                        dve.wait_ge(dpoly, (p * IC + i) * 3 + 1)
                        nc.vector.scalar_tensor_tensor(gC[:, i, :], gC[:, i, :], 1.0, gA[:, i, :],
                                                       ALU.add, ALU.mult).then_inc(dpoly, 1)
                        dve.wait_ge(dpoly, (p * IC + i) * 3 + 2)
                        dve.wait_ge(dln, p * IC + i + 1)
                        nc.vector.scalar_tensor_tensor(gC[:, i, :], gB[:, i, :], -LN_SLACK, gC[:, i, :],
                                                       ALU.add, ALU.max).then_inc(dpoly, 1)
                        dve.wait_ge(dpoly, (p * IC + i) * 3 + 3)
                        nc.vector.tensor_tensor(dt[o][:, i, :], gC[:, i, :], uc[:, i, :], ALU.max
                                                ).then_inc(dt_ready, 1)
                    for i in turns("dve_zclamp", slot):
                        wait_taken(dve, pre_tile(p, J_Z + i))
                        nc.vector.tensor_scalar(gZ[:, i, :], zraw[:, i, :], -40.0, None, ALU.max
                                                ).then_inc(zclamp, 1)

                def finish_y(k, o, i):
                    t = post_tile(k, O_Y + i)
                    if i == 0:
                        dve.wait_ge(z_ready, k * IC)
                    wait_full(dve, t)
                    nc.vector.tensor_tensor(y[:, i, :], shared[t[0]][:, :HT], zs[o][:, i, :], ALU.mult
                                            ).then_inc(sh_free[t[0]], 1)

                def add_residual(k, o, i):
                    t = post_tile(k, O_OUT + i)
                    wait_full(dve, t)
                    j = o * HNT + 2 * i
                    nc.vector.tensor_tensor(xres[:, j:j + 2, :], xres[:, j:j + 2, :],
                                            shared[t[0]][:TT, :2 * D].rearrange("q (a d) -> q a d", a=2),
                                            ALU.add).then_inc(sh_free[t[0]], 1)

                def times_c(k, n):
                    dve.wait_ge(scan_done, k * UNITS + (n + 1) * IC + CREDIT)
                    dve.wait_ge(c_ready, k * NS + n + 1)
                    if n >= R_HC or not first_of(k):
                        dve.wait_ge(reduce_done, k * NS + n - R_HC + 1)
                    nc.vector.tensor_tensor(
                        hc[:, n % R_HC, :, :], hst[:, n % R_H, :, :],
                        cbank[:, :HT].rearrange("q (o t) -> q o t", o=1).to_broadcast([128, IC, HT]),
                        ALU.mult).then_inc(m2_done, 1)

                def step(l, h, first, last):
                    k = l * 2 + h
                    for v in range(UNITS):
                        n, i = divmod(v, IC)
                        if i == 0:
                            dve.wait_ge(m1_done, k * NS + n + 1)
                            if n >= R_H or not first:
                                dve.wait_ge(m2_done, k * NS + n - R_H + 1)
                        dve.wait_ge(exp_done, k * UNITS + v + 1)
                        nc.vector.tensor_tensor_scan(hst[:, n % R_H, i, :], dab[v % R_DA][:, :HT],
                                                     dbu[:, n % R_DBU, i, :], 0.0, ALU.mult, ALU.add
                                                     ).then_inc(scan_done, 1)
                        if turns("dve_times_c", i) and n >= 1:
                            times_c(k, n - 1)
                        for c in turns("dve_y", v):
                            if not first:
                                finish_y(k, 1 - h, c)
                        for c in turns("dve_resid", v):
                            if not first:
                                add_residual(k, 1 - h, c)
                        if not last:
                            pre(k + 1, v, 1 - h)
                    times_c(k, NS - 1)

                nc.vector.memset(one[:], 1.0).then_inc(zeroed, 1)
                nc.vector.memset(third[:], 1.0 / 3.0).then_inc(zeroed, 1)
                for b in dab:
                    nc.vector.memset(b[:], 0.0).then_inc(zeroed, 1)
                for r in range(CREDIT):
                    nc.vector.memset(dbu[:, r // IC, r % IC, 0:1], 0.0).then_inc(scan_done, 1)
                dve.wait_ge(id3_in, 16)
                nc.vector.tensor_copy(sel[:], id3[:, NS:].rearrange("q (n o) -> q n o", o=1)
                                      .to_broadcast([XR, NS, 128])).then_inc(sel_ready, 1)
                dve.wait_ge(zeroed, 5)
                for slot in range(UNITS):
                    pre(0, slot, 0)
                for h in range(2):
                    step(0, h, h == 0, False)
                with dve.Fori(1, NL - 1) as l:
                    for h in range(2):
                        step(l, h, False, False)
                for h in range(2):
                    step(NL - 1, h, False, h == 1)
                for i in range(IC):
                    finish_y(2 * NL, 1, i)
                for i in range(2):
                    add_residual(2 * NL, 1, i)

            @block.tensor
            def _(pe):
                def open_shared(tile):
                    if not first_of(tile[1]):
                        pe.wait_ge(sh_free[tile[0]], tile[1])
                    return shared[tile[0]]

                def in_projection(tile, q):
                    bank = open_shared(tile)
                    for c in range(DC):
                        mm = nc.tensor.matmul(bank[:, :HT], win[:, c, q * 128:(q + 1) * 128], hT[:, c, :],
                                              start=(c == 0), stop=(c == DC - 1))
                    mm.then_inc(sh_full, 1)

                def pre(p, slot, o, diagonals):
                    for c in turns("pe_hT", slot):
                        bank = open_shared(pre_tile(p, J_TR + c))
                        pe.wait_ge(xn_ready, p * HNT + HNT)
                        for j in range(HNT):
                            mm = nc.tensor.transpose(bank[:DP, j * TT:(j + 1) * TT],
                                                     xn[:, j, c * DP:(c + 1) * DP], ident[:TT, :TT])
                        mm.then_inc(sh_full, 1)
                    for i in turns("pe_u", slot):
                        if i == 0:
                            wait_taken(pe, pre_tile(p, J_TR))
                            wait_taken(pe, pre_tile(p, J_TR + 1))
                        in_projection(pre_tile(p, J_U + i), i)
                    for i in turns("pe_conv", slot):
                        bank = open_shared(pre_tile(p, J_CONV + i))
                        wait_taken(pe, pre_tile(p, J_U + i))
                        if i == 0:
                            pe.wait_ge(diag_ready, diagonals)
                        for t in range(K):
                            mm = nc.tensor.matmul(bank[:, :HT], cdiag[:, i, t, :], upad[:, i, :, t:t + SEQ],
                                                  start=(t == 0), stop=(t == K - 1))
                        mm.then_inc(sh_full, 1)
                    for _ in turns("pe_xp", slot):
                        bank = open_shared(pre_tile(p, J_XP))
                        for i in range(IC):
                            pe.wait_ge(u_ready, p * IC + i + 1)
                            mm = nc.tensor.matmul(bank[:XR, :HT], wxp[:, i, :], u[o][:, i, :],
                                                  start=(i == 0), stop=(i == IC - 1))
                        mm.then_inc(sh_full, 1)
                    for i in turns("pe_dt", slot):
                        bank = open_shared(pre_tile(p, J_DT + i))
                        if i == 0:
                            pe.wait_ge(bc_hi, p * 3 + 1)
                        nc.tensor.matmul(bank[:, :HT], wdt[:, i * 128:(i + 1) * 128], dtr[:],
                                         start=True, stop=True).then_inc(sh_full, 1)
                    for i in turns("pe_z", slot):
                        in_projection(pre_tile(p, J_Z + i), IC + i)

                def broadcast_c(k, h, n):
                    if n == 0:
                        pe.wait_ge(parts_ready, k + 1)
                    if n >= 1 or not first_of(k):
                        pe.wait_ge(m2_done, k * NS + n)
                    nc.tensor.matmul(cbank[:, :HT], sel[:, n, :], parts[h][:], start=True, stop=True
                                     ).then_inc(c_ready, 1)

                def reduce(k, n):
                    pe.wait_ge(m2_done, k * NS + n + 1)
                    for i in range(IC):
                        if n == 0 and not first_of(k):
                            pe.wait_ge(sums_copied, (k - 1) * IC + i + 1)
                        for j in range(HNT):
                            mm = nc.tensor.matmul(yacc[i][:TT, j * 128:(j + 1) * 128],
                                                  hc[:, n % R_HC, i, j * TT:(j + 1) * TT], ident[:],
                                                  is_transpose=True, start=(n == 0 and j == 0),
                                                  stop=(n == NS - 1 and j == HNT - 1), skip_group_check=True)
                    mm.then_inc(reduce_done, 1)

                def sums_back(k, o, i, diagonals):
                    bank = open_shared(post_tile(k, O_Y + i))
                    pe.wait_ge(sums_copied, (k - 1) * IC + i + 1)
                    for j in range(HNT):
                        nc.tensor.matmul(bank[:, j * TT:(j + 1) * TT], sums[:, i, j * 128:(j + 1) * 128],
                                         ident[:TT, :TT], is_transpose=True, start=(j == 0), stop=False,
                                         skip_group_check=True)
                    if i == 0:
                        pe.wait_ge(ddiag_ready, diagonals)
                    mm = nc.tensor.matmul(bank[:, :HT], ddiag[:, i, :], u[o][:, i, :], start=False,
                                          stop=True, skip_group_check=True)
                    mm.then_inc(sh_full, 1)

                def out_projection(k, i):
                    bank = open_shared(post_tile(k, O_OUT + i))
                    if i == 0:
                        for c in range(IC):
                            wait_taken(pe, post_tile(k, O_Y + c))
                    for jj in range(2):
                        j = 2 * i + jj
                        for c in range(IC):
                            mm = nc.tensor.matmul(bank[:TT, jj * D:(jj + 1) * D], y[:, c, j * TT:(j + 1) * TT],
                                                  wout[:, c, :], start=(c == 0), stop=(c == IC - 1))
                    mm.then_inc(sh_full, 1)

                def step(l, h, first, last):
                    k = l * 2 + h
                    broadcast_c(k, h, 0)
                    for v in range(UNITS):
                        n, i = divmod(v, IC)
                        if turns("pe_broadcast", i) and n >= 1:
                            broadcast_c(k, h, n)
                        if turns("pe_reduce", i) and n >= 1:
                            reduce(k, n - 1)
                        for c in turns("pe_sums", v):
                            if not first:
                                sums_back(k, 1 - h, c, (l + h) * IC)
                        for c in turns("pe_out", v):
                            if not first:
                                out_projection(k, c)
                        if not last:
                            if h == 1 and v == WHEN["pe_u"][0]:
                                pe.wait_ge(pre_in, l * 80 + 160)
                            pre(k + 1, v, 1 - h, (l + 1 + h) * IC * K)
                    reduce(k, NS - 1)

                pe.wait_ge(zeroed, 5)
                pe.wait_ge(sel_ready, 1)
                pe.wait_ge(pre_in, 80)
                for slot in range(UNITS):
                    pre(0, slot, 0, IC * K)
                for h in range(2):
                    step(0, h, h == 0, False)
                with pe.Fori(1, NL - 1) as l:
                    for h in range(2):
                        step(l, h, False, False)
                for h in range(2):
                    step(NL - 1, h, False, h == 1)
                for i in range(IC):
                    sums_back(2 * NL, 1, i, NL * IC)
                for i in range(2):
                    out_projection(2 * NL, i)


def gating_program(nc, a, h0, xres, eps5, ident, xl, zt, put, get, weights):
    with ExitStack() as ctx:
        def sb(name, shape, dt=fp32):
            return ctx.enter_context(nc.sbuf_tensor(name, shape, dt))

        def sem(name):
            return ctx.enter_context(nc.semaphore(name))

        fnw = sb("fnw", [TT, D])
        gw = sb("gw", [DP, DC, E])
        trif, onesf = sb("trif", [TT, TT]), sb("onesf", [TT, TT])
        tri, ones = sb("tri", [TT, TT], bf16), sb("ones", [TT, TT], bf16)
        rank = sb("rank", [TT, NT, E])
        eps6 = sb("eps6", [128, 1])
        sq, sq2 = sb("sqe", [TT, NT, D]), sb("sqf", [TT, NT, D])
        ssq, ssq2 = sb("ssqe", [TT, NT]), sb("ssqf", [TT, NT])
        rrms, rstd, rrms2 = sb("rrmse", [TT, NT]), sb("rstde", [TT, NT]), sb("rrmsf", [TT, NT])
        stats, mv = sb("statse", [TT, NT, 6]), sb("mve", [TT, NT, 2])
        xT = sb("xT", [DP, DC, NTOK])
        lg, lg2 = sb("lg", [TT, NT, E]), sb("lg2", [TT, NT, E])
        mask1, mask2 = sb("mask1", [TT, NT, E]), sb("mask2", [TT, NT, E])
        both = sb("both", [TT, NT, E], bf16)
        top1, top2, idx = sb("top1", [TT, NT]), sb("top2", [TT, NT]), sb("idx", [TT, NT])
        w1, w2 = sb("w1", [TT, NT]), sb("w2", [TT, NT])
        keep = sb("keep", [TT, NT, E])
        row = sb("row", [TT, NT, E])
        first_row = sb("first_row", [TT, NT, E])
        behind = sb("behind", [TT, 2, NT])
        pick_keep, pick_row = sb("pick_keep", [TT, NT, E]), sb("pick_row", [TT, NT, E])
        kept, got, moved = sb("kept", [TT, NT]), sb("got", [TT, NT]), sb("moved", [TT, NT])
        pb = [ctx.enter_context(nc.psum_tensor(f"pg{i}", [128, 512], fp32)) for i in range(6)]
        plogit, pplace = pb[4], pb[5]

        const_in, own = sem("const_in"), sem("vector_chain")
        eps_set, sq_done, ln1, rms_ready, mv_ready, ln2, std_ready, xl_ready = (
            sem("eps_set"), sem("sqe_done"), sem("ln1"), sem("rmse_ready"), sem("mve_ready"), sem("ln2"),
            sem("std_ready"), sem("xl_ready"))
        sq2_done, ln3, rms2_ready, zt_ready = sem("sqf_done"), sem("ln3"), sem("rmsf_ready"), sem("zt_ready")
        xt_full, xt_copied = sem("xt_full"), sem("xt_copied")
        logits_full, logits_ready, gap_ready, gap_exp, both_ready, places_full, tri_ready = (
            sem("logits_full"), sem("logits_ready"), sem("gap_ready"), sem("gap_exp"), sem("both_ready"),
            sem("places_full"), sem("tri_ready"))

        with nc.Block() as block:
            @block.sync
            def _(sp):
                for dst, src in ((fnw, "fnw"), (gw, "gw"), (trif, "tri"), (onesf, "ones"), (rank, "rank"),
                                 (first_row, "first_row"), (behind, "behind")):
                    sp.dma_start(dst[:], a[src]).then_inc(const_in, 16)

            @block.scalar
            def _(act):
                for j in range(NT):
                    nc.scalar.activation(sq[:, j, :], xres[:, j, :], ACT.Square, accum_out=ssq[:, j:j + 1]
                                         ).then_inc(sq_done, 1)
                act.wait_ge(sq_done, NT)
                nc.scalar.activation(rrms[:], ssq[:], ACT.Ln, bias=eps5[:TT, 0:1], scale=1.0 / D).then_inc(ln1, 1)
                act.wait_ge(ln1, 1)
                nc.scalar.activation(rrms[:], rrms[:], ACT.Exp, scale=-0.5).then_inc(rms_ready, 1)
                act.wait_ge(mv_ready, NT)
                nc.scalar.activation(rstd[:], mv[:, :, 1], ACT.Ln, bias=eps5[:TT, 0:1]).then_inc(ln2, 1)
                act.wait_ge(ln2, 1)
                nc.scalar.activation(rstd[:], rstd[:], ACT.Exp, scale=-0.5).then_inc(std_ready, 1)
                for j in range(NT):
                    act.wait_ge(xl_ready, j + 1)
                    nc.scalar.activation(sq2[:, j, :], xl[:, j, :], ACT.Square, accum_out=ssq2[:, j:j + 1]
                                         ).then_inc(sq2_done, 1)
                act.wait_ge(sq2_done, NT)
                act.wait_ge(eps_set, 1)
                nc.scalar.activation(rrms2[:], ssq2[:], ACT.Ln, bias=eps6[:TT, 0:1], scale=4.0 / D).then_inc(ln3, 1)
                act.wait_ge(ln3, 1)
                nc.scalar.activation(rrms2[:], rrms2[:], ACT.Exp, scale=-0.5).then_inc(rms2_ready, 1)
                for b in range(2 * DC):
                    c, hf = divmod(b, 2)
                    act.wait_ge(xt_full, b + 1)
                    nc.scalar.copy(xT[:, c, hf * HT:(hf + 1) * HT], pb[b][:DP, :HT]).then_inc(xt_copied, 1)
                act.wait_ge(logits_full, 1)
                nc.scalar.copy(lg[:].rearrange("q j e -> q (j e)"), plogit[:TT, :NT * E]).then_inc(logits_ready, 1)
                act.wait_ge(gap_ready, 1)
                nc.scalar.activation(w2[:], w2[:], ACT.Exp).then_inc(gap_exp, 1)

            @block.tensor
            def _(pe):
                for b in range(2 * DC):
                    c, hf = divmod(b, 2)
                    pe.wait_ge(xl_ready, hf * HNT + HNT)
                    for jj in range(HNT):
                        mm = nc.tensor.transpose(pb[b][:DP, jj * TT:(jj + 1) * TT],
                                                 xl[:, hf * HNT + jj, c * DP:(c + 1) * DP], ident[:TT, :TT])
                    mm.then_inc(xt_full, 1)
                pe.wait_ge(const_in, 112)
                pe.wait_ge(xt_copied, 2 * DC)
                for j in range(NT):
                    for c in range(DC):
                        mm = nc.tensor.matmul(plogit[:TT, j * E:(j + 1) * E], xT[:, c, j * TT:(j + 1) * TT],
                                              gw[:, c, :], start=(c == 0), stop=(c == DC - 1))
                mm.then_inc(logits_full, 1)
                pe.wait_ge(tri_ready, 2)
                pe.wait_ge(both_ready, 1)
                for j in range(NT):
                    for jj in range(j):
                        nc.tensor.matmul(pplace[:TT, j * E:(j + 1) * E], ones[:], both[:, jj, :],
                                         start=(jj == 0), stop=False)
                    mm = nc.tensor.matmul(pplace[:TT, j * E:(j + 1) * E], tri[:], both[:, j, :],
                                          start=(j == 0), stop=True)
                mm.then_inc(places_full, 1)

            @block.vector
            def _(dve):
                n = [0]

                def link(ins):
                    n[0] += 1
                    ins.then_inc(own, 1)
                    dve.wait_ge(own, n[0])

                vec = nc.vector
                vec.memset(eps6[:], 1e-6).then_inc(eps_set, 1)
                dve.wait_ge(const_in, 112)
                vec.tensor_copy(tri[:], trif[:]).then_inc(tri_ready, 1)
                vec.tensor_copy(ones[:], onesf[:]).then_inc(tri_ready, 1)
                dve.wait_ge(rms_ready, 1)
                for j in range(NT):
                    link(vec.scalar_tensor_tensor(xl[:, j, :], xres[:, j, :], rrms[:, j:j + 1], fnw[:],
                                                  ALU.mult, ALU.mult))
                    link(vec.tensor_tensor(h0[:, j, :], h0[:, j, :], xl[:, j, :], ALU.add))
                    link(vec.bn_stats(stats[:, j, :], h0[:, j, :]))
                    vec.bn_aggr(mv[:, j, :], stats[:, j, :]).then_inc(mv_ready, 1)
                dve.wait_ge(std_ready, 1)
                for j in range(NT):
                    vec.tensor_scalar(xl[:, j, :], h0[:, j, :], mv[:, j, 0:1], rstd[:, j:j + 1],
                                      ALU.subtract, ALU.mult).then_inc(xl_ready, 1)
                dve.wait_ge(rms2_ready, 1)
                for j in range(NT):
                    vec.tensor_scalar(zt[:, j, :], xl[:, j, :], rrms2[:, j:j + 1], 2.0, ALU.mult, ALU.mult
                                      ).then_inc(zt_ready, 1)

                def spread(t):
                    return t[:].rearrange("q (j o) -> q j o", o=1).to_broadcast([TT, NT, E])

                def pick(logits, top, mask):
                    link(vec.tensor_reduce(top[:], logits[:], AX.X, ALU.max))
                    link(vec.tensor_tensor(mask[:], logits[:], spread(top), ALU.is_equal))
                    link(vec.tensor_tensor(mask[:], mask[:], rank[:], ALU.mult))
                    link(vec.tensor_reduce(idx[:], mask[:], AX.X, ALU.max))
                    link(vec.tensor_tensor(mask[:], rank[:], spread(idx), ALU.is_equal))

                dve.wait_ge(logits_ready, 1)
                pick(lg, top1, mask1)
                link(vec.tensor_scalar(lg2[:], mask1[:], -3.0e38, None, ALU.mult))
                link(vec.tensor_tensor(lg2[:], lg2[:], lg[:], ALU.add))
                pick(lg2, top2, mask2)
                vec.tensor_tensor(both[:], mask1[:], mask2[:], ALU.add).then_inc(both_ready, 1)
                vec.tensor_tensor(w2[:], top2[:], top1[:], ALU.subtract).then_inc(gap_ready, 1)
                dve.wait_ge(gap_exp, 1)
                link(vec.tensor_scalar(w1[:], w2[:], 1.0, None, ALU.add))
                link(vec.reciprocal(w1[:], w1[:]))
                link(vec.tensor_tensor(w2[:], w2[:], w1[:], ALU.mult))
                dve.wait_ge(places_full, 1)
                place = pplace[:TT, :NT * E].rearrange("q (j e) -> q j e", e=E)
                link(vec.tensor_scalar(keep[:], place, float(CAP), None, ALU.is_lt))
                link(vec.tensor_scalar(row[:], place, float(CAP - 1), None, ALU.min))
                link(vec.tensor_tensor(row[:], row[:], first_row[:], ALU.add))
                for i, (mask, w) in enumerate(((mask1, w1), (mask2, w2))):
                    link(vec.tensor_tensor(pick_keep[:], mask[:], keep[:], ALU.mult))
                    link(vec.tensor_reduce(kept[:], pick_keep[:], AX.X, ALU.add))
                    link(vec.tensor_tensor(pick_row[:], mask[:], row[:], ALU.mult))
                    link(vec.tensor_reduce(got[:], pick_row[:], AX.X, ALU.add))
                    link(vec.tensor_copy(get[:, i, :], got[:]))
                    link(vec.tensor_tensor(moved[:], got[:], behind[:, i, :], ALU.subtract))
                    link(vec.tensor_tensor(moved[:], moved[:], kept[:], ALU.mult))
                    link(vec.tensor_tensor(moved[:], moved[:], behind[:, i, :], ALU.add))
                    link(vec.tensor_copy(put[:, i, :], moved[:]))
                    link(vec.tensor_tensor(weights[:, i, :], w[:], kept[:], ALU.mult))
                link(vec.tensor_tensor(weights[:, 2, :], weights[:, 0, :], weights[:, 1, :], ALU.add))


def expert_program(nc, a, h0, xl, ident, zt, put, get, weights, out):
    with ExitStack() as ctx:
        def sb(name, shape, dt=fp32):
            return ctx.enter_context(nc.sbuf_tensor(name, shape, dt))

        def sem(name):
            return ctx.enter_context(nc.semaphore(name))

        enw = sb("enw", [DP, DC, E])
        acc = sb("acc", [TT, NT, D])
        back = sb("back", [TT, 2, NT, D])
        w13 = [sb(f"w13_{b}", [DP, DC, 2 * FF]) for b in range(2)]
        wd = [sb(f"wd_{b}", [128, FC, D]) for b in range(2)]
        zin = [sb(f"zin{b}", [TT, QT, D]) for b in range(2)]
        ze = [sb(f"ze{b}", [DP, DC, CAP]) for b in range(2)]
        hid = [sb(f"hid{b}", [128, FC, CAP]) for b in range(2)]
        ys = [sb(f"ys{b}", [TT, QT, D]) for b in range(2)]
        sg = [sb(f"sg{b}", [128, CAP]) for b in range(2)]
        pb = [ctx.enter_context(nc.psum_tensor(f"px{i}", [128, 512], fp32)) for i in range(8)]
        tbank, gbank, ubank, ybank = pb[0:2], pb[2:4], pb[4:6], pb[6:8]
        enw_in, w_in, z_in, y_out = (sem("enw_in"), [sem(f"we_in{b}") for b in range(2)],
                                     [sem(f"ze_in{b}") for b in range(2)], [sem(f"ye_out{b}") for b in range(2)])
        scattered, back_in = sem("scattered"), [sem(f"back_in{j}") for j in range(NT)]
        t_full, ze_ready, gu_ready, silu_ready, hid_ready, y_ready, ys_ready, base_ready, acc_ready, out_done = (
            sem("t_full"), sem("ze_ready"), sem("gu_ready"), sem("silu_ready"), sem("hid_ready"),
            sem("ye_ready"), sem("ys_ready"), sem("base_ready"), sem("acc_ready"), sem("out_done"))

        def queue_rows(j):
            return min(TT, CAP - j * TT)

        with nc.Block() as block:
            @block.sync
            def _(sp):
                def load_weights(e, b):
                    sp.dma_start(w13[b][:], a["w13"][bass.ds(e, 1)].rearrange("o p a b -> p (o a) b")
                                 ).then_inc(w_in[b], 16)
                    sp.dma_start(wd[b][:], a["wd"][bass.ds(e, 1)].rearrange("o p a b -> p (o a) b")
                                 ).then_inc(w_in[b], 16)

                def load_queue(e, b):
                    sp.dma_start(zin[b][:, :QT - 1, :],
                                 a["queues"][bass.ds(e * CAP, (QT - 1) * TT), :]
                                 .rearrange("(j q) d -> q j d", q=TT)).then_inc(z_in[b], 16)
                    sp.dma_start(zin[b][:queue_rows(QT - 1), QT - 1, :],
                                 a["queues"][bass.ds(e * CAP + (QT - 1) * TT, queue_rows(QT - 1)), :]
                                 ).then_inc(z_in[b], 16)

                def store_results(e, b):
                    sp.dma_start(a["results"][bass.ds(e * CAP, (QT - 1) * TT), :]
                                 .rearrange("(j q) d -> q j d", q=TT), ys[b][:, :QT - 1, :]
                                 ).then_inc(y_out[b], 16)
                    sp.dma_start(a["results"][bass.ds(e * CAP + (QT - 1) * TT, queue_rows(QT - 1)), :],
                                 ys[b][:queue_rows(QT - 1), QT - 1, :]).then_inc(y_out[b], 16)

                sp.dma_start(enw[:], a["enw"]).then_inc(enw_in, 16)
                load_weights(0, 0)
                load_weights(1, 1)
                sp.wait_ge(scattered, 16 * 2 * NT)
                load_queue(0, 0)
                load_queue(1, 1)
                for e in range(E):
                    b = e % 2
                    if e + 2 < E:
                        sp.wait_ge(t_full, (e + 1) * DC)
                        load_queue(e + 2, b)
                    if e + 2 < E:
                        sp.wait_ge(y_ready, (e + 1) * QT)
                        load_weights(e + 2, b)
                    sp.wait_ge(ys_ready, (e + 1) * QT)
                    store_results(e, b)
                outv = out.rearrange("(j g) t d -> j (g t) d", j=NT)
                for j in range(NT):
                    sp.wait_ge(acc_ready, 2 * j + 2)
                    sp.dma_start(outv[j], acc[:, j, :]).then_inc(out_done, 16)
                sp.wait_ge(out_done, 16 * NT)

            @block.gpsimd
            def _(pool):
                for i in range(2):
                    for j in range(NT):
                        pool.indirect_dma_start(a["queues"], bass.IndirectOffsetOnAxis(ap=put[:, i, j:j + 1], axis=0),
                                                zt[:, j, :], None).then_inc(scattered, 16)
                for b in range(2):
                    pool.wait_ge(y_out[b], E // 2 * 32)
                for j in range(NT):
                    for i in range(2):
                        pool.indirect_dma_start(back[:, i, j, :], None, a["results"],
                                                bass.IndirectOffsetOnAxis(ap=get[:, i, j:j + 1], axis=0)
                                                ).then_inc(back_in[j], 16)

            @block.tensor
            def _(pe):
                def transposes(q, b, first=False):
                    pe.wait_ge(z_in[b], q * 32 + 32)
                    for c in range(DC):
                        if not first:
                            pe.wait_ge(ze_ready, (q * 2 + b - 1) * DC + (c + 1))
                        for j in range(QT):
                            n = queue_rows(j)
                            mm = nc.tensor.transpose(tbank[c][:DP, j * TT:j * TT + n],
                                                     zin[b][:n, j, c * DP:(c + 1) * DP], ident[:n, :n])
                        mm.then_inc(t_full, 1)

                def gate_up(q, b, first=False):
                    pe.wait_ge(w_in[b], q * 32 + 32)
                    pe.wait_ge(ze_ready, (q * 2 + b + 1) * DC)
                    for t in range(FC):
                        if t >= 2 or not first:
                            pe.wait_ge(hid_ready, (q * 2 + b) * FC + (t - 1))
                        for bank, off in ((gbank[t % 2], 0), (ubank[t % 2], FF)):
                            for c in range(DC):
                                mm = nc.tensor.matmul(bank[:, :CAP], w13[b][:, c, off + t * 128:off + (t + 1) * 128],
                                                      ze[b][:, c, :], start=(c == 0), stop=(c == DC - 1))
                        mm.then_inc(gu_ready, 1)

                def down(q, b, first=False):
                    pe.wait_ge(hid_ready, (q * 2 + b + 1) * FC)
                    for j in range(QT):
                        if j >= 2 or not first:
                            pe.wait_ge(ys_ready, (q * 2 + b) * QT + (j - 1))
                        n = queue_rows(j)
                        for t in range(FC):
                            mm = nc.tensor.matmul(ybank[(b + j) % 2][:n, :D], hid[b][:, t, j * TT:j * TT + n],
                                                  wd[b][:, t, :], start=(t == 0), stop=(t == FC - 1))
                        mm.then_inc(y_ready, 1)

                transposes(0, 0, True)
                transposes(0, 1)
                gate_up(0, 0, True)
                transposes(1, 0)
                gate_up(0, 1)
                down(0, 0, True)
                transposes(1, 1)
                gate_up(1, 0)
                down(0, 1)
                with pe.Fori(1, E // 2 - 1) as q:
                    transposes(q + 1, 0)
                    gate_up(q, 1)
                    down(q, 0)
                    transposes(q + 1, 1)
                    gate_up(q + 1, 0)
                    down(q, 1)
                gate_up(E // 2 - 1, 1)
                down(E // 2 - 1, 0)
                down(E // 2 - 1, 1)

            @block.scalar
            def _(act):
                def expert_norm(q, b):
                    for c in range(DC):
                        act.wait_ge(t_full, (q * 2 + b) * DC + (c + 1))
                        nc.scalar.activation(ze[b][:, c, :], tbank[c][:DP, :CAP], ACT.Copy,
                                             scale=enw[:, c, bass.ds(q * 2 + b, 1)]).then_inc(ze_ready, 1)

                def silu(q, b):
                    for t in range(FC):
                        act.wait_ge(gu_ready, (q * 2 + b) * FC + (t + 1))
                        nc.scalar.activation(sg[t % 2][:], gbank[t % 2][:, :CAP], ACT.Silu).then_inc(silu_ready, 1)

                act.wait_ge(enw_in, 16)
                expert_norm(0, 0)
                expert_norm(0, 1)
                with act.Fori(0, E // 2 - 1) as q:
                    for b in range(2):
                        silu(q, b)
                        expert_norm(q + 1, b)
                for b in range(2):
                    silu(E // 2 - 1, b)

            @block.vector
            def _(dve):
                def hidden(q, b):
                    for t in range(FC):
                        dve.wait_ge(silu_ready, (q * 2 + b) * FC + (t + 1))
                        nc.vector.tensor_tensor(hid[b][:, t, :], sg[t % 2][:], ubank[t % 2][:, :CAP], ALU.mult
                                                ).then_inc(hid_ready, 1)

                def results(q, b, first=False):
                    if not first:
                        dve.wait_ge(y_out[b], q * 32)
                    for j in range(QT):
                        n = queue_rows(j)
                        dve.wait_ge(y_ready, (q * 2 + b) * QT + (j + 1))
                        nc.vector.tensor_copy(ys[b][:n, j, :], ybank[(b + j) % 2][:n, :D]).then_inc(ys_ready, 1)

                for j in range(NT):
                    nc.vector.scalar_tensor_tensor(acc[:, j, :], xl[:, j, :], weights[:, 2, j:j + 1], h0[:, j, :],
                                                   ALU.mult, ALU.add).then_inc(base_ready, 1)
                hidden(0, 0)
                hidden(0, 1)
                results(0, 0, True)
                hidden(1, 0)
                results(0, 1, True)
                with dve.Fori(1, E // 2 - 1) as q:
                    hidden(q, 1)
                    results(q, 0)
                    hidden(q + 1, 0)
                    results(q, 1)
                hidden(E // 2 - 1, 1)
                results(E // 2 - 1, 0)
                results(E // 2 - 1, 1)
                dve.wait_ge(base_ready, NT)
                for j in range(NT):
                    dve.wait_ge(back_in[j], 32)
                    for i in range(2):
                        if i == 1:
                            dve.wait_ge(acc_ready, 2 * j + 1)
                        nc.vector.scalar_tensor_tensor(acc[:, j, :], back[:, i, j, :], weights[:, i, j:j + 1],
                                                       acc[:, j, :], ALU.mult, ALU.add).then_inc(acc_ready, 1)


def build(nc, a, out):
    with ExitStack() as ctx:
        def sb(name, shape, dt=fp32):
            return ctx.enter_context(nc.sbuf_tensor(name, shape, dt))

        h0 = sb("h0", [TT, NT, D])
        xres = sb("xres", [TT, NT, D])
        eps5 = sb("eps5", [128, 1])
        ident = sb("ident", [128, 128])
        ident_in = ctx.enter_context(nc.semaphore("ident_in"))
        with nc.Block() as block:
            @block.sync
            def _(sp):
                sp.dma_start(ident[:], a["ident"]).then_inc(ident_in, 16)
                sp.wait_ge(ident_in, 16)
        embed_program(nc, a, h0, xres, eps5)
        mamba_program(nc, a, xres, eps5, ident)
        xl, zt = sb("xl", [TT, NT, D]), sb("zt", [TT, NT, D])
        put, get = sb("put", [TT, 2, NT], int32), sb("get", [TT, 2, NT], int32)
        weights = sb("weights", [TT, 3, NT])
        gating_program(nc, a, h0, xres, eps5, ident, xl, zt, put, get, weights)
        expert_program(nc, a, h0, xl, ident, zt, put, get, weights, out)


def kernel(**inputs):
    import numpy as np
    import concourse.bacc as bacc
    from concourse.bass_utils import run_bass_kernel_spmd

    g = {name: np.asarray(v) for name, v in inputs.items()}
    f = lambda name: g[name]
    rows = lambda t, p: t.reshape(t.shape[0], t.shape[1] // p, p, *t.shape[2:]).swapaxes(1, 2)
    side = 84 // 16
    px = f("x")[:, :, :side * 16, :side * 16].reshape(NB, 3, side, 16, side, 16).transpose(1, 3, 5, 0, 2, 4)
    patches = np.zeros((KP * KC, NB, SEQ), np.float32)
    patches[:, :, 1:] = px.reshape(KP * KC, NB, side * side)
    cells = 32
    edges = np.arange(1.0 / cells, 1.0, 1.0 / cells, dtype=np.float32)
    frac = np.arange(0.0, 1.0 - 1e-06, 1.0 / side, dtype=np.float32)
    at = np.searchsorted(edges, frac, side="right")
    pos = f("L0_tok_pos_table")[(at[:, None] * cells + at).reshape(-1)]
    posb = np.tile(np.concatenate([f("cls_tok").reshape(1, D), pos]), (TT // SEQ, 1))
    cbias = np.zeros((TT // SEQ, SEQ, D), np.float32)
    cbias[:, 1:] = f("L0_tok_conv_b")
    xp = f("L0_attn_x_proj_w").swapaxes(1, 2)
    wxp = np.zeros((NL, I, XR), np.float32)
    wxp[:, :, :R] = xp[:, :, :R]
    wxp[:, :, BC0:] = xp[:, :, R:]
    chan = np.concatenate([f("L0_attn_conv_w").reshape(NL, I, K), f("L0_attn_conv_b")[:, :, None],
                           f("L0_attn_dt_proj_b")[:, :, None]], 2)
    ident = np.eye(128, dtype=np.float32)
    arrays = {
        "patches": patches.reshape(KC, KP, NTOK).swapaxes(0, 1),
        "wconv": f("L0_tok_conv_w").reshape(D, KC, KP).transpose(2, 1, 0),
        "posb": posb, "cbias": cbias.reshape(TT, D),
        "ident": ident, "id3": np.tile(np.eye(NBC, dtype=np.float32), (3, 1)),
        "win": rows(f("L0_attn_in_proj_w").swapaxes(1, 2), DP),
        "nw": rows(f("L0_attn_norm_w"), DP), "chan": rows(chan, 128), "wxp": rows(wxp, 128),
        "wdt": f("L0_attn_dt_proj_w").swapaxes(1, 2), "wout": rows(f("L0_attn_out_proj_w").swapaxes(1, 2), 128),
        "dskip": rows(f("L0_attn_D"), 128),
        "alog": rows(f("L0_attn_A_log"), 128).reshape(NL, 128, IC * NS),
        "fnw": np.tile(f("L0_attn_final_norm_w"), (TT, 1)),
        "gw": f("L0_ffn_gate_w").T.reshape(DC, DP, E).swapaxes(0, 1),
        "enw": f("L0_ffn_norm_w").T.reshape(DC, DP, E).swapaxes(0, 1),
        "w13": rows(f("L0_ffn_w13").swapaxes(1, 2), DP), "wd": rows(f("L0_ffn_w2").swapaxes(1, 2), 128),
        "tri": np.triu(np.ones((TT, TT), np.float32), 1), "ones": np.ones((TT, TT), np.float32),
        "first_row": np.tile(np.arange(E, dtype=np.float32) * CAP, (TT, NT, 1)),
        "behind": SLOTS + np.arange(2 * NTOK, dtype=np.float32).reshape(2, NT, TT).transpose(2, 0, 1),
        "rank": np.tile(np.arange(E, 0, -1, dtype=np.float32), (TT, NT, 1)),
    }
    nc = bacc.Bacc("TRN2", target_bir_lowering=False, num_devices=1)
    maps, a = {}, {}
    for name, v in arrays.items():
        maps[f"in_{name}"] = np.ascontiguousarray(v)
        a[name] = nc.dram_tensor(f"in_{name}", v.shape, fp32, kind="ExternalInput").ap()
    a["brows"] = nc.dram_tensor("brows", (NS, HT), fp32, kind="Internal").ap()
    a["queues"] = nc.dram_tensor("queues", (SLOTS + 2 * NTOK, D), fp32, kind="Internal").ap()
    a["results"] = nc.dram_tensor("results", (SLOTS, D), fp32, kind="Internal").ap()
    out = nc.dram_tensor("out_0", (NB, SEQ, D), fp32, kind="ExternalOutput").ap()
    build(nc, a, out)
    r = run_bass_kernel_spmd(nc, [maps], core_ids=[0])
    return r.results[0]["out_0"]
```

```python
import concourse.bass as bass
from concourse import mybir
from contextlib import ExitStack

NB, SEQ, D = 32, 26, 192
NTOK = NB * SEQ
TT = 104
NT = NTOK // TT
HB = NB // 2
HT = HB * SEQ
HNT = HT // TT
KP, KC = 128, 6
DC, DP = 2, 96
NL, I, NS, R, K = 16, 384, 16, 48, 4
IC = I // 128
XR = 96
BC0, NBC = 64, 2 * NS
UNITS = NS * IC
TPAD = K - 1 + SEQ
E, FF, CAP = 8, 512, 260
FC = FF // 128
SLOTS = E * CAP
QT = 3

LN_SLACK = 1.3e-7
R_DBU, R_H, R_HC = 4, 2, 2
R_DA = 2
NQ, QS = 4, NS // 4

Z_AT, Y_AT, OUT_AT, NEARLY = (0, 1, 5), (2, 3, 4), (6, 7), 8
J_TR, J_U, J_CONV, J_XP, J_DT, NPRE = 0, (2, 3, 5), (4, 6, 7), 8, 9, 12
NSH = NEARLY + NPRE

WHEN = dict(
    act_sums=(3, 3, 4), act_spread_late=(11,), act_diagonal=(0, 6, 8, 18, 18, 18), act_rms=(11,),
    act_ddiag=(47,), act_hT=(13, 15), act_upad=(19, 21, 29), act_conv=(29, 34, 36), act_usig=(33, 35, 38),
    act_bc=(42,), act_spread=(45, 45, 45), act_dtx=(43, 43, 44), act_dexp=(43, 44, 44),
    act_z=(4, 4, 6), act_zsig=(5, 5, 9),
    dve_y=(3, 3, 4), dve_resid=(9, 9), dve_uclamp=(30, 33, 36), dve_bc=(41,),
    dve_parts=(41,), dve_dclamp=(41, 42, 44), dve_dt=(44, 44, 47), dve_zclamp=(3, 3, 6),
    pe_sums=(2, 2, 2), pe_out=(4, 4), pe_hT=(10, 12), pe_u=(13, 16, 25), pe_conv=(20, 28, 31),
    pe_xp=(37,), pe_dt=(39, 40, 40), pe_z=(2, 2, 3),
    dve_times_c=(1,), pe_broadcast=(1,), pe_reduce=(2, 2, 2),
    pool_u=(44, 44, 44), pool_poly=(47, 47, 47), pool_z=(9, 14, 16))


def turns(name, v):
    return [i for i, at in enumerate(WHEN[name]) if at == v]


fp32 = mybir.dt.float32
bf16 = mybir.dt.bfloat16
int32 = mybir.dt.int32
ALU = mybir.AluOpType
ACT = mybir.ActivationFunctionType
AX = mybir.AxisListType


def embed_program(nc, a, h0, xres, eps5):
    with ExitStack() as ctx:
        def sb(name, shape, dt=fp32):
            return ctx.enter_context(nc.sbuf_tensor(name, shape, dt))

        def sem(name):
            return ctx.enter_context(nc.semaphore(name))

        patches = sb("patches", [KP, KC, NTOK])
        wconv = sb("wconv", [KP, KC, D])
        posb = sb("posb", [TT, D])
        cbias = sb("cbias", [TT, D])
        stats = sb("stats", [TT, NT, 6])
        mv = sb("mv", [TT, NT, 2])
        rstd = sb("rstd", [TT, NT])
        ps = [ctx.enter_context(nc.psum_tensor(f"pe{i}", [128, 512], fp32)) for i in range(2)]
        patch_in = [sem(f"patch_in{i}") for i in range(KC)]
        w_in, b_in = sem("w_in"), sem("b_in")
        clear = sb("clear", [TT, SLOTS // TT * D])
        clear_set, cleared = sem("clear_set"), sem("cleared")
        eps_set = sem("eps_set")
        bias_ready, emb_ready, emb_taken = sem("bias_ready"), sem("emb_ready"), sem("emb_taken")
        stat_ready, mv_ready, ln_ready, rstd_ready, x_ready = (
            sem("stat_ready"), sem("mv_ready"), sem("ln_ready"), sem("rstd_ready"), sem("x_ready"))

        with nc.Block() as block:
            @block.sync
            def _(sp):
                sp.dma_start(wconv[:], a["wconv"]).then_inc(w_in, 16)
                for c in range(KC):
                    sp.dma_start(patches[:, c, :], a["patches"][:, c, :]).then_inc(patch_in[c], 16)
                sp.dma_start(posb[:], a["posb"]).then_inc(b_in, 16)
                sp.dma_start(cbias[:], a["cbias"]).then_inc(b_in, 16)
                sp.wait_ge(clear_set, 1)
                sp.dma_start(a["queues"][:SLOTS].rearrange("(q r) d -> q (r d)", q=TT), clear[:]
                             ).then_inc(cleared, 16)
                sp.wait_ge(cleared, 16)

            @block.gpsimd
            def _(pool):
                nc.gpsimd.memset(clear[:], 0.0).then_inc(clear_set, 1)

            @block.tensor
            def _(pe):
                pe.wait_ge(w_in, 16)
                for c in range(KC):
                    pe.wait_ge(patch_in[c], 16)
                for j in range(NT):
                    if j >= 2:
                        pe.wait_ge(emb_taken, j - 1)
                    for c in range(KC):
                        mm = nc.tensor.matmul(ps[j % 2][:TT, :D], patches[:, c, j * TT:(j + 1) * TT],
                                              wconv[:, c, :], start=(c == 0), stop=(c == KC - 1))
                    mm.then_inc(emb_ready, 1)

            @block.vector
            def _(dve):
                nc.vector.memset(eps5[:], 1e-5).then_inc(eps_set, 1)
                dve.wait_ge(b_in, 32)
                nc.vector.tensor_tensor(posb[:], posb[:], cbias[:], ALU.add).then_inc(bias_ready, 1)
                dve.wait_ge(bias_ready, 1)
                for j in range(NT):
                    dve.wait_ge(emb_ready, j + 1)
                    nc.vector.tensor_tensor(h0[:, j, :], ps[j % 2][:TT, :D], posb[:], ALU.add
                                            ).then_inc(emb_taken, 1)
                    dve.wait_ge(emb_taken, j + 1)
                    nc.vector.bn_stats(stats[:, j, :], h0[:, j, :]).then_inc(stat_ready, 1)
                    dve.wait_ge(stat_ready, j + 1)
                    nc.vector.bn_aggr(mv[:, j, :], stats[:, j, :]).then_inc(mv_ready, 1)
                dve.wait_ge(rstd_ready, 1)
                for j in range(NT):
                    nc.vector.tensor_scalar(xres[:, j, :], h0[:, j, :], mv[:, j, 0:1], rstd[:, j:j + 1],
                                            ALU.subtract, ALU.mult).then_inc(x_ready, 1)

            @block.scalar
            def _(act):
                nc.scalar.preload_act_table_set("natural_log_exp_and_others")
                act.wait_ge(eps_set, 1)
                act.wait_ge(mv_ready, NT)
                nc.scalar.activation(rstd[:], mv[:, :, 1], ACT.Ln, bias=eps5[:TT, 0:1]).then_inc(ln_ready, 1)
                act.wait_ge(ln_ready, 1)
                nc.scalar.activation(rstd[:], rstd[:], ACT.Exp, scale=-0.5).then_inc(rstd_ready, 1)


def mamba_program(nc, a, xres, eps5, ident):
    with ExitStack() as ctx:
        def sb(name, shape, dt=fp32):
            return ctx.enter_context(nc.sbuf_tensor(name, shape, dt))

        def sem(name):
            return ctx.enter_context(nc.semaphore(name))

        winu, winz = sb("winu", [DP, DC, I]), sb("winz", [DP, DC, I])
        nw = sb("nw", [DP, DC])
        chan = sb("chan", [128, IC, K + 2])
        cdiag = sb("cdiag", [128, IC, K, 128])
        wxp = sb("wxp", [128, IC, XR])
        wdt = sb("wdt", [R, I])
        wout = sb("wout", [128, IC, D])
        dskip = sb("dskip", [128, IC])
        ddiag = sb("ddiag", [128, IC, 128])
        alog = sb("alog", [128, IC * NS])
        nega = sb("nega", [128, IC * NS])
        id3 = sb("id3", [XR, NBC])
        sel = sb("sel", [XR, NS, 128], bf16)
        one, third = sb("one", [128, 1]), sb("third", [128, 1])
        sq = sb("sq", [TT, HNT, D])
        ssq = sb("ssq", [TT, HNT])
        rrms = sb("rrms", [TT, HNT])
        xn = sb("xn", [TT, HNT, D])
        hT = sb("hT", [DP, DC, HT])
        upad = sb("upad", [128, IC, HB, TPAD])
        uc = sb("uc", [128, IC, HT])
        zraw = sb("zraw", [128, IC, HT])
        gA = sb("gA", [128, IC, HT])
        gB = sb("gB", [128, IC, HT])
        gC = sb("gC", [128, IC, HT])
        gZ = sb("gZ", [128, IC, HT])
        dtr = sb("dtr", [R, HT])
        brow = sb("brow", [NS, HT])
        resid = sb("resid", [XR, HT])
        u = [sb(f"u{h}", [128, IC, HT]) for h in range(2)]
        zs = [sb(f"zs{h}", [128, IC, HT]) for h in range(2)]
        dt = [sb(f"dt{h}", [128, IC, HT]) for h in range(2)]
        dtu = [sb(f"dtu{h}", [128, IC, HT]) for h in range(2)]
        parts = [sb(f"parts{h}", [XR, HT], bf16) for h in range(2)]
        sums = sb("sums", [TT, IC, HNT * 128])
        y = sb("y", [128, IC, HT])
        ball = sb("ball", [128, NS, HT])
        dbu = sb("dbu", [128, R_DBU, IC, HT])
        hst = sb("hst", [128, R_H, IC, HT])
        hc = sb("hc", [128, R_HC, IC, HT])

        pb = [ctx.enter_context(nc.psum_tensor(f"pm{i}", [128, 512], fp32)) for i in range(8)]
        yacc = pb[0:3]
        cbank = pb[3]
        dab = pb[4:6]
        shared = pb[6:8]

        zeroed = sem("zeroed")
        z_in, pre_in, post_in, alog_in, id3_in = sem("z_in"), sem("pre_in"), sem("post_in"), sem("alog_in"), sem("id3_in")
        sel_ready, nega_exp, nega_ready = sem("sel_ready"), sem("nega_exp"), sem("nega_ready")
        diag_ready, ddiag_ready = sem("diag_ready"), sem("ddiag_ready")
        sh_full, sh_free = sem("sh_full"), [sem("sh_free0"), sem("sh_free1")]
        exp_done, m1_done, scan_done, c_ready, m2_done, reduce_done = (
            sem("exp_done"), sem("m1_done"), sem("scan_done"), sem("c_ready"), sem("m2_done"),
            sem("reduce_done"))
        sums_copied = sem("sums_copied")
        sq_done, rms_ln, rms_ready, xn_ready = sem("sq_done"), sem("rms_ln"), sem("rms_ready"), sem("xn_ready")
        uclamp, uexp, uln, usig, u_ready = sem("uclamp"), sem("uexp"), sem("uln"), sem("usig"), sem("u_ready")
        zclamp, zexp, zln, zsig, z_ready = sem("zclamp"), sem("zexp"), sem("zln"), sem("zsig"), sem("z_ready")
        bc_hi, bc_mid, parts_ready = sem("bc_hi"), sem("bc_mid"), sem("parts_ready")
        b_saved = sem("b_saved")
        b_in = [sem(f"b_in{q}") for q in range(NQ)]
        dclamp, dexp, dln, dpoly = sem("dclamp"), sem("dexp"), sem("dln"), sem("dpoly")
        dpoly4, dpoly3 = sem("dpoly4"), sem("dpoly3")
        dt_ready, dtu_ready = sem("dt_ready"), sem("dtu_ready")

        NM1 = NS - 1 + IC
        CREDIT = R_DBU * IC

        def first_of(x):
            return isinstance(x, int) and x == 0

        def tile(k, i):
            i += NPRE - len(Y_AT) - len(OUT_AT)
            return i % 2, k * (NSH // 2) + i // 2, k * NSH + i

        def pre_tile(p, j):
            return (j % 2, j // 2, j) if first_of(p) else tile(p, j - NPRE)

        def z_tile(k, i):
            return (i % 2, (NPRE + i) // 2, NPRE + i) if first_of(k) else tile(k, Z_AT[i])

        def post_tile(k, i):
            if isinstance(k, int) and k == 2 * NL:
                return tile(k, i - NPRE)
            return tile(k, (Y_AT + OUT_AT)[i])

        def wait_full(engine, t):
            engine.wait_ge(sh_full, t[2] + 1)

        def wait_taken(engine, t):
            engine.wait_ge(sh_free[t[0]], t[1] + 1)

        with nc.Block() as block:
            @block.sync
            def _(sp):
                def load_pre(l):
                    for dst, src in ((winu, "winu"), (nw, "nw"), (chan, "chan"), (wxp, "wxp"), (wdt, "wdt")):
                        s = a[src]
                        sp.dma_start(dst[:], s[bass.ds(l, 1)].rearrange(
                            "o p a b -> p (o a) b" if len(s.shape) == 4 else "o p a -> p (o a)")
                        ).then_inc(pre_in, 16)

                def load_z(l):
                    sp.dma_start(winz[:], a["winz"][bass.ds(l, 1)].rearrange("o p a b -> p (o a) b")
                                 ).then_inc(z_in, 16)

                def load_post(l):
                    sp.dma_start(wout[:], a["wout"][bass.ds(l, 1)].rearrange("o p a b -> p (o a) b")
                                 ).then_inc(post_in, 16)
                    sp.dma_start(dskip[:], a["dskip"][bass.ds(l, 1)].rearrange("o p a -> p (o a)")
                                 ).then_inc(post_in, 16)

                def load_alog(l):
                    sp.dma_start(alog[:], a["alog"][bass.ds(l, 1)].rearrange("o p a -> p (o a)")
                                 ).then_inc(alog_in, 16)

                def layer(l, first, last):
                    if not first:
                        sp.wait_ge(sh_full, post_tile(2 * l, IC + 1)[2] + 1)
                        load_post(l)
                    if not last:
                        sp.wait_ge(nega_ready, l + 1)
                        load_alog(l + 1)
                    if not last:
                        wait_taken(sp, pre_tile(l * 2 + 1, J_DT + IC - 1))
                        load_pre(l + 1)
                        sp.wait_ge(sh_full, z_tile(l * 2 + 1, IC - 1)[2] + 1)
                        load_z(l + 1)

                sp.dma_start(id3[:], a["id3"]).then_inc(id3_in, 16)
                load_pre(0)
                load_z(0)
                load_alog(0)
                load_post(0)
                layer(0, True, False)
                with sp.Fori(1, NL - 1) as l:
                    layer(l, False, False)
                layer(NL - 1, False, True)

            @block.gpsimd
            def _(pool):
                def pre(p, slot, o):
                    for i in turns("pool_u", slot):
                        pool.wait_ge(usig, p * IC + i + 1)
                        nc.gpsimd.tensor_tensor(u[o][:, i, :], uc[:, i, :], gA[:, i, :], ALU.mult
                                                ).then_inc(u_ready, 1)
                    for i in turns("pool_poly", slot):
                        pool.wait_ge(dpoly4, p * IC + i + 1)
                        nc.gpsimd.tensor_tensor(gC[:, i, :], gC[:, i, :], gA[:, i, :], ALU.mult
                                                ).then_inc(dpoly3, 1)

                def first_state(k, h, i):
                    pool.wait_ge(dt_ready, k * IC + i + 1)
                    nc.gpsimd.tensor_tensor(dtu[h][:, i, :], dt[h][:, i, :], u[h][:, i, :], ALU.mult
                                            ).then_inc(dtu_ready, 1)
                    if i == 0:
                        pool.wait_ge(b_in[0], k * 16 + 16)
                        pool.wait_ge(scan_done, k * UNITS + IC)
                    pool.wait_ge(dtu_ready, k * IC + i + 1)
                    nc.gpsimd.tensor_tensor(dbu[:, 0, i, :], dtu[h][:, i, :], ball[:, 0, :], ALU.mult
                                            ).then_inc(m1_done, 1)

                def times_b(k, h, n):
                    if n % QS == 0:
                        pool.wait_ge(b_in[n // QS], k * 16 + 16)
                    pool.wait_ge(scan_done, k * UNITS + (n + 1) * IC)
                    nc.gpsimd.tensor_tensor(
                        dbu[:, n % R_DBU, :, :], dtu[h][:],
                        ball[:, n, :].rearrange("q (o t) -> q o t", o=1).to_broadcast([128, IC, HT]),
                        ALU.mult).then_inc(m1_done, 1)

                def step(l, h, first, last):
                    k = l * 2 + h
                    for v in range(UNITS):
                        n, i = divmod(v, IC)
                        if v == 0:
                            for c in range(IC):
                                first_state(k, h, c)
                        elif i == 0:
                            times_b(k, h, n)
                        for c in turns("pool_z", v):
                            pool.wait_ge(zsig, k * IC + c + 1)
                            nc.gpsimd.tensor_tensor(zs[h][:, c, :], zraw[:, c, :], gZ[:, c, :], ALU.mult
                                                    ).then_inc(z_ready, 1)
                        if not last:
                            pre(k + 1, v, 1 - h)

                nc.gpsimd.memset(upad[:], 0.0).then_inc(zeroed, 1)
                for slot in range(UNITS):
                    pre(0, slot, 0)
                for h in range(2):
                    step(0, h, h == 0, False)
                with pool.Fori(1, NL - 1) as l:
                    for h in range(2):
                        step(l, h, False, False)
                for h in range(2):
                    step(NL - 1, h, False, h == 1)

            @block.scalar
            def _(act):
                def diagonal(i, t):
                    nc.scalar.activation(cdiag[:, i, t, :], ident[:], ACT.Copy,
                                         scale=chan[:, i, t:t + 1]).then_inc(diag_ready, 1)

                def take(t, out, rows, func=ACT.Identity, **kw):
                    wait_full(act, t)
                    src = shared[t[0]][rows, :HT]
                    if len(out.shape) == 3:
                        src = src.rearrange("q (b t) -> q b t", t=SEQ)
                    return nc.scalar.activation(out, src, func, **kw)

                def sigmoid(x, i, p, clamped, exps, lns, done):
                    act.wait_ge(clamped, p * IC + i + 1)
                    nc.scalar.activation(x[:, i, :], x[:, i, :], ACT.Exp, scale=-1.0).then_inc(exps, 1)
                    act.wait_ge(exps, p * IC + i + 1)
                    nc.scalar.activation(x[:, i, :], x[:, i, :], ACT.Ln, bias=one[:, 0:1]).then_inc(lns, 1)
                    act.wait_ge(lns, p * IC + i + 1)
                    nc.scalar.activation(x[:, i, :], x[:, i, :], ACT.Exp, scale=-1.0).then_inc(done, 1)

                def save_b(p):
                    if not first_of(p):
                        for q in range(NQ):
                            act.wait_ge(b_in[q], p * 16)
                    act.wait_ge(bc_hi, p * 3 + 2)
                    act.dma_start(a["brows"], brow[:]).then_inc(b_saved, 16)

                def spread_b(p, q):
                    if not first_of(p):
                        act.wait_ge(m1_done, p * NM1 + ((q + 1) * QS - NS))
                    act.wait_ge(b_saved, p * 16 + 16)
                    act.dma_start(ball[:, q * QS:(q + 1) * QS, :],
                                  a["brows"][q * QS:(q + 1) * QS, :].rearrange("(o n) t -> o n t", o=1)
                                  .to_broadcast([128, QS, HT])).then_inc(b_in[q], 16)

                def pre(p, slot, o):
                    for _ in turns("act_rms", slot):
                        for j in range(HNT):
                            nc.scalar.activation(sq[:, j, :], xres[:, o * HNT + j, :], ACT.Square,
                                                 accum_out=ssq[:, j:j + 1]).then_inc(sq_done, 1)
                        act.wait_ge(sq_done, p * HNT + HNT)
                        nc.scalar.activation(rrms[:], ssq[:], ACT.Ln, bias=eps5[:TT, 0:1], scale=1.0 / D
                                             ).then_inc(rms_ln, 1)
                        act.wait_ge(rms_ln, p + 1)
                        nc.scalar.activation(rrms[:], rrms[:], ACT.Exp, scale=-0.5).then_inc(rms_ready, 1)
                        act.wait_ge(rms_ready, p + 1)
                        for j in range(HNT):
                            nc.scalar.activation(xn[:, j, :], xres[:, o * HNT + j, :], ACT.Copy,
                                                 scale=rrms[:, j:j + 1]).then_inc(xn_ready, 1)
                    for c in turns("act_hT", slot):
                        t = pre_tile(p, J_TR + c)
                        take(t, hT[:, c, :], slice(0, DP), scale=nw[:, c:c + 1]).then_inc(sh_free[t[0]], 1)
                    for i in turns("act_upad", slot):
                        t = pre_tile(p, J_U[i])
                        take(t, upad[:, i, :, K - 1:], slice(0, 128)).then_inc(sh_free[t[0]], 1)
                    for i in turns("act_conv", slot):
                        t = pre_tile(p, J_CONV[i])
                        take(t, uc[:, i, :], slice(0, 128), bias=chan[:, i, K:K + 1]).then_inc(sh_free[t[0]], 1)
                    for i in turns("act_usig", slot):
                        sigmoid(gA, i, p, uclamp, uexp, uln, usig)
                    for _ in turns("act_bc", slot):
                        t = pre_tile(p, J_XP)
                        take(t, dtr[:], slice(0, R)).then_inc(bc_hi, 1)
                        if not first_of(p):
                            act.wait_ge(b_saved, p * 16)
                        take(t, brow[:], slice(BC0, BC0 + NS)).then_inc(bc_hi, 1)
                        take(t, parts[o][0:NBC, :], slice(BC0, XR)).then_inc(bc_hi, 1)
                        save_b(p)
                    for q in turns("act_spread", slot):
                        spread_b(p, q)
                    for i in turns("act_dtx", slot):
                        t = pre_tile(p, J_DT + i)
                        take(t, uc[:, i, :], slice(0, 128), bias=chan[:, i, K + 1:K + 2]
                             ).then_inc(sh_free[t[0]], 1)
                    for i in turns("act_dexp", slot):
                        act.wait_ge(dclamp, p * IC + i + 1)
                        nc.scalar.activation(gA[:, i, :], gA[:, i, :], ACT.Exp).then_inc(dexp, 1)
                        act.wait_ge(dexp, p * IC + i + 1)
                        nc.scalar.activation(gC[:, i, :], gA[:, i, :], ACT.Identity, bias=third[:, 0:1],
                                             scale=-0.25).then_inc(dpoly4, 1)
                        nc.scalar.activation(gB[:, i, :], gA[:, i, :], ACT.Ln, bias=one[:, 0:1]).then_inc(dln, 1)

                def copy_sums(k, i):
                    act.wait_ge(reduce_done, k * (NS * IC) - IC + i + 1)
                    nc.scalar.copy(sums[:, i, :], yacc[i][:TT, :]).then_inc(sums_copied, 1)

                def step(l, h, first, last):
                    k = l * 2 + h
                    if h == 0:
                        act.wait_ge(alog_in, l * 16 + 16)
                        if not first:
                            act.wait_ge(exp_done, k * UNITS)
                        nc.scalar.activation(nega[:], alog[:], ACT.Exp).then_inc(nega_exp, 1)
                        act.wait_ge(nega_exp, l + 1)
                        nc.scalar.mul(nega[:], nega[:], -1.0).then_inc(nega_ready, 1)
                        act.wait_ge(nega_ready, l + 1)
                    for v in range(UNITS):
                        n, i = divmod(v, IC)
                        if n == 0:
                            act.wait_ge(dt_ready, k * IC + i + 1)
                        act.wait_ge(scan_done, k * UNITS + v - R_DA + 1 + CREDIT)
                        nc.scalar.activation(
                            dab[v % R_DA][:, :HT].rearrange("q (b t) -> q b t", t=SEQ)[:, :, 1:],
                            dt[h][:, i, :].rearrange("q (b t) -> q b t", t=SEQ)[:, :, 1:],
                            ACT.Exp, scale=nega[:, i * NS + n:i * NS + n + 1]).then_inc(exp_done, 1)
                        for i in turns("act_z", v):
                            t = z_tile(k, i)
                            take(t, zraw[:, i, :], slice(0, 128)).then_inc(sh_free[t[0]], 1)
                        for i in turns("act_zsig", v):
                            sigmoid(gZ, i, k, zclamp, zexp, zln, zsig)
                        for i in turns("act_sums", v):
                            if not first:
                                copy_sums(k, i)
                        for _ in turns("act_ddiag", v):
                            if h == 0:
                                act.wait_ge(post_in, l * 32 + 32)
                                if not first:
                                    wait_full(act, post_tile(k, IC))
                                for c in range(IC):
                                    nc.scalar.activation(ddiag[:, c, :], ident[:], ACT.Copy,
                                                         scale=dskip[:, c:c + 1]).then_inc(ddiag_ready, 1)
                        for _ in turns("act_spread_late", v):
                            spread_b(k, NQ - 1)
                        if not last:
                            for q in turns("act_diagonal", v):
                                if h == 0:
                                    break
                                if q == 0:
                                    act.wait_ge(pre_in, l * 80 + 160)
                                for t in range(2):
                                    diagonal(q // 2, (q % 2) * 2 + t)
                            if v == WHEN["act_rms"][0] and not first:
                                wait_taken(act, post_tile(k, IC))
                                wait_taken(act, post_tile(k, IC + 1))
                            pre(k + 1, v, 1 - h)

                act.wait_ge(zeroed, 5)
                for slot in range(UNITS):
                    pre(0, slot, 0)
                    if slot == WHEN["act_rms"][0]:
                        act.wait_ge(pre_in, 80)
                        for i in range(IC):
                            for t in range(K):
                                diagonal(i, t)
                for h in range(2):
                    step(0, h, h == 0, False)
                with act.Fori(1, NL - 1) as l:
                    for h in range(2):
                        step(l, h, False, False)
                for h in range(2):
                    step(NL - 1, h, False, h == 1)
                for i in range(IC):
                    copy_sums(2 * NL, i)

            @block.vector
            def _(dve):
                def pre(p, slot, o):
                    for i in turns("dve_uclamp", slot):
                        wait_taken(dve, pre_tile(p, J_CONV[i]))
                        nc.vector.tensor_scalar(gA[:, i, :], uc[:, i, :], -40.0, None, ALU.max
                                                ).then_inc(uclamp, 1)
                    for _ in turns("dve_bc", slot):
                        t = pre_tile(p, J_XP)
                        dve.wait_ge(bc_hi, p * 3 + 3)
                        nc.vector.tensor_tensor(resid[NBC:2 * NBC, :], shared[t[0]][BC0:XR, :HT],
                                                parts[o][0:NBC, :], ALU.subtract).then_inc(sh_free[t[0]], 1)
                    for _ in turns("dve_parts", slot):
                        wait_taken(dve, pre_tile(p, J_XP))
                        nc.vector.tensor_copy(parts[o][NBC:2 * NBC, :], resid[NBC:2 * NBC, :]).then_inc(bc_mid, 1)
                        dve.wait_ge(bc_mid, p + 1)
                        nc.vector.tensor_tensor(parts[o][2 * NBC:XR, :], resid[NBC:2 * NBC, :],
                                                parts[o][NBC:2 * NBC, :], ALU.subtract).then_inc(parts_ready, 1)
                    for i in turns("dve_dclamp", slot):
                        wait_taken(dve, pre_tile(p, J_DT + i))
                        nc.vector.tensor_scalar(gA[:, i, :], uc[:, i, :], 17.0, None, ALU.min
                                                ).then_inc(dclamp, 1)
                    for i in turns("dve_dt", slot):
                        dve.wait_ge(dpoly3, p * IC + i + 1)
                        nc.vector.scalar_tensor_tensor(gC[:, i, :], gC[:, i, :], -0.5, gA[:, i, :],
                                                       ALU.add, ALU.mult).then_inc(dpoly, 1)
                        dve.wait_ge(dpoly, (p * IC + i) * 3 + 1)
                        nc.vector.scalar_tensor_tensor(gC[:, i, :], gC[:, i, :], 1.0, gA[:, i, :],
                                                       ALU.add, ALU.mult).then_inc(dpoly, 1)
                        dve.wait_ge(dpoly, (p * IC + i) * 3 + 2)
                        dve.wait_ge(dln, p * IC + i + 1)
                        nc.vector.scalar_tensor_tensor(gC[:, i, :], gB[:, i, :], -LN_SLACK, gC[:, i, :],
                                                       ALU.add, ALU.max).then_inc(dpoly, 1)
                        dve.wait_ge(dpoly, (p * IC + i) * 3 + 3)
                        nc.vector.tensor_tensor(dt[o][:, i, :], gC[:, i, :], uc[:, i, :], ALU.max
                                                ).then_inc(dt_ready, 1)

                def finish_y(k, o, i):
                    t = post_tile(k, i)
                    if i == 0:
                        dve.wait_ge(z_ready, k * IC)
                    wait_full(dve, t)
                    nc.vector.tensor_tensor(y[:, i, :], shared[t[0]][:, :HT], zs[o][:, i, :], ALU.mult
                                            ).then_inc(sh_free[t[0]], 1)

                def add_residual(k, o, i):
                    t = post_tile(k, IC + i)
                    wait_full(dve, t)
                    j = o * HNT + 2 * i
                    nc.vector.tensor_tensor(xres[:, j:j + 2, :], xres[:, j:j + 2, :],
                                            shared[t[0]][:TT, :2 * D].rearrange("q (a d) -> q a d", a=2),
                                            ALU.add).then_inc(sh_free[t[0]], 1)

                def times_c(k, n):
                    dve.wait_ge(scan_done, k * UNITS + (n + 1) * IC + CREDIT)
                    dve.wait_ge(c_ready, k * NS + n + 1)
                    if n >= R_HC or not first_of(k):
                        dve.wait_ge(reduce_done, k * (NS * IC) + (n - R_HC + 1) * IC)
                    nc.vector.tensor_tensor(
                        hc[:, n % R_HC, :, :], hst[:, n % R_H, :, :],
                        cbank[:, :HT].rearrange("q (o t) -> q o t", o=1).to_broadcast([128, IC, HT]),
                        ALU.mult).then_inc(m2_done, 1)

                def step(l, h, first, last):
                    k = l * 2 + h
                    for v in range(UNITS):
                        n, i = divmod(v, IC)
                        if i == 0 or n == 0:
                            dve.wait_ge(m1_done, k * NM1 + (v + 1 if n == 0 else n + IC))
                        if i == 0:
                            if n >= R_H or not first:
                                dve.wait_ge(m2_done, k * NS + n - R_H + 1)
                        dve.wait_ge(exp_done, k * UNITS + v + 1)
                        nc.vector.tensor_tensor_scan(hst[:, n % R_H, i, :], dab[v % R_DA][:, :HT],
                                                     dbu[:, n % R_DBU, i, :], 0.0, ALU.mult, ALU.add
                                                     ).then_inc(scan_done, 1)
                        if turns("dve_times_c", i) and n >= 1:
                            times_c(k, n - 1)
                        for i in turns("dve_zclamp", v):
                            wait_taken(dve, z_tile(k, i))
                            nc.vector.tensor_scalar(gZ[:, i, :], zraw[:, i, :], -40.0, None, ALU.max
                                                    ).then_inc(zclamp, 1)
                        for c in turns("dve_y", v):
                            if not first:
                                finish_y(k, 1 - h, c)
                        for c in turns("dve_resid", v):
                            if not first:
                                add_residual(k, 1 - h, c)
                        if not last:
                            pre(k + 1, v, 1 - h)
                    times_c(k, NS - 1)

                nc.vector.memset(one[:], 1.0).then_inc(zeroed, 1)
                nc.vector.memset(third[:], 1.0 / 3.0).then_inc(zeroed, 1)
                for b in dab:
                    nc.vector.memset(b[:], 0.0).then_inc(zeroed, 1)
                for r in range(CREDIT):
                    nc.vector.memset(dbu[:, r // IC, r % IC, 0:1], 0.0).then_inc(scan_done, 1)
                dve.wait_ge(id3_in, 16)
                nc.vector.tensor_copy(sel[:], id3[:, NS:].rearrange("q (n o) -> q n o", o=1)
                                      .to_broadcast([XR, NS, 128])).then_inc(sel_ready, 1)
                dve.wait_ge(zeroed, 5)
                for slot in range(UNITS):
                    pre(0, slot, 0)
                for h in range(2):
                    step(0, h, h == 0, False)
                with dve.Fori(1, NL - 1) as l:
                    for h in range(2):
                        step(l, h, False, False)
                for h in range(2):
                    step(NL - 1, h, False, h == 1)
                for i in range(IC):
                    finish_y(2 * NL, 1, i)
                for i in range(2):
                    add_residual(2 * NL, 1, i)

            @block.tensor
            def _(pe):
                def open_shared(t):
                    if not first_of(t[1]):
                        pe.wait_ge(sh_free[t[0]], t[1])
                    return shared[t[0]]

                def in_projection(t, w, i):
                    bank = open_shared(t)
                    for c in range(DC):
                        mm = nc.tensor.matmul(bank[:, :HT], w[:, c, i * 128:(i + 1) * 128], hT[:, c, :],
                                              start=(c == 0), stop=(c == DC - 1))
                    mm.then_inc(sh_full, 1)

                def pre(p, slot, o, diagonals):
                    for c in turns("pe_hT", slot):
                        bank = open_shared(pre_tile(p, J_TR + c))
                        pe.wait_ge(xn_ready, p * HNT + HNT)
                        for j in range(HNT):
                            mm = nc.tensor.transpose(bank[:DP, j * TT:(j + 1) * TT],
                                                     xn[:, j, c * DP:(c + 1) * DP], ident[:TT, :TT])
                        mm.then_inc(sh_full, 1)
                    for i in turns("pe_u", slot):
                        if i == 0:
                            wait_taken(pe, pre_tile(p, J_TR))
                            wait_taken(pe, pre_tile(p, J_TR + 1))
                        in_projection(pre_tile(p, J_U[i]), winu, i)
                    for i in turns("pe_conv", slot):
                        bank = open_shared(pre_tile(p, J_CONV[i]))
                        wait_taken(pe, pre_tile(p, J_U[i]))
                        if i == 0:
                            pe.wait_ge(diag_ready, diagonals)
                        for t in range(K):
                            mm = nc.tensor.matmul(bank[:, :HT], cdiag[:, i, t, :], upad[:, i, :, t:t + SEQ],
                                                  start=(t == 0), stop=(t == K - 1))
                        mm.then_inc(sh_full, 1)
                    for _ in turns("pe_xp", slot):
                        bank = open_shared(pre_tile(p, J_XP))
                        for i in range(IC):
                            pe.wait_ge(u_ready, p * IC + i + 1)
                            mm = nc.tensor.matmul(bank[:XR, :HT], wxp[:, i, :], u[o][:, i, :],
                                                  start=(i == 0), stop=(i == IC - 1))
                        mm.then_inc(sh_full, 1)
                    for i in turns("pe_dt", slot):
                        bank = open_shared(pre_tile(p, J_DT + i))
                        if i == 0:
                            pe.wait_ge(bc_hi, p * 3 + 1)
                        nc.tensor.matmul(bank[:, :HT], wdt[:, i * 128:(i + 1) * 128], dtr[:],
                                         start=True, stop=True).then_inc(sh_full, 1)

                def broadcast_c(k, h, n):
                    if n == 0:
                        pe.wait_ge(parts_ready, k + 1)
                    if n >= 1 or not first_of(k):
                        pe.wait_ge(m2_done, k * NS + n)
                    nc.tensor.matmul(cbank[:, :HT], sel[:, n, :], parts[h][:], start=True, stop=True
                                     ).then_inc(c_ready, 1)

                def reduce(k, n, i):
                    if i == 0:
                        pe.wait_ge(m2_done, k * NS + n + 1)
                    if n == 0 and not first_of(k):
                        pe.wait_ge(sums_copied, (k - 1) * IC + i + 1)
                    for j in range(HNT):
                        mm = nc.tensor.matmul(yacc[i][:TT, j * 128:(j + 1) * 128],
                                              hc[:, n % R_HC, i, j * TT:(j + 1) * TT], ident[:],
                                              is_transpose=True, start=(n == 0 and j == 0),
                                              stop=(n == NS - 1 and j == HNT - 1), skip_group_check=True)
                    mm.then_inc(reduce_done, 1)

                def sums_back(k, o, i, diagonals):
                    bank = open_shared(post_tile(k, i))
                    pe.wait_ge(sums_copied, (k - 1) * IC + i + 1)
                    for j in range(HNT):
                        nc.tensor.matmul(bank[:, j * TT:(j + 1) * TT], sums[:, i, j * 128:(j + 1) * 128],
                                         ident[:TT, :TT], is_transpose=True, start=(j == 0), stop=False,
                                         skip_group_check=True)
                    if i == 0:
                        pe.wait_ge(ddiag_ready, diagonals)
                    mm = nc.tensor.matmul(bank[:, :HT], ddiag[:, i, :], u[o][:, i, :], start=False,
                                          stop=True, skip_group_check=True)
                    mm.then_inc(sh_full, 1)

                def out_projection(k, i):
                    bank = open_shared(post_tile(k, IC + i))
                    if i == 0:
                        for c in range(1, IC):
                            wait_taken(pe, post_tile(k, c))
                    for jj in range(2):
                        j = 2 * i + jj
                        for c in range(IC):
                            mm = nc.tensor.matmul(bank[:TT, jj * D:(jj + 1) * D], y[:, c, j * TT:(j + 1) * TT],
                                                  wout[:, c, :], start=(c == 0), stop=(c == IC - 1))
                    mm.then_inc(sh_full, 1)

                def step(l, h, first, last):
                    k = l * 2 + h
                    broadcast_c(k, h, 0)
                    for v in range(UNITS):
                        n, i = divmod(v, IC)
                        if turns("pe_broadcast", i) and n >= 1:
                            broadcast_c(k, h, n)
                        for c in turns("pe_reduce", i):
                            if n >= 1:
                                reduce(k, n - 1, c)
                        for i in turns("pe_z", v):
                            if i == 0 and h == 0:
                                pe.wait_ge(z_in, l * 16 + 16)
                            in_projection(z_tile(k, i), winz, i)
                        for c in turns("pe_sums", v):
                            if not first:
                                sums_back(k, 1 - h, c, (l + h) * IC)
                        for c in turns("pe_out", v):
                            if not first:
                                out_projection(k, c)
                        if not last:
                            if h == 1 and v == WHEN["pe_u"][0]:
                                pe.wait_ge(pre_in, l * 80 + 160)
                            pre(k + 1, v, 1 - h, (l + 1 + h) * IC * K)
                    for c in range(IC):
                        reduce(k, NS - 1, c)

                pe.wait_ge(zeroed, 5)
                pe.wait_ge(sel_ready, 1)
                pe.wait_ge(pre_in, 80)
                for slot in range(UNITS):
                    pre(0, slot, 0, IC * K)
                for h in range(2):
                    step(0, h, h == 0, False)
                with pe.Fori(1, NL - 1) as l:
                    for h in range(2):
                        step(l, h, False, False)
                for h in range(2):
                    step(NL - 1, h, False, h == 1)
                for i in range(IC):
                    sums_back(2 * NL, 1, i, NL * IC)
                for i in range(2):
                    out_projection(2 * NL, i)


def gating_program(nc, a, h0, xres, eps5, ident, xl, zt, put, get, weights):
    with ExitStack() as ctx:
        def sb(name, shape, dt=fp32):
            return ctx.enter_context(nc.sbuf_tensor(name, shape, dt))

        def sem(name):
            return ctx.enter_context(nc.semaphore(name))

        fnw = sb("fnw", [TT, D])
        gw = sb("gw", [DP, DC, E])
        trif, onesf = sb("trif", [TT, TT]), sb("onesf", [TT, TT])
        tri, ones = sb("tri", [TT, TT], bf16), sb("ones", [TT, TT], bf16)
        rank = sb("rank", [TT, NT, E])
        eps6 = sb("eps6", [128, 1])
        sq, sq2 = sb("sqe", [TT, NT, D]), sb("sqf", [TT, NT, D])
        ssq, ssq2 = sb("ssqe", [TT, NT]), sb("ssqf", [TT, NT])
        rrms, rstd, rrms2 = sb("rrmse", [TT, NT]), sb("rstde", [TT, NT]), sb("rrmsf", [TT, NT])
        stats, mv = sb("statse", [TT, NT, 6]), sb("mve", [TT, NT, 2])
        xT = sb("xT", [DP, DC, NTOK])
        lg, lg2 = sb("lg", [TT, NT, E]), sb("lg2", [TT, NT, E])
        masks = sb("masks", [TT, 2, NT, E])
        both = sb("both", [TT, NT, E], bf16)
        top1, top2, idx = sb("top1", [TT, NT]), sb("top2", [TT, NT]), sb("idx", [TT, NT])
        share = sb("share", [TT, 2, NT])
        keep = sb("keep", [TT, NT, E])
        row = sb("row", [TT, NT, E])
        first_row = sb("first_row", [TT, NT, E])
        behind = sb("behind", [TT, 2, NT])
        pick_keep, pick_row = sb("pick_keep", [TT, 2, NT, E]), sb("pick_row", [TT, 2, NT, E])
        kept, got, moved = sb("kept", [TT, 2, NT]), sb("got", [TT, 2, NT]), sb("moved", [TT, 2, NT])
        pb = [ctx.enter_context(nc.psum_tensor(f"pg{i}", [128, 512], fp32)) for i in range(6)]
        plogit, pplace = pb[4], pb[5]

        const_in, own = sem("const_in"), sem("vector_chain")
        normed, stat_ready = sem("normed"), sem("stat_ready_e")
        eps_set, sq_done, ln1, rms_ready, mv_ready, ln2, std_ready, xl_ready = (
            sem("eps_set"), sem("sqe_done"), sem("ln1"), sem("rmse_ready"), sem("mve_ready"), sem("ln2"),
            sem("std_ready"), sem("xl_ready"))
        sq2_done, ln3, rms2_ready = sem("sqf_done"), sem("ln3"), sem("rmsf_ready")
        xt_full, xt_copied = sem("xt_full"), sem("xt_copied")
        logits_full, logits_ready, gap_ready, gap_exp, both_ready, places_full, tri_ready = (
            sem("logits_full"), sem("logits_ready"), sem("gap_ready"), sem("gap_exp"), sem("both_ready"),
            sem("places_full"), sem("tri_ready"))

        with nc.Block() as block:
            @block.sync
            def _(sp):
                for dst, src in ((fnw, "fnw"), (gw, "gw"), (trif, "tri"), (onesf, "ones"), (rank, "rank"),
                                 (first_row, "first_row"), (behind, "behind")):
                    sp.dma_start(dst[:], a[src]).then_inc(const_in, 16)

            @block.scalar
            def _(act):
                for j in range(NT):
                    nc.scalar.activation(sq[:, j, :], xres[:, j, :], ACT.Square, accum_out=ssq[:, j:j + 1]
                                         ).then_inc(sq_done, 1)
                act.wait_ge(sq_done, NT)
                nc.scalar.activation(rrms[:], ssq[:], ACT.Ln, bias=eps5[:TT, 0:1], scale=1.0 / D).then_inc(ln1, 1)
                act.wait_ge(ln1, 1)
                nc.scalar.activation(rrms[:], rrms[:], ACT.Exp, scale=-0.5).then_inc(rms_ready, 1)
                act.wait_ge(mv_ready, NT)
                nc.scalar.activation(rstd[:], mv[:, :, 1], ACT.Ln, bias=eps5[:TT, 0:1]).then_inc(ln2, 1)
                act.wait_ge(ln2, 1)
                nc.scalar.activation(rstd[:], rstd[:], ACT.Exp, scale=-0.5).then_inc(std_ready, 1)
                for j in range(NT):
                    act.wait_ge(xl_ready, j + 1)
                    nc.scalar.activation(sq2[:, j, :], xl[:, j, :], ACT.Square, accum_out=ssq2[:, j:j + 1]
                                         ).then_inc(sq2_done, 1)
                act.wait_ge(sq2_done, NT)
                act.wait_ge(eps_set, 1)
                nc.scalar.activation(rrms2[:], ssq2[:], ACT.Ln, bias=eps6[:TT, 0:1], scale=4.0 / D).then_inc(ln3, 1)
                act.wait_ge(ln3, 1)
                nc.scalar.activation(rrms2[:], rrms2[:], ACT.Exp, scale=-0.5).then_inc(rms2_ready, 1)
                for b in range(2 * DC):
                    c, hf = divmod(b, 2)
                    act.wait_ge(xt_full, b + 1)
                    nc.scalar.copy(xT[:, c, hf * HT:(hf + 1) * HT], pb[b][:DP, :HT]).then_inc(xt_copied, 1)
                act.wait_ge(logits_full, 1)
                nc.scalar.copy(lg[:].rearrange("q j e -> q (j e)"), plogit[:TT, :NT * E]).then_inc(logits_ready, 1)
                act.wait_ge(gap_ready, 1)
                nc.scalar.activation(share[:, 1, :], share[:, 1, :], ACT.Exp).then_inc(gap_exp, 1)

            @block.tensor
            def _(pe):
                for b in range(2 * DC):
                    c, hf = divmod(b, 2)
                    pe.wait_ge(xl_ready, hf * HNT + HNT)
                    for jj in range(HNT):
                        mm = nc.tensor.transpose(pb[b][:DP, jj * TT:(jj + 1) * TT],
                                                 xl[:, hf * HNT + jj, c * DP:(c + 1) * DP], ident[:TT, :TT])
                    mm.then_inc(xt_full, 1)
                pe.wait_ge(const_in, 112)
                pe.wait_ge(xt_copied, 2 * DC)
                for j in range(NT):
                    for c in range(DC):
                        mm = nc.tensor.matmul(plogit[:TT, j * E:(j + 1) * E], xT[:, c, j * TT:(j + 1) * TT],
                                              gw[:, c, :], start=(c == 0), stop=(c == DC - 1))
                mm.then_inc(logits_full, 1)
                pe.wait_ge(tri_ready, 2)
                pe.wait_ge(both_ready, 1)
                for j in range(NT):
                    for jj in range(j):
                        nc.tensor.matmul(pplace[:TT, j * E:(j + 1) * E], ones[:], both[:, jj, :],
                                         start=(jj == 0), stop=False)
                    mm = nc.tensor.matmul(pplace[:TT, j * E:(j + 1) * E], tri[:], both[:, j, :],
                                          start=(j == 0), stop=True)
                mm.then_inc(places_full, 1)

            @block.vector
            def _(dve):
                n = [0]

                def link(ins):
                    n[0] += 1
                    ins.then_inc(own, 1)
                    dve.wait_ge(own, n[0])

                vec = nc.vector
                vec.memset(eps6[:], 1e-6).then_inc(eps_set, 1)
                dve.wait_ge(const_in, 112)
                vec.tensor_copy(tri[:], trif[:]).then_inc(tri_ready, 1)
                vec.tensor_copy(ones[:], onesf[:]).then_inc(tri_ready, 1)
                dve.wait_ge(rms_ready, 1)
                for j in range(NT):
                    vec.scalar_tensor_tensor(xl[:, j, :], xres[:, j, :], rrms[:, j:j + 1], fnw[:],
                                             ALU.mult, ALU.mult).then_inc(normed, 1)
                dve.wait_ge(normed, NT)
                link(vec.tensor_tensor(h0[:], h0[:], xl[:], ALU.add))
                for j in range(NT):
                    vec.bn_stats(stats[:, j, :], h0[:, j, :]).then_inc(stat_ready, 1)
                for j in range(NT):
                    dve.wait_ge(stat_ready, j + 1)
                    vec.bn_aggr(mv[:, j, :], stats[:, j, :]).then_inc(mv_ready, 1)
                dve.wait_ge(std_ready, 1)
                for j in range(NT):
                    vec.tensor_scalar(xl[:, j, :], h0[:, j, :], mv[:, j, 0:1], rstd[:, j:j + 1],
                                      ALU.subtract, ALU.mult).then_inc(xl_ready, 1)

                def spread(t):
                    return t[:].rearrange("q (j o) -> q j o", o=1).to_broadcast([TT, NT, E])

                def pick(logits, top, mask):
                    link(vec.tensor_reduce(top[:], logits[:], AX.X, ALU.max))
                    link(vec.tensor_tensor(mask, logits[:], spread(top), ALU.is_equal))
                    link(vec.tensor_tensor(mask, mask, rank[:], ALU.mult))
                    link(vec.tensor_reduce(idx[:], mask, AX.X, ALU.max))
                    link(vec.tensor_tensor(mask, rank[:], spread(idx), ALU.is_equal))

                dve.wait_ge(logits_ready, 1)
                pick(lg, top1, masks[:, 0])
                link(vec.tensor_scalar(lg2[:], masks[:, 0], -3.0e38, None, ALU.mult))
                link(vec.tensor_tensor(lg2[:], lg2[:], lg[:], ALU.add))
                pick(lg2, top2, masks[:, 1])
                vec.tensor_tensor(both[:], masks[:, 0], masks[:, 1], ALU.add).then_inc(both_ready, 1)
                w1, w2 = share[:, 0, :], share[:, 1, :]
                vec.tensor_tensor(w2, top2[:], top1[:], ALU.subtract).then_inc(gap_ready, 1)
                dve.wait_ge(rms2_ready, 1)
                for j in range(NT):
                    vec.tensor_scalar(zt[:, j, :], xl[:, j, :], rrms2[:, j:j + 1], 2.0, ALU.mult, ALU.mult)
                dve.wait_ge(gap_exp, 1)
                link(vec.tensor_scalar(w1, w2, 1.0, None, ALU.add))
                link(vec.reciprocal(w1, w1))
                link(vec.tensor_tensor(w2, w2, w1, ALU.mult))

                def for_both(t):
                    return t[:].rearrange("q j e -> q (j e)").rearrange("q (o x) -> q o x", o=1
                                                                        ).to_broadcast([TT, 2, NT * E])

                def flat(t):
                    return t[:].rearrange("q i j e -> q i (j e)")

                dve.wait_ge(places_full, 1)
                place = pplace[:TT, :NT * E].rearrange("q (j e) -> q j e", e=E)
                link(vec.tensor_scalar(row[:], place, float(CAP - 1), None, ALU.min))
                link(vec.tensor_tensor(row[:], row[:], first_row[:], ALU.add))
                link(vec.tensor_scalar(keep[:], place, float(CAP), None, ALU.is_lt))
                link(vec.tensor_tensor(flat(pick_keep), flat(masks), for_both(keep), ALU.mult))
                link(vec.tensor_tensor(flat(pick_row), flat(masks), for_both(row), ALU.mult))
                link(vec.tensor_reduce(kept[:], pick_keep[:], AX.X, ALU.add))
                link(vec.tensor_reduce(got[:], pick_row[:], AX.X, ALU.add))
                link(vec.tensor_tensor(moved[:], got[:], behind[:], ALU.subtract))
                link(vec.tensor_tensor(moved[:], moved[:], kept[:], ALU.mult))
                link(vec.tensor_tensor(moved[:], moved[:], behind[:], ALU.add))
                link(vec.tensor_copy(put[:], moved[:]))
                link(vec.tensor_copy(get[:], got[:]))
                link(vec.tensor_tensor(weights[:, 0:2, :], share[:], kept[:], ALU.mult))
                link(vec.tensor_tensor(weights[:, 2, :], weights[:, 0, :], weights[:, 1, :], ALU.add))


def expert_program(nc, a, h0, xl, ident, zt, put, get, weights, out):
    with ExitStack() as ctx:
        def sb(name, shape, dt=fp32):
            return ctx.enter_context(nc.sbuf_tensor(name, shape, dt))

        def sem(name):
            return ctx.enter_context(nc.semaphore(name))

        enw = sb("enw", [DP, DC, E])
        acc = sb("acc", [TT, NT, D])
        back = sb("back", [TT, 2, NT, D])
        w13 = [sb(f"w13_{b}", [DP, DC, 2 * FF]) for b in range(2)]
        wd = [sb(f"wd_{b}", [128, FC, D]) for b in range(2)]
        zin = [sb(f"zin{b}", [TT, QT, D]) for b in range(2)]
        ze = [sb(f"ze{b}", [DP, DC, CAP]) for b in range(2)]
        hid = [sb(f"hid{b}", [128, FC, CAP]) for b in range(2)]
        ys = [sb(f"ys{b}", [TT, QT, D]) for b in range(2)]
        sg = [sb(f"sg{b}", [128, CAP]) for b in range(2)]
        pb = [ctx.enter_context(nc.psum_tensor(f"px{i}", [128, 512], fp32)) for i in range(8)]
        tbank, gbank, ubank, ybank = pb[0:2], pb[2:4], pb[4:6], pb[6:8]
        enw_in, w13_in, wd_in, y_out = (
            sem("enw_in"), [sem(f"w13_in{b}") for b in range(2)], [sem(f"wd_in{b}") for b in range(2)],
            [sem(f"ye_out{b}") for b in range(2)])
        z_in = [sem(f"ze_in{b}") for b in range(2)]
        scattered, back_in = sem("scattered"), [sem(f"back_in{j}") for j in range(NT)]
        t_full, ze_ready, gu_ready, silu_ready, hid_ready, y_ready, ys_ready, base_ready, acc_ready, out_done = (
            sem("t_full"), sem("ze_ready"), sem("gu_ready"), sem("silu_ready"), sem("hid_ready"),
            sem("ye_ready"), sem("ys_ready"), sem("base_ready"), sem("acc_ready"), sem("out_done"))

        def queue_rows(j):
            return min(TT, CAP - j * TT)

        with nc.Block() as block:
            @block.sync
            def _(sp):
                def load_w13(e, b):
                    sp.dma_start(w13[b][:], a["w13"][bass.ds(e, 1)].rearrange("o p a b -> p (o a) b")
                                 ).then_inc(w13_in[b], 16)

                def load_wd(e, b):
                    sp.dma_start(wd[b][:], a["wd"][bass.ds(e, 1)].rearrange("o p a b -> p (o a) b")
                                 ).then_inc(wd_in[b], 16)

                def load_queue(e, b):
                    sp.dma_start(zin[b][:, :QT - 1, :],
                                 a["queues"][bass.ds(e * CAP, (QT - 1) * TT), :]
                                 .rearrange("(j q) d -> q j d", q=TT)).then_inc(z_in[b], 16)
                    sp.dma_start(zin[b][:queue_rows(QT - 1), QT - 1, :],
                                 a["queues"][bass.ds(e * CAP + (QT - 1) * TT, queue_rows(QT - 1)), :]
                                 ).then_inc(z_in[b], 16)

                def store_results(e, b):
                    sp.dma_start(a["results"][bass.ds(e * CAP, (QT - 1) * TT), :]
                                 .rearrange("(j q) d -> q j d", q=TT), ys[b][:, :QT - 1, :]
                                 ).then_inc(y_out[b], 16)
                    sp.dma_start(a["results"][bass.ds(e * CAP + (QT - 1) * TT, queue_rows(QT - 1)), :],
                                 ys[b][:queue_rows(QT - 1), QT - 1, :]).then_inc(y_out[b], 16)

                sp.dma_start(enw[:], a["enw"]).then_inc(enw_in, 16)
                for b in range(2):
                    load_w13(b, b)
                    load_wd(b, b)
                sp.wait_ge(scattered, 16 * 2 * NT)
                for b in range(2):
                    load_queue(b, b)
                sp.wait_ge(t_full, DC)
                load_queue(2, 0)
                sp.wait_ge(gu_ready, FC)
                load_w13(2, 0)
                for e in range(E):
                    b = e % 2
                    if e + 3 < E:
                        sp.wait_ge(t_full, (e + 2) * DC)
                        load_queue(e + 3, 1 - b)
                        sp.wait_ge(gu_ready, (e + 2) * FC)
                        load_w13(e + 3, 1 - b)
                    if e + 2 < E:
                        sp.wait_ge(y_ready, (e + 1) * QT)
                        load_wd(e + 2, b)
                    sp.wait_ge(ys_ready, (e + 1) * QT)
                    store_results(e, b)
                outv = out.rearrange("(j g) t d -> j (g t) d", j=NT)
                for j in range(NT):
                    sp.wait_ge(acc_ready, 2 * j + 2)
                    sp.dma_start(outv[j], acc[:, j, :]).then_inc(out_done, 16)
                sp.wait_ge(out_done, 16 * NT)

            @block.gpsimd
            def _(pool):
                for i in range(2):
                    for j in range(NT):
                        pool.indirect_dma_start(a["queues"], bass.IndirectOffsetOnAxis(ap=put[:, i, j:j + 1], axis=0),
                                                zt[:, j, :], None).then_inc(scattered, 16)
                for b in range(2):
                    pool.wait_ge(y_out[b], E // 2 * 32)
                for j in range(NT):
                    for i in range(2):
                        pool.indirect_dma_start(back[:, i, j, :], None, a["results"],
                                                bass.IndirectOffsetOnAxis(ap=get[:, i, j:j + 1], axis=0)
                                                ).then_inc(back_in[j], 16)

            @block.tensor
            def _(pe):
                def transposes(q, b, first=False):
                    pe.wait_ge(z_in[b], q * 32 + 32)
                    for c in range(DC):
                        if not first:
                            pe.wait_ge(ze_ready, (q * 2 + b - 1) * DC + (c + 1))
                        for j in range(QT):
                            n = queue_rows(j)
                            mm = nc.tensor.transpose(tbank[c][:DP, j * TT:j * TT + n],
                                                     zin[b][:n, j, c * DP:(c + 1) * DP], ident[:n, :n])
                        mm.then_inc(t_full, 1)

                def gate_up(q, b, first=False):
                    pe.wait_ge(w13_in[b], q * 16 + 16)
                    pe.wait_ge(ze_ready, (q * 2 + b + 1) * DC)
                    for t in range(FC):
                        if t >= 2 or not first:
                            pe.wait_ge(hid_ready, (q * 2 + b) * FC + (t - 1))
                        for bank, off in ((gbank[t % 2], 0), (ubank[t % 2], FF)):
                            for c in range(DC):
                                mm = nc.tensor.matmul(bank[:, :CAP], w13[b][:, c, off + t * 128:off + (t + 1) * 128],
                                                      ze[b][:, c, :], start=(c == 0), stop=(c == DC - 1))
                        mm.then_inc(gu_ready, 1)

                def down(q, b, first=False):
                    pe.wait_ge(wd_in[b], q * 16 + 16)
                    pe.wait_ge(hid_ready, (q * 2 + b + 1) * FC)
                    for j in range(QT):
                        if j >= 2 or not first:
                            pe.wait_ge(ys_ready, (q * 2 + b) * QT + (j - 1))
                        n = queue_rows(j)
                        for t in range(FC):
                            mm = nc.tensor.matmul(ybank[(b + j) % 2][:n, :D], hid[b][:, t, j * TT:j * TT + n],
                                                  wd[b][:, t, :], start=(t == 0), stop=(t == FC - 1))
                        mm.then_inc(y_ready, 1)

                transposes(0, 0, True)
                transposes(0, 1)
                gate_up(0, 0, True)
                transposes(1, 0)
                gate_up(0, 1)
                down(0, 0, True)
                transposes(1, 1)
                gate_up(1, 0)
                down(0, 1)
                with pe.Fori(1, E // 2 - 1) as q:
                    transposes(q + 1, 0)
                    gate_up(q, 1)
                    down(q, 0)
                    transposes(q + 1, 1)
                    gate_up(q + 1, 0)
                    down(q, 1)
                gate_up(E // 2 - 1, 1)
                down(E // 2 - 1, 0)
                down(E // 2 - 1, 1)

            @block.scalar
            def _(act):
                def expert_norm(q, b):
                    for c in range(DC):
                        act.wait_ge(t_full, (q * 2 + b) * DC + (c + 1))
                        nc.scalar.activation(ze[b][:, c, :], tbank[c][:DP, :CAP], ACT.Copy,
                                             scale=enw[:, c, bass.ds(q * 2 + b, 1)]).then_inc(ze_ready, 1)

                def silu(q, b):
                    for t in range(FC):
                        act.wait_ge(gu_ready, (q * 2 + b) * FC + (t + 1))
                        nc.scalar.activation(sg[t % 2][:], gbank[t % 2][:, :CAP], ACT.Silu).then_inc(silu_ready, 1)

                act.wait_ge(enw_in, 16)
                expert_norm(0, 0)
                expert_norm(0, 1)
                with act.Fori(0, E // 2 - 1) as q:
                    for b in range(2):
                        silu(q, b)
                        expert_norm(q + 1, b)
                for b in range(2):
                    silu(E // 2 - 1, b)

            @block.vector
            def _(dve):
                def hidden(q, b):
                    for t in range(FC):
                        dve.wait_ge(silu_ready, (q * 2 + b) * FC + (t + 1))
                        nc.vector.tensor_tensor(hid[b][:, t, :], sg[t % 2][:], ubank[t % 2][:, :CAP], ALU.mult
                                                ).then_inc(hid_ready, 1)

                def results(q, b, first=False):
                    if not first:
                        dve.wait_ge(y_out[b], q * 32)
                    for j in range(QT):
                        n = queue_rows(j)
                        dve.wait_ge(y_ready, (q * 2 + b) * QT + (j + 1))
                        nc.vector.tensor_copy(ys[b][:n, j, :], ybank[(b + j) % 2][:n, :D]).then_inc(ys_ready, 1)

                for j in range(NT):
                    nc.vector.scalar_tensor_tensor(acc[:, j, :], xl[:, j, :], weights[:, 2, j:j + 1], h0[:, j, :],
                                                   ALU.mult, ALU.add).then_inc(base_ready, 1)
                hidden(0, 0)
                hidden(0, 1)
                results(0, 0, True)
                hidden(1, 0)
                results(0, 1, True)
                with dve.Fori(1, E // 2 - 1) as q:
                    hidden(q, 1)
                    results(q, 0)
                    hidden(q + 1, 0)
                    results(q, 1)
                hidden(E // 2 - 1, 1)
                results(E // 2 - 1, 0)
                results(E // 2 - 1, 1)
                dve.wait_ge(base_ready, NT)
                for j in range(NT):
                    dve.wait_ge(back_in[j], 32)
                    for i in range(2):
                        if i == 1:
                            dve.wait_ge(acc_ready, 2 * j + 1)
                        nc.vector.scalar_tensor_tensor(acc[:, j, :], back[:, i, j, :], weights[:, i, j:j + 1],
                                                       acc[:, j, :], ALU.mult, ALU.add).then_inc(acc_ready, 1)


def build(nc, a, out):
    with ExitStack() as ctx:
        def sb(name, shape, dt=fp32):
            return ctx.enter_context(nc.sbuf_tensor(name, shape, dt))

        h0 = sb("h0", [TT, NT, D])
        xres = sb("xres", [TT, NT, D])
        eps5 = sb("eps5", [128, 1])
        ident = sb("ident", [128, 128])
        ident_in = ctx.enter_context(nc.semaphore("ident_in"))
        with nc.Block() as block:
            @block.sync
            def _(sp):
                sp.dma_start(ident[:], a["ident"]).then_inc(ident_in, 16)
                sp.wait_ge(ident_in, 16)
        embed_program(nc, a, h0, xres, eps5)
        mamba_program(nc, a, xres, eps5, ident)
        xl, zt = sb("xl", [TT, NT, D]), sb("zt", [TT, NT, D])
        put, get = sb("put", [TT, 2, NT], int32), sb("get", [TT, 2, NT], int32)
        weights = sb("weights", [TT, 3, NT])
        gating_program(nc, a, h0, xres, eps5, ident, xl, zt, put, get, weights)
        expert_program(nc, a, h0, xl, ident, zt, put, get, weights, out)


def kernel(**inputs):
    import numpy as np
    import concourse.bacc as bacc
    from concourse.bass_utils import run_bass_kernel_spmd

    g = {name: np.asarray(v) for name, v in inputs.items()}
    f = lambda name: g[name]
    rows = lambda t, p: t.reshape(t.shape[0], t.shape[1] // p, p, *t.shape[2:]).swapaxes(1, 2)
    side = 84 // 16
    px = f("x")[:, :, :side * 16, :side * 16].reshape(NB, 3, side, 16, side, 16).transpose(1, 3, 5, 0, 2, 4)
    patches = np.zeros((KP * KC, NB, SEQ), np.float32)
    patches[:, :, 1:] = px.reshape(KP * KC, NB, side * side)
    cells = 32
    edges = np.arange(1.0 / cells, 1.0, 1.0 / cells, dtype=np.float32)
    frac = np.arange(0.0, 1.0 - 1e-06, 1.0 / side, dtype=np.float32)
    at = np.searchsorted(edges, frac, side="right")
    pos = f("L0_tok_pos_table")[(at[:, None] * cells + at).reshape(-1)]
    posb = np.tile(np.concatenate([f("cls_tok").reshape(1, D), pos]), (TT // SEQ, 1))
    cbias = np.zeros((TT // SEQ, SEQ, D), np.float32)
    cbias[:, 1:] = f("L0_tok_conv_b")
    xp = f("L0_attn_x_proj_w").swapaxes(1, 2)
    wxp = np.zeros((NL, I, XR), np.float32)
    wxp[:, :, :R] = xp[:, :, :R]
    wxp[:, :, BC0:] = xp[:, :, R:]
    chan = np.concatenate([f("L0_attn_conv_w").reshape(NL, I, K), f("L0_attn_conv_b")[:, :, None],
                           f("L0_attn_dt_proj_b")[:, :, None]], 2)
    ident = np.eye(128, dtype=np.float32)
    arrays = {
        "patches": patches.reshape(KC, KP, NTOK).swapaxes(0, 1),
        "wconv": f("L0_tok_conv_w").reshape(D, KC, KP).transpose(2, 1, 0),
        "posb": posb, "cbias": cbias.reshape(TT, D),
        "ident": ident, "id3": np.tile(np.eye(NBC, dtype=np.float32), (3, 1)),
        "winu": rows(f("L0_attn_in_proj_w")[:, :I].swapaxes(1, 2), DP),
        "winz": rows(f("L0_attn_in_proj_w")[:, I:].swapaxes(1, 2), DP),
        "nw": rows(f("L0_attn_norm_w"), DP), "chan": rows(chan, 128), "wxp": rows(wxp, 128),
        "wdt": f("L0_attn_dt_proj_w").swapaxes(1, 2), "wout": rows(f("L0_attn_out_proj_w").swapaxes(1, 2), 128),
        "dskip": rows(f("L0_attn_D"), 128),
        "alog": rows(f("L0_attn_A_log"), 128).reshape(NL, 128, IC * NS),
        "fnw": np.tile(f("L0_attn_final_norm_w"), (TT, 1)),
        "gw": f("L0_ffn_gate_w").T.reshape(DC, DP, E).swapaxes(0, 1),
        "enw": f("L0_ffn_norm_w").T.reshape(DC, DP, E).swapaxes(0, 1),
        "w13": rows(f("L0_ffn_w13").swapaxes(1, 2), DP), "wd": rows(f("L0_ffn_w2").swapaxes(1, 2), 128),
        "tri": np.triu(np.ones((TT, TT), np.float32), 1), "ones": np.ones((TT, TT), np.float32),
        "first_row": np.tile(np.arange(E, dtype=np.float32) * CAP, (TT, NT, 1)),
        "behind": SLOTS + np.arange(2 * NTOK, dtype=np.float32).reshape(2, NT, TT).transpose(2, 0, 1),
        "rank": np.tile(np.arange(E, 0, -1, dtype=np.float32), (TT, NT, 1)),
    }
    nc = bacc.Bacc("TRN2", target_bir_lowering=False, num_devices=1)
    maps, a = {}, {}
    for name, v in arrays.items():
        maps[f"in_{name}"] = np.ascontiguousarray(v)
        a[name] = nc.dram_tensor(f"in_{name}", v.shape, fp32, kind="ExternalInput").ap()
    a["brows"] = nc.dram_tensor("brows", (NS, HT), fp32, kind="Internal").ap()
    a["queues"] = nc.dram_tensor("queues", (SLOTS + 2 * NTOK, D), fp32, kind="Internal").ap()
    a["results"] = nc.dram_tensor("results", (SLOTS, D), fp32, kind="Internal").ap()
    out = nc.dram_tensor("out_0", (NB, SEQ, D), fp32, kind="ExternalOutput").ap()
    build(nc, a, out)
    r = run_bass_kernel_spmd(nc, [maps], core_ids=[0])
    return r.results[0]["out_0"]
```
